# Optimizing a Trainium2 kernel written in Bass

```python
import numpy as np
import jax
import jax.numpy as jnp

def _softmax(x, axis=-1):
    return jax.nn.softmax(x, axis=axis)

def _gelu(x):
    return jax.nn.gelu(x, approximate=True)

def _silu(x):
    return jax.nn.silu(x)

def _sigmoid(x):
    return jax.nn.sigmoid(x)

def _layernorm(x, axis=-1, eps=1e-05):
    m = jnp.mean(x, axis=axis, keepdims=True)
    v = jnp.var(x, axis=axis, keepdims=True)
    return (x - m) / jnp.sqrt(v + eps)

def _scatter_add(tgt, idx, src, axis=0):
    return tgt.at[idx].add(src)

def _segment_sum(src, seg, n):
    return jax.ops.segment_sum(src, seg, n)
kernel_name = 'mk_adj_resnorm_d4_adj_r2_8a01af'

def setup_inputs(seed: int=0):
    np.random.seed(seed)
    _w = jnp.asarray

    def _rec_inputs():
        import jax
        import jax.numpy as jnp
        _gk = jax.random.key(seed)
        x = 7.22e-05 + 1 * jax.random.normal(jax.random.fold_in(_gk, 1), (128, 64, 256), jnp.float32)
        _a = jax.random.bernoulli(jax.random.fold_in(_gk, 2), 0.125, (64, 64))
        adj = _a.astype(jnp.int32)
        return (x, adj)
    x, adj = _rec_inputs()

    def _L0_gnn_setup():
        import jax, jax.numpy as jnp
        import numpy as np
        LEAKY_ALPHA = 0.01
        NEG_INF = -1000000000.0
        LN_EPS = 1e-05

        def _gat_heads(x, adj, W, a):
            O = W.shape[-1]
            Wh = jnp.einsum('bnf,hfo->bhno', x, W)
            f1 = jnp.einsum('bhno,ho->bhn', Wh, a[:, :O])
            f2 = jnp.einsum('bhno,ho->bhn', Wh, a[:, O:])
            e = f1[:, :, :, None] + f2[:, :, None, :]
            e = jnp.where(e > 0, e, LEAKY_ALPHA * e)
            e = jnp.where(adj[None, None] > 0, e, NEG_INF)
            attn = jax.nn.softmax(e, axis=-1)
            return jnp.einsum('bhnm,bhmo->bhno', attn, Wh)
        key = jax.random.key(seed)
        ks = jax.random.split(key, 10)
        B, N, F_in, F_hid, H, F_out, D_ff = (8, 1024, 256, 256, 4, 256, 256)
        s = 0.05
        return {'enc_inputs': jax.random.normal(ks[0], (B, N, F_in), jnp.float32), 'adj': jax.random.randint(ks[1], (N, N), 0, 2, jnp.int32), 'W_heads': jax.random.normal(ks[2], (H, F_in, F_hid), jnp.float32) * s, 'a_heads': jax.random.normal(ks[3], (H, 2 * F_hid), jnp.float32) * s, 'W_out': jax.random.normal(ks[4], (H * F_hid, F_out), jnp.float32) * s, 'a_out': jax.random.normal(ks[5], (2 * F_out,), jnp.float32) * s, 'w1': jax.random.normal(ks[6], (F_out, D_ff), jnp.float32) * s, 'b1': jnp.zeros((D_ff,), jnp.float32), 'w2': jax.random.normal(ks[7], (D_ff, F_out), jnp.float32) * s, 'b2': jnp.zeros((F_out,), jnp.float32), 'ln_gamma': jnp.ones((F_out,), jnp.float32), 'ln_beta': jnp.zeros((F_out,), jnp.float32)}
    _L0_gnn_all = _L0_gnn_setup()
    _L0_gnn_in = {k: v for k, v in _L0_gnn_all.items() if k in ('W_heads', 'a_heads', 'W_out', 'a_out', 'w1', 'b1', 'w2', 'b2', 'ln_gamma', 'ln_beta')}
    del _L0_gnn_all

    def _L1_gnn_setup():
        import jax, jax.numpy as jnp
        import numpy as np
        D_MODEL = 256
        NUM_HEADS = 8
        D_HEAD = D_MODEL // NUM_HEADS
        B, N = (4, 1024)
        key = jax.random.key(seed)
        ks = jax.random.split(key, 10)
        s = 1.0 / np.sqrt(D_MODEL)
        inp = {'h': jax.random.normal(ks[0], (B, N, D_MODEL), dtype=jnp.float32), 'adj': jax.random.randint(ks[1], (N, N), 0, 2, dtype=jnp.int32), 'Wq': jax.random.uniform(ks[2], (D_MODEL, D_MODEL), jnp.float32, -s, s), 'bq': jax.random.uniform(ks[3], (D_MODEL,), jnp.float32, -s, s), 'Wk': jax.random.uniform(ks[4], (D_MODEL, D_MODEL), jnp.float32, -s, s), 'bk': jax.random.uniform(ks[5], (D_MODEL,), jnp.float32, -s, s), 'Wv': jax.random.uniform(ks[6], (D_MODEL, D_MODEL), jnp.float32, -s, s), 'bv': jax.random.uniform(ks[7], (D_MODEL,), jnp.float32, -s, s), 'Wo': jax.random.uniform(ks[8], (D_MODEL, D_MODEL), jnp.float32, -s, s), 'bo': jax.random.uniform(ks[9], (D_MODEL,), jnp.float32, -s, s)}
        return inp
    _L1_gnn_all = _L1_gnn_setup()
    _L1_gnn_in = {k: v for k, v in _L1_gnn_all.items() if k in ('Wq', 'bq', 'Wk', 'bk', 'Wv', 'bv', 'Wo', 'bo')}
    del _L1_gnn_all

    def _L2_gnn_setup():
        import jax, jax.numpy as jnp
        import numpy as np
        B, K, DIN, DOUT = (32, 64, 256, 256)
        key = jax.random.key(seed)
        k1, k2, k3, k4 = jax.random.split(key, 4)
        x = jax.random.normal(k1, (B, K, DIN), dtype=jnp.float32)
        adj = jax.random.randint(k2, (K, K), 0, 2, dtype=jnp.int32)
        W = jax.random.normal(k3, (DOUT, 2 * DIN), dtype=jnp.float32) * 0.02
        b = jax.random.normal(k4, (DOUT,), dtype=jnp.float32) * 0.02
        return {'x': x, 'adj': adj, 'W': W, 'b': b}
    _L2_gnn_all = _L2_gnn_setup()
    _L2_gnn_in = {k: v for k, v in _L2_gnn_all.items() if k in ('W', 'b')}
    del _L2_gnn_all

    def _L3_gnn_setup():
        import jax, jax.numpy as jnp
        import numpy as np
        B, N, F, F1 = (512, 75, 256, 128)
        NEG = -1000000000.0
        ALPHA = 0.2
        key = jax.random.key(seed)
        k1, k2, k3, k4 = jax.random.split(key, 4)
        X = jax.random.normal(k1, (B, N, F), dtype=jnp.float32)
        A = jax.random.randint(k2, (N, N), 0, 2, dtype=jnp.int32)
        W = jax.random.normal(k3, (F, F1), dtype=jnp.float32) * (1.0 / np.sqrt(F))
        a = jax.random.normal(k4, (2, F1, 1), dtype=jnp.float32) * (1.0 / np.sqrt(F1))
        return {'X': X, 'A': A, 'W': W, 'a': a}
    _L3_gnn_all = _L3_gnn_setup()
    _L3_gnn_in = {k: v for k, v in _L3_gnn_all.items() if k in ('W', 'a')}
    del _L3_gnn_all
    return {'x': x, 'adj': adj, 'L0_gnn_W_heads': _L0_gnn_in['W_heads'], 'L0_gnn_a_heads': _L0_gnn_in['a_heads'], 'L0_gnn_W_out': _L0_gnn_in['W_out'], 'L0_gnn_a_out': _L0_gnn_in['a_out'], 'L0_gnn_w1': _L0_gnn_in['w1'], 'L0_gnn_b1': _L0_gnn_in['b1'], 'L0_gnn_w2': _L0_gnn_in['w2'], 'L0_gnn_b2': _L0_gnn_in['b2'], 'L0_gnn_ln_gamma': _L0_gnn_in['ln_gamma'], 'L0_gnn_ln_beta': _L0_gnn_in['ln_beta'], 'L1_gnn_Wq': _L1_gnn_in['Wq'], 'L1_gnn_bq': _L1_gnn_in['bq'], 'L1_gnn_Wk': _L1_gnn_in['Wk'], 'L1_gnn_bk': _L1_gnn_in['bk'], 'L1_gnn_Wv': _L1_gnn_in['Wv'], 'L1_gnn_bv': _L1_gnn_in['bv'], 'L1_gnn_Wo': _L1_gnn_in['Wo'], 'L1_gnn_bo': _L1_gnn_in['bo'], 'L2_gnn_W': _L2_gnn_in['W'], 'L2_gnn_b': _L2_gnn_in['b'], 'L3_gnn_W': _L3_gnn_in['W'], 'L3_gnn_a': _L3_gnn_in['a']}

def reference(x, adj, L0_gnn_W_heads, L0_gnn_a_heads, L0_gnn_W_out, L0_gnn_a_out, L0_gnn_w1, L0_gnn_b1, L0_gnn_w2, L0_gnn_b2, L0_gnn_ln_gamma, L0_gnn_ln_beta, L1_gnn_Wq, L1_gnn_bq, L1_gnn_Wk, L1_gnn_bk, L1_gnn_Wv, L1_gnn_bv, L1_gnn_Wo, L1_gnn_bo, L2_gnn_W, L2_gnn_b, L3_gnn_W, L3_gnn_a):
    import jax
    import jax.numpy as jnp

    def _L0_gnn_ref(enc_inputs, adj, W_heads, a_heads, W_out, a_out, w1, b1, w2, b2, ln_gamma, ln_beta):
        import jax, jax.numpy as jnp
        import numpy as np
        LEAKY_ALPHA = 0.01
        NEG_INF = -1000000000.0
        LN_EPS = 1e-05

        def _gat_heads(x, adj, W, a):
            O = W.shape[-1]
            Wh = jnp.einsum('bnf,hfo->bhno', x, W)
            f1 = jnp.einsum('bhno,ho->bhn', Wh, a[:, :O])
            f2 = jnp.einsum('bhno,ho->bhn', Wh, a[:, O:])
            e = f1[:, :, :, None] + f2[:, :, None, :]
            e = jnp.where(e > 0, e, LEAKY_ALPHA * e)
            e = jnp.where(adj[None, None] > 0, e, NEG_INF)
            attn = jax.nn.softmax(e, axis=-1)
            return jnp.einsum('bhnm,bhmo->bhno', attn, Wh)
        B, N, _ = enc_inputs.shape
        h = jax.nn.elu(_gat_heads(enc_inputs, adj, W_heads, a_heads))
        h = jnp.transpose(h, (0, 2, 1, 3)).reshape(B, N, -1)
        out = _gat_heads(h, adj, W_out[None], a_out[None])[:, 0]
        out = jax.nn.elu(out)
        ffn = jnp.maximum(out @ w1 + b1, 0.0) @ w2 + b2
        y = ffn + out
        mu = jnp.mean(y, axis=-1, keepdims=True)
        var = jnp.var(y, axis=-1, keepdims=True)
        return (y - mu) / jnp.sqrt(var + LN_EPS) * ln_gamma + ln_beta

    def _L1_gnn_ref(h, adj, Wq, bq, Wk, bk, Wv, bv, Wo, bo):
        import jax, jax.numpy as jnp
        import numpy as np
        D_MODEL = 256
        NUM_HEADS = 8
        D_HEAD = D_MODEL // NUM_HEADS
        B, N = (4, 1024)
        b, n, _ = h.shape

        def split_heads(x):
            return x.reshape(b, n, NUM_HEADS, D_HEAD).transpose(0, 2, 1, 3)
        q = split_heads(h @ Wq.T + bq)
        k = split_heads(h @ Wk.T + bk)
        v = split_heads(h @ Wv.T + bv)
        scale = 1.0 / np.sqrt(D_HEAD)
        scores = jnp.einsum('bhqd,bhkd->bhqk', q, k) * scale
        mask = (adj == 0)[None, None, :, :]
        scores = jnp.where(mask, -jnp.inf, scores)
        attn = jax.nn.softmax(scores, axis=-1)
        out = jnp.einsum('bhqk,bhkd->bhqd', attn, v)
        out = out.transpose(0, 2, 1, 3).reshape(b, n, D_MODEL)
        return out @ Wo.T + bo

    def _L2_gnn_ref(x, adj, W, b):
        import jax, jax.numpy as jnp
        import numpy as np
        B, K, DIN, DOUT = (32, 64, 256, 256)
        Din = x.shape[-1]
        Wi, Wj = (W[:, :Din], W[:, Din:])
        mi = jnp.einsum('bkd,od->bko', x, Wi)
        mj = jnp.einsum('bkd,od->bko', x, Wj)
        a = adj.astype(x.dtype)
        deg = a.sum(axis=1)
        out = deg[None, :, None] * (mi + b) + jnp.einsum('ij,bjo->bio', a, mj)
        return out

    def _L3_gnn_ref(X, A, W, a):
        import jax, jax.numpy as jnp
        import numpy as np
        B, N, F, F1 = (512, 75, 256, 128)
        NEG = -1000000000.0
        ALPHA = 0.2
        h = jnp.einsum('bnf,fo->bno', X, W)
        att_self = jnp.einsum('bno,od->bnd', h, a[0])
        att_neigh = jnp.einsum('bno,od->bnd', h, a[1])
        e = att_self + jnp.swapaxes(att_neigh, 1, 2)
        e = jax.nn.leaky_relu(e, ALPHA)
        adj = A.astype(h.dtype)
        e = e + NEG * (1.0 - adj)[None, :, :]
        alpha = jax.nn.softmax(e, axis=-1)
        out = jnp.einsum('bij,bjo->bio', alpha, h)
        return jnp.concatenate([out, h], axis=-1)
    x = _layernorm(x + _L0_gnn_ref(x, adj, L0_gnn_W_heads, L0_gnn_a_heads, L0_gnn_W_out, L0_gnn_a_out, L0_gnn_w1, L0_gnn_b1, L0_gnn_w2, L0_gnn_b2, L0_gnn_ln_gamma, L0_gnn_ln_beta), axis=-1)
    x = _layernorm(x + _L1_gnn_ref(x, adj, L1_gnn_Wq, L1_gnn_bq, L1_gnn_Wk, L1_gnn_bk, L1_gnn_Wv, L1_gnn_bv, L1_gnn_Wo, L1_gnn_bo), axis=-1)
    x = _layernorm(x + _L2_gnn_ref(x, adj, L2_gnn_W, L2_gnn_b), axis=-1)
    x = _layernorm(x + _L3_gnn_ref(x, adj, L3_gnn_W, L3_gnn_a), axis=-1)
    return x

_drawn_inputs = setup_inputs


def setup_inputs(seed=0):
    import zlib

    import numpy as np

    out = dict(_drawn_inputs(seed))
    spreads = {'L0_gnn_b1': (0.0, 0.1),
     'L0_gnn_b2': (0.0, 0.1),
     'L0_gnn_ln_gamma': (1.0, 0.2),
     'L0_gnn_ln_beta': (0.0, 0.1)}
    factors = {'L1_gnn_bq': 39.728, 'L1_gnn_bk': 64.0}
    for name, (base, spread) in spreads.items():
        noise = np.random.default_rng([zlib.crc32(name.encode()), seed]).standard_normal(out[name].shape)
        drawn = base * np.exp(spread * noise) if base else spread * noise
        out[name] = jnp.asarray(drawn.astype(out[name].dtype))
    for name, factor in factors.items():
        out[name] = (out[name] * factor).astype(out[name].dtype)
    return out
```

```python
from contextlib import ExitStack

import concourse.bass as bass
from concourse import mybir

F32 = mybir.dt.float32
F32R = mybir.dt.float32r
F16 = mybir.dt.float16
I32 = mybir.dt.int32
ALU = mybir.AluOpType
ACT = mybir.ActivationFunctionType
AX_X = mybir.AxisListType.X

P = 128
NODES = 64
D = 256
C = D // P
T = 2
G = T * P
H0 = 4
H1 = 8
HC = 4
DH = D // H1
D3 = 128
BIG = -(2.0 ** 100)
EPS = 1e-5
MAGIC = float(0x5F3759DF)


class Banks:

    def __init__(self, tensor, full, free, uses):
        self.tensor, self.full, self.free, self.uses = tensor, full, free, uses
        self.n = len(full)

    def per_group(self, b):
        return (self.uses - b + self.n - 1) // self.n

    def bank(self, u):
        return self.tensor[:, u % self.n, :]

    def before(self, g, u):
        return g * self.per_group(u % self.n) + u // self.n + 1

    def acquire(self, pe, g, u):
        pe.wait_ge(self.free[u % self.n], self.before(g, u))

    def arrived(self, eng, g, u):
        eng.wait_ge(self.full[u % self.n], self.before(g, u))

    def evacuated(self, eng, g, u):
        eng.wait_ge(self.free[u % self.n], self.before(g, u) + 1)

    def filled(self, ins, u):
        ins.then_inc(self.full[u % self.n], 1)

    def release(self, ins, u):
        ins.then_inc(self.free[u % self.n], 1)


class Chain:

    def __init__(self, eng, sem, per_group):
        self.eng, self.sem, self.per_group = eng, sem, per_group

    def start(self, g):
        self.base, self.n = g * self.per_group, 0

    def add(self, ins):
        self.n += 1
        ins.then_inc(self.sem, 1)

    def link(self, ins):
        self.add(ins)
        self.eng.wait_ge(self.sem, self.base + self.n)

    def end(self):
        assert self.n == self.per_group, (self.n, self.per_group)


def build_program(nc, io):
    groups = io["x"].shape[0] // G
    with ExitStack() as ctx:
        def sb(name, shape, dt):
            return ctx.enter_context(nc.sbuf_tensor(name, shape, dt))

        def sem(name):
            return ctx.enter_context(nc.semaphore(name))

        def pair(name, shape):
            return sb(name + "_hi", shape, F32R), sb(name + "_lo", shape, F32R)

        wh = pair("w_heads", [P, H0, C, D])
        wo = pair("w_out", [P, H0 * C, D + 2])
        wf = pair("w_ffn", [P, 2, C, D])
        wp = pair("w_proj", [P, 4, C, D])
        wm = pair("w_msg", [P, 2, C, D])
        w3 = pair("w_last", [P, C, D3 + 2])
        wa = sb("w_att", [P, C, 2, 2 * H0], F32R)

        ident = sb("ident", [P, P], F32R)
        ident16 = sb("ident16", [P, P], F16)
        eye2 = sb("eye2", [P, NODES], F32)
        same = sb("same_graph", [P, P], F32R)
        mask0 = sb("mask0", [P, NODES], F32R)
        mask1 = sb("mask1", [P, NODES], F32)
        adj_t = sb("adj_t", [P, P], F32R)
        deg = sb("deg", [P, 1], F32)
        row_ok = sb("row_ok", [P, 1], F32)
        b2_bc = sb("b2_bc", [P, D], F32)
        gamma_bc = sb("gamma_bc", [P, D], F32)
        beta_bc = sb("beta_bc", [P, D], F32)
        bo_bc = sb("bo_bc", [P, D], F32)
        degb_bc = sb("degb_bc", [P, D], F32)
        b1c = sb("b1c", [P, C], F32)
        bqc = sb("bqc", [P, C], F32)
        bkc = sb("bkc", [P, C], F32)
        bvc = sb("bvc", [P, C], F32)
        adj_i = sb("adj_i", [P, NODES], I32)
        adjt_i = sb("adjt_i", [P, NODES], I32)
        adj_f = sb("adj_f", [P, NODES], F32)
        tmpc = sb("tmpc", [P, 64], F32)
        wide = sb("identf", [P, P], F32)

        work = sb("work", [P, 9000], F32)
        at = [0]

        def w32(*shape):
            n = 1
            for s in shape:
                n *= s
            v = work[:, at[0]:at[0] + n]
            at[0] += n
            if len(shape) == 2:
                v = v.rearrange("p (a b) -> p a b", a=shape[0])
            if len(shape) == 3:
                v = v.rearrange("p (a b c) -> p a b c", a=shape[0], b=shape[1])
            return v

        x_in = w32(T, D)
        xt_in = w32(C, G)
        x_beta = w32(T, D)
        f_raw = w32(T, 16)
        f_sum = w32(T, 8)
        lg = w32(T * H0, NODES)
        pr = w32(T * H0, NODES)
        rmax = w32(1, T * H0)
        rden = w32(1, T * H0)
        ex = [w32(C, G) for _ in range(2)]
        hf = [w32(C, G) for _ in range(2)]
        g2 = w32(T, 2)
        hid = hf[1]
        y0 = ex[1]
        z0 = ex[0]
        st0 = w32(T, 6)
        mv0 = w32(T, 2)
        nr0 = w32(4, T)
        x1 = w32(T, D)
        x1b = w32(T, D)
        sc = w32(T * H1, NODES)
        smax = w32(1, T * H1)
        sden = w32(1, T * H1)
        y1 = w32(T, D)
        ot1 = y1
        x2 = w32(T, D)
        x2b = x1b
        x3 = x1
        t1 = sc.rearrange("p a n -> p (a n)")[:, 0:T * D].rearrange("p (t n) -> p t n", t=T)
        h3 = w32(T, D3 + 2)
        lg3 = w32(T, NODES)
        m3 = w32(1, T)
        d3 = w32(1, T)
        st1 = w32(T, 6)
        mv1 = w32(T, 2)
        nr1 = w32(4, T)
        res = w32(T, D)

        raw_wh = work[:, 0:2048].rearrange("p (h c n) -> p h c n", h=H0, c=C)
        raw_wo = work[:, 2048:4096].rearrange("p (k n) -> p k n", k=H0 * C)
        raw_wp = work[:, 0:2048].rearrange("p (k c n) -> p k c n", k=4, c=C)
        raw_wf = work[:, 2048:3072].rearrange("p (k c n) -> p k c n", k=2, c=C)
        raw_wm = work[:, 3072:4096].rearrange("p (k c n) -> p k c n", k=2, c=C)
        raw_w3 = work[:, 4096:4352].rearrange("p (c n) -> p c n", c=C)
        raw_a = work[:, 4352:6400].rearrange("p (h k n) -> p h k n", h=H0, k=2)
        raw_ao = work[:, 6400:6912].rearrange("p (k n) -> p k n", k=2)
        raw_a3 = work[:, 6912:7168].rearrange("p (k n) -> p k n", k=2)
        junk = work[:, 7168:7424]
        att_f = work[:, 7424:7440].rearrange("p (c n) -> p c n", c=C)
        out_f = work[:, 7440:7456].rearrange("p (k n) -> p k n", k=H0 * C)
        last_f = work[:, 7456:7460].rearrange("p (c n) -> p c n", c=C)

        def rpair(name, shape):
            return sb(name + "_hi", shape, F32R), sb(name + "_lo", shape, F32R)

        xn = rpair("x_rows", [P, T, D])
        xt = rpair("x_cols", [P, C, G])
        dg = [xt[s][:, :, :].rearrange("p c n -> p (c n)") for s in range(2)]
        share = sb("share", [P, 2, C * H0 * G], F32R)
        zt = [share[:, s, :].rearrange("p (c h n) -> p c h n", c=C, h=H0) for s in range(2)]
        wh2 = [share[:, s, 0:516].rearrange("p (t n) -> p t n", t=T) for s in range(2)]
        dg2 = [share[:, s, 516:644] for s in range(2)]
        pt2 = [share[:, s, 644:900].rearrange("p (t n) -> p t n", t=T) for s in range(2)]
        ott = [share[:, s, 900:1412].rearrange("p (c n) -> p c n", c=C) for s in range(2)]
        hdt = [share[:, s, 1412:1924].rearrange("p (c n) -> p c n", c=C) for s in range(2)]
        ht = rpair("heads", [P, H0 * C, G])
        pt0 = ht[0][:, :, :].rearrange("p k n -> p (k n)").rearrange("p (s t n) -> p s t n", s=2, t=T)
        fsm_hi = sb("fsm_hi", [P, T, H0], F32R)
        fsm_lo = sb("fsm_lo", [P, T, H0], F32R)
        fsm3_hi = sb("fsm3_hi", [P, T], F32R)
        fsm3_lo = sb("fsm3_lo", [P, T], F32R)
        pb = [sb(f"pb{s}", [P, T * H0, P], F16) for s in range(2)]
        pb2 = [sb(f"pb2{s}", [P, T, P], F16) for s in range(2)]
        x16 = sb("x16", [P, 2, T, D], F16)

        xt1 = sb("xt1", [P, 2, C, G], F32R)
        qt = rpair("qt", [P, C, G])
        kt = rpair("kt", [P, C, G])
        kd = rpair("k_diag", [P, C, T, HC, P])
        vv = rpair("v", [P, T, D])
        pb1 = [sb(f"pb1{s}", [P, T, H1, P], F16) for s in range(2)]
        pt1 = sb("pt1", [P, 2, 2, HC * P], F32R)
        o1 = qt
        mj = [vv[s][:, :, :] for s in range(2)]
        h3r = [qt[s][:, :, :].rearrange("p c n -> p (c n)")[:, 0:T * D3].rearrange("p (t n) -> p t n", t=T)
               for s in range(2)]
        dg3 = [kt[s][:, 0, 0:T * NODES] for s in range(2)]
        pt3 = [kt[s][:, 1, 0:T * P].rearrange("p (t n) -> p t n", t=T) for s in range(2)]
        pb3 = [sb(f"pb3{s}", [P, T, P], F16) for s in range(2)]

        psum_a = ctx.enter_context(nc.psum_tensor("psum_a", [P, 4, 512], F32))
        psum_b = ctx.enter_context(nc.psum_tensor("psum_b", [P, 4, 512], F32))
        A = Banks(psum_a, [sem(f"a_full{i}") for i in range(4)], [sem(f"a_free{i}") for i in range(4)], 19)
        B = Banks(psum_b, [sem(f"b_full{i}") for i in range(4)], [sem(f"b_free{i}") for i in range(4)], 26)

        raw_loaded = sem("raw_loaded")
        const_loaded = sem("const_loaded")
        pool_set = sem("pool_set")
        set_act = sem("set_act")
        set_dve = sem("set_dve")
        set_chain = sem("set_chain")
        x_loaded = sem("x_loaded")
        x_split = sem("x_split")
        a_chain = sem("a_chain")
        b_chain = sem("b_chain")
        diag_ready = sem("diag_ready")
        logits_ready = sem("logits_ready")
        exp_ready = sem("exp_ready")
        prob_ready = sem("prob_ready")
        ph_ready = sem("ph_ready")
        pl_ready = sem("pl_ready")
        zt_hi = sem("zt_hi")
        zt_lo = sem("zt_lo")
        ex_ready = sem("ex_ready")
        ht_hi = sem("ht_hi")
        ht_lo = sem("ht_lo")
        wh2_hi = sem("wh2_hi")
        wh2_lo = sem("wh2_lo")
        diag2_ready = sem("diag2_ready")
        logits2_ready = sem("logits2_ready")
        exp2_ready = sem("exp2_ready")
        prob2_ready = sem("prob2_ready")
        ph2_ready = sem("ph2_ready")
        pl2_ready = sem("pl2_ready")
        hid_hi = sem("hid_hi")
        hid_lo = sem("hid_lo")
        xs_ready = sem("xs_ready")
        x16_hi = sem("x16_hi")
        x16_lo = sem("x16_lo")
        x1b_ready = sem("x1b_ready")
        cols_ready = sem("cols_ready")
        q_hi = sem("q_hi")
        k_hi = sem("k_hi")
        v_hi = sem("v_hi")
        v_lo = sem("v_lo")
        kd_loaded = sem("kd_loaded")
        s_ready = sem("s_ready")
        s_exp = sem("s_exp")
        s_prob = sem("s_prob")
        s_ph = sem("s_ph")
        s_pl = sem("s_pl")
        o_hi = sem("o_hi")
        o_lo = sem("o_lo")
        mj_hi = sem("mj_hi")
        mj_lo = sem("mj_lo")
        h3_hi = sem("h3_hi")
        diag3_ready = sem("diag3_ready")
        logits3_ready = sem("logits3_ready")
        exp3_ready = sem("exp3_ready")
        prob3_ready = sem("prob3_ready")
        ph3_ready = sem("ph3_ready")
        pl3_ready = sem("pl3_ready")
        res_ready = sem("res_ready")
        stored = sem("stored")

        x_rows = io["x"].rearrange("(g t p) n -> g p t n", t=T, p=P)
        x_cols = io["xT"].rearrange("(c p) (g n) -> g p c n", c=C, n=G)
        out_rows = io["out"].rearrange("(g t p) n -> g p t n", t=T, p=P)

        def bc(v, shape):
            return v.broadcast_to(shape)

        def col(v):
            return v.rearrange("p (n a) -> p n a", a=1)

        def row(name):
            return io[name].rearrange("(a n) -> a n", a=1)

        RAW0, RAW1 = 6, 7

        block = ctx.enter_context(nc.Block())

        @block.sync
        def _(sp):
            def first(*pairs):
                for dst, src in pairs:
                    sp.dma_start(dst, src).then_inc(raw_loaded, 16)

            first((raw_wh, io["w_heads"].rearrange("h (c p) n -> p h c n", p=P)),
                  (raw_wo, io["w_out"].rearrange("(k p) n -> p k n", p=P)),
                  (raw_w3, io["w3"].rearrange("(c p) n -> p c n", p=P)),
                  (raw_a, io["a_heads"].rearrange("(a h) (k n) -> a h k n", a=1, k=2).broadcast_to([P, H0, 2, D])),
                  (raw_ao, io["a_out"].rearrange("(a k n) -> a k n", a=1, k=2).broadcast_to([P, 2, D])),
                  (raw_a3, io["a3"].rearrange("(a k) n -> a k n", a=1).broadcast_to([P, 2, D3])))
            sp.wait_ge(set_act, 6)
            sp.wait_ge(set_dve, 6)
            first((raw_wp[:, 0], io["wqT"].rearrange("(c p) n -> p c n", p=P)),
                  (raw_wp[:, 1], io["wkT"].rearrange("(c p) n -> p c n", p=P)),
                  (raw_wp[:, 2], io["wvT"].rearrange("(c p) n -> p c n", p=P)),
                  (raw_wp[:, 3], io["woT"].rearrange("(c p) n -> p c n", p=P)),
                  (raw_wf[:, 0], io["w1"].rearrange("(c p) n -> p c n", p=P)),
                  (raw_wf[:, 1], io["w2"].rearrange("(c p) n -> p c n", p=P)),
                  (raw_wm, io["wmT"].rearrange("(k c p) n -> p k c n", k=2, p=P)))
            sp.wait_ge(set_act, 9)
            sp.wait_ge(set_dve, 9)

            def group(g):
                sp.wait_ge(x_split, 5 * g + 5)
                sp.dma_start(x_in, x_rows[g]).then_inc(x_loaded, 16)
                sp.dma_start(xt_in, x_cols[g]).then_inc(x_loaded, 16)

            def keys(g):
                for s in range(2):
                    if s == 0:
                        sp.wait_ge(k_hi, g + 1)
                    else:
                        B.evacuated(sp, g, 1)
                    for h in range(HC):
                        rows = slice(32 * h, 32 * h + 32)
                        sp.dma_start(kd[s][rows, :, :, h, :].bitcast(F32),
                                     kt[s][rows].rearrange("p c (t n) -> p c t n", t=T).bitcast(F32)).then_inc(kd_loaded, 16)

            def store(g):
                sp.wait_ge(res_ready, g + 1)
                sp.dma_start(out_rows[g], res).then_inc(stored, 16)

            sp.sem_inc(stored, 16)
            with sp.Fori(0, groups) as g:
                group(g)
                keys(g)
                store(g)
            sp.wait_ge(stored, 16 * groups + 16)

        @block.gpsimd
        def _(pool):
            po = nc.gpsimd
            for dst, src in ((b2_bc[:, :], row("b2").broadcast_to([P, D])),
                             (gamma_bc[:, :], row("gamma").broadcast_to([P, D])),
                             (beta_bc[:, :], row("beta").broadcast_to([P, D])),
                             (bo_bc[:, :], row("bo").broadcast_to([P, D])),
                             (degb_bc[:, :], row("bm").broadcast_to([P, D])),
                             (adj_i[0:NODES, :], io["adj"]), (adj_i[NODES:P, :], io["adj"]),
                             (adjt_i[0:NODES, :], io["adjT"]), (adjt_i[NODES:P, :], io["adjT"])):
                pool.dma_start(dst, src).then_inc(const_loaded, 16)
            for n, (dst, src) in enumerate(((b1c, "b1"), (bqc, "bq"), (bkc, "bk"), (bvc, "bv"))):
                pool.dma_start(dst[:, :], io[src]).then_inc(const_loaded, 16)
            po.memset(wide[:, :], 0.0).then_inc(pool_set, 1)
            po.memset(eye2[:, :], 0.0).then_inc(pool_set, 1)
            po.memset(same[:, :].bitcast(F32), 0.0).then_inc(pool_set, 1)
            po.memset(adj_t[:, :].bitcast(F32), 0.0).then_inc(pool_set, 1)
            for t in (*pb, *pb1, *pb2, *pb3, *kd):
                v = t[tuple([slice(None)] * len(t.shape))]
                po.memset(v.bitcast(F32) if t.dtype == F32R else v, 0.0).then_inc(pool_set, 1)
            pool.wait_ge(pool_set, 14)
            po.affine_select(out=wide[:, :], in_=wide[:, :], compare_op=ALU.not_equal, fill=1.0, base=0,
                             pattern=[[-1, P]], channel_multiplier=1).then_inc(pool_set, 1)
            po.affine_select(out=eye2[:, :], in_=eye2[:, :], compare_op=ALU.not_equal, fill=1.0, base=0,
                             pattern=[[-1, NODES]], channel_multiplier=1).then_inc(pool_set, 1)
            pool.wait_ge(pool_set, 16)
            po.affine_select(out=eye2[:, :], in_=eye2[:, :], compare_op=ALU.not_equal, fill=1.0, base=-NODES,
                             pattern=[[-1, NODES]], channel_multiplier=1).then_inc(pool_set, 1)
            po.tensor_copy(ident[:, :], wide[:, :]).then_inc(pool_set, 1)
            po.tensor_copy(ident16[:, :], wide[:, :]).then_inc(pool_set, 1)
            pool.wait_ge(pool_set, 19)
            pool.sem_inc(x_split, 5)
            pool.wait_ge(const_loaded, 16 * 13)
            pool.wait_ge(set_dve, 16)

            def split(g):
                pool.wait_ge(x_loaded, 32 * g + 32)
                po.tensor_tensor(x_beta, x_in, bc(beta_bc[:, :].rearrange("p (a n) -> p a n", a=1), [P, T, D]),
                                 ALU.add).then_inc(x_split, 1)
                po.tensor_copy(xt[0][:, :, :], xt_in).then_inc(x_split, 1)
                pool.wait_ge(x_split, 5 * g + 7)
                po.tensor_tensor(xt[1][:, :, :], xt_in, xt[0][:, :, :].bitcast(F32), ALU.subtract).then_inc(x_split, 1)
                po.tensor_copy(xn[0][:, :, :], x_in).then_inc(x_split, 1)
                pool.wait_ge(x_split, 5 * g + 9)
                po.tensor_tensor(xn[1][:, :, :], x_in, xn[0][:, :, :].bitcast(F32), ALU.subtract).then_inc(x_split, 1)

            def l0(g):
                for h in range(H0):
                    pool.wait_ge(ht_hi, 5 * g + h + 1)
                    po.tensor_tensor(ht[1][:, C * h:C * h + C, :], hf[h % 2],
                                     ht[0][:, C * h:C * h + C, :].bitcast(F32), ALU.subtract).then_inc(ht_lo, 1)
                pool.wait_ge(ht_hi, 5 * g + 5)
                po.tensor_tensor(ott[1], hf[0], ott[0].bitcast(F32), ALU.subtract).then_inc(ht_lo, 1)
                pool.wait_ge(hid_hi, g + 1)
                po.tensor_tensor(hdt[1], hid, hdt[0].bitcast(F32), ALU.subtract).then_inc(hid_lo, 1)

            def l13(g):
                pool.wait_ge(xs_ready, 3 * g + 1)
                po.tensor_tensor(x1b, x1, bc(bo_bc[:, :].rearrange("p (a n) -> p a n", a=1), [P, T, D]),
                                 ALU.add).then_inc(x1b_ready, 1)
                pool.wait_ge(xs_ready, 3 * g + 2)
                po.tensor_tensor(x2b, x2, bc(degb_bc[:, :].rearrange("p (a n) -> p a n", a=1), [P, T, D]),
                                 ALU.add).then_inc(x1b_ready, 1)

            with pool.Fori(0, groups) as g:
                split(g)
                l0(g)
                l13(g)

        @block.scalar
        def _(act):
            sc_ = nc.scalar
            act.wait_ge(raw_loaded, 16 * RAW0)
            sc_.activation(wh[0][:, :, :, :], raw_wh, ACT.Copy).then_inc(set_act, 1)
            sc_.activation(wo[0][:, :, 0:D], raw_wo, ACT.Copy).then_inc(set_act, 1)
            sc_.activation(w3[0][:, :, 0:D3], raw_w3, ACT.Copy).then_inc(set_act, 1)
            act.wait_ge(set_chain, 16 + 16 + 4)
            for src, dst in ((att_f, wa[:, :, 0, :]), (out_f, wo[0][:, :, D:D + 2]), (last_f, w3[0][:, :, D3:D3 + 2])):
                sc_.activation(dst, src, ACT.Copy).then_inc(set_act, 1)
            act.wait_ge(raw_loaded, 16 * (RAW0 + RAW1))
            for dst, src in ((wf[0], raw_wf), (wp[0], raw_wp), (wm[0], raw_wm)):
                sc_.activation(dst[:, :, :, :], src, ACT.Copy).then_inc(set_act, 1)

            act.wait_ge(const_loaded, 16 * 13)
            act.wait_ge(pool_set, 19)
            act.wait_ge(set_dve, 16)

            def softmax_parts(eng, g, logits, ready, exp_done, n=1, scale=1.0):
                eng.wait_ge(ready, n * g + n)
                sc_.activation(logits, logits, ACT.Exp, scale=scale).then_inc(exp_done, 1)

            def high(g, src, dst, ready, done):
                act.wait_ge(ready, g + 1)
                sc_.activation(dst[0:NODES, :, 0:NODES], src[0:NODES], ACT.Copy).then_inc(done, 1)
                sc_.activation(dst[NODES:P, :, NODES:P], src[NODES:P], ACT.Copy).then_inc(done, 1)

            def l0(g):
                softmax_parts(act, g, lg, logits_ready, exp_ready)
                high(g, pr, pb[0][:, :, :], prob_ready, ph_ready)
                A.arrived(act, g, 2)
                A.release(sc_.activation(pt0[:, :, 0, :], A.bank(2).bitcast(F16).rearrange("p (s n) -> p s n", s=2),
                                         ACT.Copy), 2)
                for t in range(T):
                    for c in range(C):
                        u = 4 + C * t + c
                        A.arrived(act, g, u)
                        sc_.activation(zt[0][:, c, :, t * P:t * P + P], A.bank(u).rearrange("p (h n) -> p h n", h=H0),
                                       ACT.Copy).then_inc(zt_hi, 1)

                def elu_parts(n, u, dst):
                    A.arrived(act, g, u)
                    if n >= 2:
                        A.evacuated(act, g, 8 + n - 2)
                    sc_.activation(ex[n % 2], A.bank(u).rearrange("p (c n) -> p c n", c=C), ACT.Exp).then_inc(ex_ready, 1)
                    A.evacuated(act, g, u)
                    sc_.activation(dst, hf[n % 2], ACT.Copy).then_inc(ht_hi, 1)

                for h in range(H0):
                    elu_parts(h, 8 + h, ht[0][:, C * h:C * h + C, :])
                for t in range(T):
                    A.arrived(act, g, 12 + t)
                    sc_.activation(wh2[0][:, t, :], A.bank(12 + t)[:, 0:D + 2], ACT.Copy).then_inc(wh2_hi, 1)
                softmax_parts(act, g, lg[:, 0:T, :], logits2_ready, exp2_ready)
                high(g, pr[:, 0:T, :], pb2[0][:, :, :], prob2_ready, ph2_ready)
                A.arrived(act, g, 15)
                for s in range(2):
                    last = sc_.activation(pt2[s], A.bank(15).bitcast(F16)[:, s * T * P:(s + 1) * T * P]
                                          .rearrange("p (t n) -> p t n", t=T), ACT.Copy)
                A.release(last, 15)
                elu_parts(4, 16, ott[0])
                A.arrived(act, g, 17)
                for c in range(C):
                    last = sc_.activation(hid[:, c, :], A.bank(17)[:, c * G:(c + 1) * G], ACT.Relu, bias=b1c[:, c:c + 1])
                A.release(last, 17)
                A.evacuated(act, g, 17)
                sc_.activation(hdt[0], hid, ACT.Copy).then_inc(hid_hi, 1)
                act.wait_ge(xs_ready, 3 * g + 1)
                sc_.activation(x16[:, 0], x1, ACT.Copy).then_inc(x16_hi, 1)

            def cols(g, n, u):
                B.arrived(act, g, u)
                B.release(sc_.activation(xt1[:, :, :, :].rearrange("p s c n -> p (s c n)"),
                                         B.bank(u).bitcast(F16), ACT.Copy), u)

            def l13(g):
                cols(g, 0, 0)
                for u, dst, bias, done in ((1, kt, bkc, k_hi), (2, qt, bqc, q_hi)):
                    B.arrived(act, g, u)
                    for c in range(C):
                        last = sc_.activation(dst[0][:, c, :], B.bank(u)[:, c * G:(c + 1) * G], ACT.Identity,
                                              bias=bias[:, c:c + 1])
                    last.then_inc(done, 1)
                B.arrived(act, g, 3)
                sc_.activation(vv[0][:, :, :], B.bank(3).rearrange("p (t n) -> p t n", t=T), ACT.Copy).then_inc(v_hi, 1)
                softmax_parts(act, g, sc, s_ready, s_exp, scale=DH ** -0.5)
                act.wait_ge(s_prob, g + 1)
                for q, (a, b) in enumerate(((0, NODES), (NODES, P))):
                    sc_.activation(pb1[0][a:b, :, :, a:b].rearrange("p t h n -> p (t h) n"), sc[a:b], ACT.Copy).then_inc(s_ph, 1)
                for n in range(T * C):
                    B.arrived(act, g, 8 + 2 * n)
                    if n >= 2:
                        B.arrived(act, g, 9 + 2 * (n - 2))
                    last = sc_.activation(pt1[:, n % 2], B.bank(8 + 2 * n).bitcast(F16).rearrange("p (s n) -> p s n", s=2),
                                          ACT.Copy)
                    B.release(last, 8 + 2 * n)
                B.evacuated(act, g, 15)
                for c in range(C):
                    last = sc_.activation(o1[0][:, c, :], ot1[:, c, :], ACT.Identity, bias=bvc[:, c:c + 1])
                last.then_inc(o_hi, 1)
                act.wait_ge(xs_ready, 3 * g + 2)
                sc_.activation(x16[:, 0], x2, ACT.Copy).then_inc(x16_hi, 1)
                cols(g, 1, 17)
                B.arrived(act, g, 18)
                B.release(sc_.activation(t1, B.bank(18).rearrange("p (t n) -> p t n", t=T), ACT.Copy, scale=deg[:, 0:1]), 18)
                B.arrived(act, g, 19)
                sc_.activation(mj[0], B.bank(19).rearrange("p (t n) -> p t n", t=T), ACT.Copy).then_inc(mj_hi, 1)
                act.wait_ge(xs_ready, 3 * g + 3)
                sc_.activation(x16[:, 0], x3, ACT.Copy).then_inc(x16_hi, 1)
                cols(g, 2, 21)
                B.evacuated(act, g, 22)
                sc_.activation(h3r[0], h3[:, :, 0:D3], ACT.Copy).then_inc(h3_hi, 1)
                softmax_parts(act, g, lg3, logits3_ready, exp3_ready)
                high(g, lg3, pb3[0][:, :, :], prob3_ready, ph3_ready)
                B.arrived(act, g, 24)
                for s in range(2):
                    last = sc_.activation(pt3[s], B.bank(24).bitcast(F16)[:, s * T * P:(s + 1) * T * P]
                                          .rearrange("p (t n) -> p t n", t=T), ACT.Copy)
                B.release(last, 24)

            with act.Fori(0, groups) as g:
                l0(g)
                l13(g)

        @block.vector
        def _(dve):
            ve = nc.vector
            for bank in (*A.free, *B.free):
                dve.sem_inc(bank, 1)
            setup = Chain(dve, set_chain, 0)
            setup.start(0)
            dve.wait_ge(raw_loaded, 16 * RAW0)
            for c in range(C):
                for h in range(H0):
                    for k in range(2):
                        setup.link(ve.tensor_tensor_reduce(junk, raw_wh[:, h, c, :], raw_a[:, h, k, :], 1.0, 0.0,
                                                           ALU.mult, ALU.add, att_f[:, c, k * H0 + h:k * H0 + h + 1]))
            for q in range(H0 * C):
                for k in range(2):
                    setup.link(ve.tensor_tensor_reduce(junk, raw_wo[:, q, :], raw_ao[:, k, :], 1.0, 0.0,
                                                       ALU.mult, ALU.add, out_f[:, q, k:k + 1]))
            for c in range(C):
                for k in range(2):
                    setup.link(ve.tensor_tensor_reduce(junk[:, 0:D3], raw_w3[:, c, :], raw_a3[:, k, :], 1.0, 0.0,
                                                       ALU.mult, ALU.add, last_f[:, c, k:k + 1]))
            dve.wait_ge(set_act, 6)
            ve.tensor_tensor(wh[1][:, :, :, :], raw_wh, wh[0][:, :, :, :].bitcast(F32), ALU.subtract).then_inc(set_dve, 1)
            ve.tensor_tensor(wo[1][:, :, 0:D], raw_wo, wo[0][:, :, 0:D].bitcast(F32), ALU.subtract).then_inc(set_dve, 1)
            ve.tensor_tensor(w3[1][:, :, 0:D3], raw_w3, w3[0][:, :, 0:D3].bitcast(F32), ALU.subtract).then_inc(set_dve, 1)
            ve.tensor_tensor(wo[1][:, :, D:D + 2], out_f, wo[0][:, :, D:D + 2].bitcast(F32), ALU.subtract).then_inc(set_dve, 1)
            ve.tensor_tensor(w3[1][:, :, D3:D3 + 2], last_f, w3[0][:, :, D3:D3 + 2].bitcast(F32), ALU.subtract).then_inc(set_dve, 1)
            ve.tensor_tensor(wa[:, :, 1, :], att_f, wa[:, :, 0, :].bitcast(F32), ALU.subtract).then_inc(set_dve, 1)
            dve.wait_ge(set_act, 9)
            for w, src in ((wf, raw_wf), (wp, raw_wp), (wm, raw_wm)):
                ve.tensor_tensor(w[1][:, :, :, :], src, w[0][:, :, :, :].bitcast(F32), ALU.subtract).then_inc(set_dve, 1)
            dve.wait_ge(pool_set, 19)
            ve.memset(same[0:NODES, 0:NODES].bitcast(F32), 1.0).then_inc(set_dve, 1)
            ve.memset(same[NODES:P, NODES:P].bitcast(F32), 1.0).then_inc(set_dve, 1)
            dve.wait_ge(const_loaded, 16 * 13)
            setup.link(ve.tensor_copy(adj_f[:, :], adj_i[:, :]))
            ve.tensor_scalar(mask0[:, :], adj_f[:, :], 0.0, BIG, ALU.is_le, ALU.mult).then_inc(set_dve, 1)
            ve.tensor_scalar(mask1[:, :], adj_f[:, :], 0.0, BIG, ALU.is_equal, ALU.mult).then_inc(set_dve, 1)
            ve.tensor_copy(adj_t[0:NODES, 0:NODES], adjt_i[0:NODES, :]).then_inc(set_dve, 1)
            ve.tensor_copy(adj_t[NODES:P, NODES:P], adjt_i[NODES:P, :]).then_inc(set_dve, 1)
            setup.link(ve.tensor_reduce(deg[:, :], adj_f[:, :], AX_X, ALU.add))
            setup.link(ve.tensor_scalar(adj_f[:, :], adj_f[:, :], 0.0, None, ALU.not_equal))
            setup.link(ve.tensor_reduce(tmpc[:, 0:1], adj_f[:, :], AX_X, ALU.add))
            setup.link(ve.reciprocal(tmpc[:, 1:2], tmpc[:, 0:1]))
            setup.link(ve.tensor_tensor(tmpc[:, 2:3], tmpc[:, 0:1], tmpc[:, 1:2], ALU.mult))
            setup.link(ve.tensor_scalar(row_ok[:, :], tmpc[:, 2:3], 0.0, 1.0, ALU.mult, ALU.add))
            ve.tensor_scalar(degb_bc[:, :], degb_bc[:, :], deg[:, 0:1], None, ALU.mult).then_inc(set_dve, 1)
            dve.wait_ge(set_dve, 16)

            ca = Chain(dve, a_chain, 66)
            cb = Chain(dve, b_chain, 80)

            def layer_norm(ch, src, dst, st, mv, nr, done=None):
                for t in range(T):
                    (ch.link if t == T - 1 else ch.add)(ve.bn_stats(st[:, t, :], src[:, t, :]))
                me, se, mo, so = (st[:, :, k] for k in (1, 2, 4, 5))
                v, q, d, y = (nr[:, k, :] for k in range(4))
                mean = mv[:, 0, :]
                ch.add(ve.tensor_tensor(mean, me, mo, ALU.add))
                ch.add(ve.tensor_tensor(d, me, mo, ALU.subtract))
                ch.link(ve.tensor_tensor(v, se, so, ALU.add))
                ch.add(ve.tensor_scalar(mean, mean, 0.5, None, ALU.mult))
                ch.add(ve.tensor_scalar(v, v, 1.0 / D, EPS, ALU.mult, ALU.add))
                ch.link(ve.tensor_tensor(d, d, d, ALU.mult))
                ch.link(ve.scalar_tensor_tensor(v, d, 0.25, v, ALU.mult, ALU.add))
                ch.link(ve.tensor_scalar(q.bitcast(I32), v.bitcast(I32), 1, None, ALU.logical_shift_right))
                ch.link(ve.tensor_scalar(y.bitcast(I32), q.bitcast(I32), -1.0, MAGIC, ALU.mult, ALU.add))
                for _ in range(3):
                    ch.link(ve.tensor_tensor(q, y, y, ALU.mult))
                    ch.link(ve.scalar_tensor_tensor(q, q, -0.5, v, ALU.mult, ALU.mult))
                    ch.link(ve.scalar_tensor_tensor(y, q, 1.5, y, ALU.add, ALU.mult))
                for t in range(T):
                    last = ve.tensor_scalar(dst[:, t, :], src[:, t, :], mv[:, 0, t:t + 1], nr[:, 3, t:t + 1],
                                            ALU.subtract, ALU.mult)
                    if t < T - 1:
                        ch.add(last)
                if done is None:
                    ch.link(last)
                else:
                    last.then_inc(done, 1)

            def soft_logits(ch, e, mx, slope, done):
                if slope is not None:
                    ch.link(ve.scalar_tensor_tensor(e, e, slope, e, ALU.mult, ALU.max))
                ch.link(ve.tensor_reduce(mx, e, AX_X, ALU.max))
                ve.tensor_tensor(e, e, bc(col(mx), list(e.shape)), ALU.subtract).then_inc(done, 1)

            def soft_probs(ch, e, pr_, dn, done, ok=False):
                ch.link(ve.tensor_reduce(dn, e, AX_X, ALU.add))
                ch.link(ve.reciprocal(dn, dn))
                if ok:
                    ch.link(ve.tensor_scalar(dn, dn, row_ok[:, 0:1], None, ALU.mult))
                ve.tensor_tensor(pr_, e, bc(col(dn), list(e.shape)), ALU.mult).then_inc(done, 1)

            def low(pr_, hi, lo, done):
                for a, b in ((0, NODES), (NODES, P)):
                    ve.tensor_tensor(lo[a:b, :, a:b], pr_[a:b], hi[a:b, :, a:b], ALU.subtract).then_inc(done, 1)

            def diag(ch, f2, dst, tmp_hi, tmp_lo, n, done):
                ch.link(ve.tensor_copy(tmp_hi, f2))
                ch.link(ve.tensor_tensor(tmp_lo, f2, tmp_hi.bitcast(F32), ALU.subtract))
                for s, v in enumerate((tmp_hi.bitcast(F32), tmp_lo.bitcast(F32))):
                    ve.tensor_tensor(dst[s].rearrange("p (a n) -> p a n", n=NODES), bc(col(v), [P, n, NODES]),
                                     bc(eye2[:, :].rearrange("p (a n) -> p a n", a=1), [P, n, NODES]),
                                     ALU.mult).then_inc(done, 1)

            def l0(g):
                ca.start(g)
                A.arrived(dve, g, 0)
                A.release(ve.tensor_copy(f_raw, A.bank(0)[:, 0:16 * T].rearrange("p (t n) -> p t n", t=T)), 0)
                A.evacuated(dve, g, 0)
                ch = ca
                ch.link(ve.tensor_tensor(f_sum, f_raw[:, :, 0:8], f_raw[:, :, 8:16], ALU.add))
                ch.link(ve.tensor_copy(fsm_hi[:, :, :], f_sum[:, :, H0:2 * H0]))
                ch.link(ve.tensor_tensor(fsm_lo[:, :, :], f_sum[:, :, H0:2 * H0], fsm_hi[:, :, :].bitcast(F32), ALU.subtract))
                for s, v in enumerate((fsm_hi, fsm_lo)):
                    ve.tensor_tensor(dg[s].rearrange("p (a n) -> p a n", n=NODES),
                                     bc(col(v[:, :, :].bitcast(F32).rearrange("p t h -> p (t h)")), [P, T * H0, NODES]),
                                     bc(eye2[:, :].rearrange("p (a n) -> p a n", a=1), [P, T * H0, NODES]),
                                     ALU.mult).then_inc(diag_ready, 1)
                A.arrived(dve, g, 1)
                last = None
                for t in range(T):
                    last = ve.tensor_tensor(lg[:, t * H0:(t + 1) * H0, :],
                                            A.bank(1)[:, t * H0 * NODES:(t + 1) * H0 * NODES].rearrange("p (h n) -> p h n", h=H0),
                                            bc(col(f_sum[:, t, 0:H0]), [P, H0, NODES]), ALU.add)
                    if t < T - 1:
                        ch.link(last)
                A.release(last, 1)
                A.evacuated(dve, g, 1)
                soft_logits(ch, lg, rmax[:, 0, :], 0.01, logits_ready)
                dve.wait_ge(exp_ready, g + 1)
                soft_probs(ch, lg, pr, rden[:, 0, :], prob_ready)
                dve.wait_ge(prob_ready, g + 1)
                dve.wait_ge(ph_ready, 2 * g + 2)
                low(pr, pb[0][:, :, :], pb[1][:, :, :], pl_ready)
                A.arrived(dve, g, 3)
                A.release(ve.tensor_copy(pt0[:, :, 1, :], A.bank(3).bitcast(F16).rearrange("p (s n) -> p s n", s=2)), 3)
                for t in range(T):
                    for c in range(C):
                        u = 4 + C * t + c
                        dve.wait_ge(zt_hi, 4 * g + C * t + c + 1)
                        A.release(ve.tensor_tensor(zt[1][:, c, :, t * P:t * P + P],
                                                   A.bank(u).rearrange("p (h n) -> p h n", h=H0),
                                                   zt[0][:, c, :, t * P:t * P + P].bitcast(F32), ALU.subtract), u)

                def elu(n, u):
                    dve.wait_ge(ex_ready, 5 * g + n + 1)
                    ch.link(ve.tensor_scalar(ex[n % 2], ex[n % 2], 1.0, -1.0, ALU.min, ALU.add))
                    if n >= 2:
                        dve.wait_ge(ht_lo, 5 * g + n - 1)
                    last = ve.scalar_tensor_tensor(hf[n % 2], A.bank(u).rearrange("p (c n) -> p c n", c=C), 0.0,
                                                   ex[n % 2], ALU.max, ALU.add)
                    A.release(last, u)

                for h in range(H0):
                    elu(h, 8 + h)
                for t in range(T):
                    dve.wait_ge(wh2_hi, T * g + t + 1)
                    ch.link(ve.tensor_copy(g2[:, t, :], A.bank(12 + t)[:, D:D + 2]))
                    A.release(ve.tensor_tensor(wh2[1][:, t, :], A.bank(12 + t)[:, 0:D + 2],
                                               wh2[0][:, t, :].bitcast(F32), ALU.subtract), 12 + t)
                ch.link(ve.tensor_copy(fsm_hi[:, 0, 0:T], g2[:, :, 1]))
                ch.link(ve.tensor_tensor(fsm_lo[:, 0, 0:T], g2[:, :, 1], fsm_hi[:, 0, 0:T].bitcast(F32), ALU.subtract))
                for s, v in enumerate((fsm_hi, fsm_lo)):
                    ve.tensor_tensor(dg2[s].rearrange("p (a n) -> p a n", n=NODES),
                                     bc(col(v[:, 0, 0:T].bitcast(F32)), [P, T, NODES]),
                                     bc(eye2[:, :].rearrange("p (a n) -> p a n", a=1), [P, T, NODES]),
                                     ALU.mult).then_inc(diag2_ready, 1)
                e2 = lg[:, 0:T, :]
                A.arrived(dve, g, 14)
                A.release(ve.tensor_tensor(e2, A.bank(14)[:, 0:T * NODES].rearrange("p (t n) -> p t n", t=T),
                                           bc(g2[:, :, 0:1], [P, T, NODES]), ALU.add), 14)
                A.evacuated(dve, g, 14)
                soft_logits(ch, e2, rmax[:, 0, 0:T], 0.01, logits2_ready)
                dve.wait_ge(exp2_ready, g + 1)
                soft_probs(ch, e2, pr[:, 0:T, :], rden[:, 0, 0:T], prob2_ready)
                dve.wait_ge(prob2_ready, g + 1)
                dve.wait_ge(ph2_ready, 2 * g + 2)
                low(pr[:, 0:T, :], pb2[0][:, :, :], pb2[1][:, :, :], pl2_ready)
                elu(4, 16)
                A.arrived(dve, g, 18)
                A.release(ve.tensor_tensor(y0, A.bank(18).rearrange("p (t n) -> p t n", t=T),
                                           bc(b2_bc[:, :].rearrange("p (a n) -> p a n", a=1), [P, T, D]), ALU.add), 18)
                A.evacuated(dve, g, 18)
                layer_norm(ch, y0, z0, st0, mv0, nr0)
                ch.link(ve.tensor_tensor(z0, z0, bc(gamma_bc[:, :].rearrange("p (a n) -> p a n", a=1), [P, T, D]), ALU.mult))
                ch.link(ve.tensor_tensor(z0, z0, x_beta, ALU.add))
                layer_norm(ch, z0, x1, st0, mv0, nr0, xs_ready)
                dve.wait_ge(x16_hi, 3 * g + 1)
                ve.tensor_tensor(x16[:, 1], x1, x16[:, 0], ALU.subtract).then_inc(x16_lo, 1)
                ca.end()

            def l13(g):
                ch = cb
                cb.start(g)
                for u, dst, bias, hi in ((1, kt, bkc, k_hi), (2, qt, bqc, q_hi)):
                    dve.wait_ge(hi, g + 1)
                    for c in range(C):
                        last = ve.scalar_tensor_tensor(dst[1][:, c, :], B.bank(u)[:, c * G:(c + 1) * G], bias[:, c:c + 1],
                                                       dst[0][:, c, :].bitcast(F32), ALU.add, ALU.subtract)
                    B.release(last, u)
                dve.wait_ge(v_hi, g + 1)
                B.release(ve.tensor_tensor(vv[1][:, :, :], B.bank(3).rearrange("p (t n) -> p t n", t=T),
                                           vv[0][:, :, :].bitcast(F32), ALU.subtract), 3)
                for t in range(T):
                    for c in range(C):
                        u = 4 + C * t + c
                        B.arrived(dve, g, u)
                        s4 = B.bank(u).rearrange("p (h n) -> p h n", h=HC)
                        for a, b in ((0, NODES), (NODES, P)):
                            k0 = t * H1 + c * HC
                            last = ve.tensor_tensor(sc[a:b, k0:k0 + HC, :], s4[a:b, :, a:b],
                                                    bc(mask1[a:b, :].rearrange("p (a n) -> p a n", a=1), [NODES, HC, NODES]),
                                                    ALU.add)
                            if a == 0:
                                ch.link(last)
                        B.release(last, u)
                for u in range(4, 8):
                    B.evacuated(dve, g, u)
                soft_logits(ch, sc, smax[:, 0, :], None, s_ready)
                dve.wait_ge(s_exp, g + 1)
                soft_probs(ch, sc, sc, sden[:, 0, :], s_prob, ok=True)
                dve.wait_ge(s_prob, g + 1)
                dve.wait_ge(s_ph, 2 * g + 2)
                for a, b in ((0, NODES), (NODES, P)):
                    ve.tensor_tensor(pb1[1][a:b, :, :, a:b].rearrange("p t h n -> p (t h) n"), sc[a:b],
                                     pb1[0][a:b, :, :, a:b].rearrange("p t h n -> p (t h) n"), ALU.subtract).then_inc(s_pl, 1)
                for n in range(T * C):
                    t, c = n // C, n % C
                    u = 9 + 2 * n
                    B.arrived(dve, g, u)
                    for h in range(HC):
                        last = ve.tensor_copy(ot1[32 * h:32 * h + 32, c, t * P:t * P + P],
                                              B.bank(u)[32 * h:32 * h + 32, h * P:h * P + P])
                    B.release(last, u)
                B.evacuated(dve, g, 15)
                dve.wait_ge(o_hi, g + 1)
                for c in range(C):
                    last = ve.scalar_tensor_tensor(o1[1][:, c, :], ot1[:, c, :], bvc[:, c:c + 1],
                                                   o1[0][:, c, :].bitcast(F32), ALU.add, ALU.subtract)
                last.then_inc(o_lo, 1)
                dve.wait_ge(x1b_ready, 2 * g + 1)
                B.arrived(dve, g, 16)
                B.release(ve.tensor_tensor(y1, B.bank(16).rearrange("p (t n) -> p t n", t=T), x1b, ALU.add), 16)
                B.evacuated(dve, g, 16)
                layer_norm(ch, y1, x2, st1, mv1, nr1, xs_ready)
                dve.wait_ge(x16_hi, 3 * g + 2)
                ve.tensor_tensor(x16[:, 1], x2, x16[:, 0], ALU.subtract).then_inc(x16_lo, 1)
                dve.wait_ge(mj_hi, g + 1)
                B.release(ve.tensor_tensor(mj[1], B.bank(19).rearrange("p (t n) -> p t n", t=T),
                                           mj[0].bitcast(F32), ALU.subtract), 19)
                B.arrived(dve, g, 20)
                B.evacuated(dve, g, 18)
                B.release(ve.tensor_tensor(y1, B.bank(20).rearrange("p (t n) -> p t n", t=T), t1, ALU.add), 20)
                B.evacuated(dve, g, 20)
                dve.wait_ge(x1b_ready, 2 * g + 2)
                ch.link(ve.tensor_tensor(y1, y1, x2b, ALU.add))
                layer_norm(ch, y1, x3, st1, mv1, nr1, xs_ready)
                dve.wait_ge(x16_hi, 3 * g + 3)
                ve.tensor_tensor(x16[:, 1], x3, x16[:, 0], ALU.subtract).then_inc(x16_lo, 1)
                B.arrived(dve, g, 22)
                B.release(ve.tensor_copy(h3, B.bank(22)[:, 0:T * (D3 + 2)].rearrange("p (t n) -> p t n", t=T)), 22)
                B.evacuated(dve, g, 22)
                ch.link(ve.tensor_copy(fsm3_hi[:, :], h3[:, :, D3 + 1]))
                ch.link(ve.tensor_tensor(fsm3_lo[:, :], h3[:, :, D3 + 1], fsm3_hi[:, :].bitcast(F32), ALU.subtract))
                for s, v in enumerate((fsm3_hi, fsm3_lo)):
                    ve.tensor_tensor(dg3[s].rearrange("p (a n) -> p a n", n=NODES), bc(col(v[:, :].bitcast(F32)), [P, T, NODES]),
                                     bc(eye2[:, :].rearrange("p (a n) -> p a n", a=1), [P, T, NODES]),
                                     ALU.mult).then_inc(diag3_ready, 1)
                dve.wait_ge(h3_hi, g + 1)
                ch.link(ve.tensor_tensor(h3r[1], h3[:, :, 0:D3], h3r[0].bitcast(F32), ALU.subtract))
                B.arrived(dve, g, 23)
                B.release(ve.tensor_tensor(lg3, B.bank(23)[:, 0:T * NODES].rearrange("p (t n) -> p t n", t=T),
                                           bc(h3[:, :, D3:D3 + 1], [P, T, NODES]), ALU.add), 23)
                B.evacuated(dve, g, 23)
                soft_logits(ch, lg3, m3[:, 0, :], 0.2, logits3_ready)
                dve.wait_ge(exp3_ready, g + 1)
                soft_probs(ch, lg3, lg3, d3[:, 0, :], prob3_ready)
                dve.wait_ge(prob3_ready, g + 1)
                dve.wait_ge(ph3_ready, 2 * g + 2)
                low(lg3, pb3[0][:, :, :], pb3[1][:, :, :], pl3_ready)
                ch.link(ve.tensor_tensor(y1[:, :, D3:D], h3[:, :, 0:D3], x3[:, :, D3:D], ALU.add))
                B.arrived(dve, g, 25)
                B.release(ve.tensor_tensor(y1[:, :, 0:D3], B.bank(25)[:, 0:T * D3].rearrange("p (t n) -> p t n", t=T),
                                           x3[:, :, 0:D3], ALU.add), 25)
                B.evacuated(dve, g, 25)
                layer_norm_last(ch, g)
                cb.end()

            def layer_norm_last(ch, g):
                dve.wait_ge(stored, 16 * g + 16)
                layer_norm(ch, y1, res, st1, mv1, nr1, res_ready)

            with dve.Fori(0, groups) as g:
                l0(g)
                l13(g)

        @block.tensor
        def _(pe):
            te = nc.tensor

            def mm3(out, lhs, rhs, start, stop):
                te.matmul(out, lhs[0], rhs[0], start=start, stop=False)
                te.matmul(out, lhs[0], rhs[1], start=False, stop=False)
                return te.matmul(out, lhs[1], rhs[0], start=False, stop=stop)

            pe.wait_ge(set_dve, 16)
            pe.wait_ge(pool_set, 19)

            def l0(g):
                pe.wait_ge(x_split, 5 * g + 8)
                A.acquire(pe, g, 0)
                for t in range(T):
                    o = A.bank(0)[:, 16 * t:16 * t + 16]
                    cs = slice(t * P, t * P + P)
                    for c in range(C):
                        if c == C - 1:
                            for k in range(C):
                                te.matmul(o[:, 0:8], xt[1][:, k, cs], wa[:, k, 0, :], start=False, stop=False)
                        last = te.matmul(o, xt[0][:, c, cs], wa[:, c, :, :].rearrange("p s n -> p (s n)"),
                                         start=(c == 0), stop=(c == C - 1))
                A.filled(last, 0)
                pe.wait_ge(diag_ready, 2 * g + 2)
                A.acquire(pe, g, 1)
                te.matmul(A.bank(1), same[:, :], dg[0], start=True, stop=False)
                te.matmul(A.bank(1), same[:, :], dg[1], start=False, stop=False)
                A.filled(te.matmul(A.bank(1).rearrange("p (a n) -> p a n", n=NODES), ident[:, :],
                                   bc(mask0[:, :].rearrange("p (a n) -> p a n", a=1), [P, T * H0, NODES]),
                                   start=False, stop=True), 1)
                pe.wait_ge(ph_ready, 2 * g + 2)
                pe.wait_ge(pl_ready, 2 * g + 2)
                for t in range(T):
                    A.acquire(pe, g, 2 + t)
                    o = A.bank(2 + t).bitcast(F16)
                    for s in range(2):
                        for h in range(H0):
                            k = (s * H0 + h) * P
                            last = te.transpose(o[:, k:k + P], pb[s][:, t * H0 + h, :], ident16[:, :])
                    A.filled(last, 2 + t)
                pe.wait_ge(x_split, 5 * g + 10)
                for t in range(T):
                    A.evacuated(pe, g, 2 + t)
                    for c in range(C):
                        u = 4 + C * t + c
                        A.acquire(pe, g, u)
                        A.filled(mm3(A.bank(u), [xn[s][:, t, c * P:c * P + P] for s in range(2)],
                                     [pt0[:, s, t, :] for s in range(2)], True, True), u)
                for u in range(4, 8):
                    A.evacuated(pe, g, u)
                for h in range(H0):
                    u = 8 + h
                    A.acquire(pe, g, u)
                    for oc in range(C):
                        for c in range(C):
                            last = mm3(A.bank(u)[:, oc * G:oc * G + G],
                                       [wh[s][:, h, c, oc * P:oc * P + P] for s in range(2)],
                                       [zt[s][:, c, h, :] for s in range(2)], c == 0, c == C - 1)
                    A.filled(last, u)
                for t in range(T):
                    u = 12 + t
                    A.acquire(pe, g, u)
                    for k in range(H0 * C):
                        if t == 0 and k % C == 0:
                            pe.wait_ge(ht_lo, 5 * g + k // C + 1)
                        last = mm3(A.bank(u)[:, 0:D + 2], [ht[s][:, k, t * P:t * P + P] for s in range(2)],
                                   [wo[s][:, k, :] for s in range(2)], k == 0, k == H0 * C - 1)
                    A.filled(last, u)
                pe.wait_ge(diag2_ready, 2 * g + 2)
                A.acquire(pe, g, 14)
                o = A.bank(14)[:, 0:T * NODES]
                te.matmul(o, same[:, :], dg2[0], start=True, stop=False)
                te.matmul(o, same[:, :], dg2[1], start=False, stop=False)
                A.filled(te.matmul(o.rearrange("p (a n) -> p a n", n=NODES), ident[:, :],
                                   bc(mask0[:, :].rearrange("p (a n) -> p a n", a=1), [P, T, NODES]),
                                   start=False, stop=True), 14)
                pe.wait_ge(ph2_ready, 2 * g + 2)
                pe.wait_ge(pl2_ready, 2 * g + 2)
                A.acquire(pe, g, 15)
                o = A.bank(15).bitcast(F16)
                for s in range(2):
                    for t in range(T):
                        k = (s * T + t) * P
                        last = te.transpose(o[:, k:k + P], pb2[s][:, t, :], ident16[:, :])
                A.filled(last, 15)
                A.evacuated(pe, g, 15)
                A.evacuated(pe, g, 13)
                A.acquire(pe, g, 16)
                for c in range(C):
                    for t in range(T):
                        k = c * G + t * P
                        last = mm3(A.bank(16)[:, k:k + P], [wh2[s][:, t, c * P:c * P + P] for s in range(2)],
                                   [pt2[s][:, t, :] for s in range(2)], True, True)
                A.filled(last, 16)
                pe.wait_ge(ht_lo, 5 * g + 5)
                A.acquire(pe, g, 17)
                for oc in range(C):
                    for c in range(C):
                        last = mm3(A.bank(17)[:, oc * G:oc * G + G], [wf[s][:, 0, c, oc * P:oc * P + P] for s in range(2)],
                                   [ott[s][:, c, :] for s in range(2)], c == 0, c == C - 1)
                A.filled(last, 17)
                pe.wait_ge(hid_lo, g + 1)
                A.acquire(pe, g, 18)
                for t in range(T):
                    o = A.bank(18)[:, t * D:t * D + D]
                    cs = slice(t * P, t * P + P)
                    for c in range(C):
                        if c == C - 1:
                            for k in range(C):
                                for s in range(2):
                                    te.matmul(o[:, k * P:k * P + P], ott[s][:, k, cs], ident[:, :], start=False, stop=False)
                        last = mm3(o, [hdt[s][:, c, cs] for s in range(2)], [wf[s][:, 1, c, :] for s in range(2)],
                                   c == 0, c == C - 1)
                A.filled(last, 18)

            def cols(g, n, u):
                pe.wait_ge(x16_hi, 3 * g + n + 1)
                pe.wait_ge(x16_lo, 3 * g + n + 1)
                B.acquire(pe, g, u)
                o = B.bank(u).bitcast(F16)
                for s in range(2):
                    for c in range(C):
                        for t in range(T):
                            k = (s * C + c) * G + t * P
                            last = te.transpose(o[:, k:k + P], x16[:, s, t, c * P:c * P + P], ident16[:, :])
                B.filled(last, u)
                B.evacuated(pe, g, u)

            def rows(u, w, n, t0=0):
                for t in range(T):
                    for c in range(C):
                        last = mm3(B.bank(u)[:, t * n:t * n + n], [xt1[:, s, c, t * P:t * P + P] for s in range(2)],
                                   [w[s][:, c, :] for s in range(2)], c == 0, c == C - 1)
                B.filled(last, u)

            def l13(g):
                cols(g, 0, 0)
                for u, m in ((1, 1), (2, 0)):
                    B.acquire(pe, g, u)
                    for oc in range(C):
                        for c in range(C):
                            last = mm3(B.bank(u)[:, oc * G:oc * G + G], [wp[s][:, m, c, oc * P:oc * P + P] for s in range(2)],
                                       [xt1[:, s, c, :] for s in range(2)], c == 0, c == C - 1)
                    B.filled(last, u)
                B.acquire(pe, g, 3)
                rows(3, [wp[s][:, 2] for s in range(2)], D)
                B.evacuated(pe, g, 2)
                pe.wait_ge(kd_loaded, 128 * g + 128)
                for t in range(T):
                    for c in range(C):
                        u = 4 + C * t + c
                        B.acquire(pe, g, u)
                        B.filled(mm3(B.bank(u), [qt[s][:, c, t * P:t * P + P] for s in range(2)],
                                     [kd[s][:, c, t, :, :].rearrange("p h n -> p (h n)") for s in range(2)], True, True), u)
                pe.wait_ge(s_ph, 2 * g + 2)
                pe.wait_ge(s_pl, 2 * g + 2)

                def turn(n):
                    t, c = n // C, n % C
                    u = 8 + 2 * n
                    B.acquire(pe, g, u)
                    o = B.bank(u).bitcast(F16)
                    for s in range(2):
                        for h in range(HC):
                            k = (s * HC + h) * P
                            last = te.transpose(o[:, k:k + P], pb1[s][:, t, c * HC + h, :], ident16[:, :])
                    B.filled(last, u)

                def values(n):
                    t, c = n // C, n % C
                    u = 9 + 2 * n
                    B.acquire(pe, g, u)
                    B.evacuated(pe, g, u - 1)
                    B.filled(mm3(B.bank(u), [vv[s][:, t, c * P:c * P + P] for s in range(2)],
                                 [pt1[:, n % 2, s, :] for s in range(2)], True, True), u)

                turn(0)
                for n in range(T * C):
                    if n + 1 < T * C:
                        turn(n + 1)
                    values(n)
                pe.wait_ge(o_lo, g + 1)
                B.acquire(pe, g, 16)
                for t in range(T):
                    for c in range(C):
                        last = mm3(B.bank(16)[:, t * D:t * D + D], [o1[s][:, c, t * P:t * P + P] for s in range(2)],
                                   [wp[s][:, 3, c, :] for s in range(2)], c == 0, c == C - 1)
                B.filled(last, 16)
                cols(g, 1, 17)
                B.acquire(pe, g, 18)
                rows(18, [wm[s][:, 0] for s in range(2)], D)
                B.acquire(pe, g, 19)
                rows(19, [wm[s][:, 1] for s in range(2)], D)
                B.evacuated(pe, g, 19)
                B.acquire(pe, g, 20)
                for s in range(2):
                    last = te.matmul(B.bank(20), adj_t[:, :], mj[s].rearrange("p t n -> p (t n)"), start=(s == 0), stop=(s == 1))
                B.filled(last, 20)
                cols(g, 2, 21)
                B.acquire(pe, g, 22)
                rows(22, [w3[s][:, :, :] for s in range(2)], D3 + 2)
                pe.wait_ge(diag3_ready, 2 * g + 2)
                B.acquire(pe, g, 23)
                o = B.bank(23)[:, 0:T * NODES]
                te.matmul(o, same[:, :], dg3[0], start=True, stop=False)
                te.matmul(o, same[:, :], dg3[1], start=False, stop=False)
                B.filled(te.matmul(o.rearrange("p (a n) -> p a n", n=NODES), ident[:, :],
                                   bc(mask0[:, :].rearrange("p (a n) -> p a n", a=1), [P, T, NODES]),
                                   start=False, stop=True), 23)
                pe.wait_ge(ph3_ready, 2 * g + 2)
                pe.wait_ge(pl3_ready, 2 * g + 2)
                B.acquire(pe, g, 24)
                o = B.bank(24).bitcast(F16)
                for s in range(2):
                    for t in range(T):
                        k = (s * T + t) * P
                        last = te.transpose(o[:, k:k + P], pb3[s][:, t, :], ident16[:, :])
                B.filled(last, 24)
                B.evacuated(pe, g, 24)
                B.acquire(pe, g, 25)
                for t in range(T):
                    last = mm3(B.bank(25)[:, t * D3:t * D3 + D3], [pt3[s][:, t, :] for s in range(2)],
                               [h3r[s][:, t, :] for s in range(2)], True, True)
                B.filled(last, 25)

            with pe.Fori(0, groups) as g:
                l0(g)
                l13(g)


def kernel(x, adj, L0_gnn_W_heads, L0_gnn_a_heads, L0_gnn_W_out, L0_gnn_a_out, L0_gnn_w1, L0_gnn_b1, L0_gnn_w2,
           L0_gnn_b2, L0_gnn_ln_gamma, L0_gnn_ln_beta, L1_gnn_Wq, L1_gnn_bq, L1_gnn_Wk, L1_gnn_bk, L1_gnn_Wv,
           L1_gnn_bv, L1_gnn_Wo, L1_gnn_bo, L2_gnn_W, L2_gnn_b, L3_gnn_W, L3_gnn_a):
    import numpy as _np
    import concourse.bacc as _bacc
    from concourse import mybir as _mybir
    from concourse.bass_utils import run_bass_kernel_spmd as _run

    def lay(a):
        return _np.ascontiguousarray(a)

    def cols(b):
        return lay(_np.reshape(b, (2, 128)).T)

    x = _np.asarray(x)
    rows = x.reshape(-1, x.shape[-1])
    arrays = {
        "x": lay(rows), "xT": lay(rows.T), "adj": lay(adj), "adjT": lay(_np.transpose(adj)),
        "w_heads": lay(L0_gnn_W_heads), "a_heads": lay(L0_gnn_a_heads), "w_out": lay(L0_gnn_W_out), "a_out": lay(L0_gnn_a_out),
        "w1": lay(L0_gnn_w1), "b1": cols(L0_gnn_b1), "w2": lay(L0_gnn_w2), "b2": lay(L0_gnn_b2),
        "gamma": lay(L0_gnn_ln_gamma), "beta": lay(L0_gnn_ln_beta),
        "wqT": lay(_np.transpose(L1_gnn_Wq)), "bq": cols(L1_gnn_bq), "wkT": lay(_np.transpose(L1_gnn_Wk)), "bk": cols(L1_gnn_bk),
        "wvT": lay(_np.transpose(L1_gnn_Wv)), "bv": cols(L1_gnn_bv), "woT": lay(_np.transpose(L1_gnn_Wo)), "bo": lay(L1_gnn_bo),
        "wmT": lay(_np.transpose(L2_gnn_W)), "bm": lay(L2_gnn_b), "w3": lay(L3_gnn_W), "a3": lay(_np.reshape(L3_gnn_a, (2, 128))),
    }
    nc = _bacc.Bacc("TRN2", target_bir_lowering=False, num_devices=1)
    io = {n: nc.dram_tensor(n + "_dram", a.shape, _mybir.dt.from_np(a.dtype), kind="ExternalInput").ap()
          for n, a in arrays.items()}
    io["out"] = nc.dram_tensor("out_dram", rows.shape, _mybir.dt.float32, kind="ExternalOutput").ap()
    build_program(nc, io)
    r = _run(nc, [{n + "_dram": a for n, a in arrays.items()}], core_ids=[0])
    return r.results[0]["out_dram"].reshape(x.shape)
```

```python
from contextlib import ExitStack

import concourse.bass as bass
from concourse import mybir

F32 = mybir.dt.float32
F32R = mybir.dt.float32r
F16 = mybir.dt.float16
I32 = mybir.dt.int32
ALU = mybir.AluOpType
ACT = mybir.ActivationFunctionType
AX_X = mybir.AxisListType.X

P = 128
NODES = 64
D = 256
C = D // P
T = 2
G = T * P
H0 = 4
H1 = 8
HC = 4
DH = D // H1
D3 = 128
WORK = 9088
BIG = -(2.0 ** 100)
EPS = 1e-5
MAGIC = float(0x5F3759DF)


ORDER = {
    "pe": "ABBCADBCDBDAABCCADBADCBBDCADBADABCCDACAXBABBBDCACDCACDDDC",
    "act": "ABBCDAADBDBACCBADDCBACBDBDACBABDACCXDCDACACDACBABBDDDBCAC",
    "dve": "ABBCABDADCDDABCBDCBAACBBDBADCXCADABCBDCBACAABDCABCDDCDADC",
    "pool": "DBDBDAABCCCCADBBADCDCABDBBADCCBBCAXCBCABAABAADACDBDDCDDAC",
}


def take(order, **stages):
    at, done = dict.fromkeys(stages, 0), dict.fromkeys(stages, 0)
    for k in order:
        if k in stages:
            at[k] += 1
            while done[k] < at[k]:
                done[k] = next(stages[k], 99)
    assert min(done.values()) == 99, done


def idle(g, first=False):
    yield from ()


def pipeline(eng, order, groups, x, a, b, c, d):
    take(order, X=x(0, True))
    take(order, X=x(1), A=a(0, True))
    take(order, X=x(2), A=a(1), B=b(0, True))
    take(order, X=x(3), A=a(2), B=b(1), C=c(0, True))
    with eng.Fori(4, groups) as g:
        take(order, X=x(g), A=a(g - 1), B=b(g - 2), C=c(g - 3), D=d(g - 4))
    take(order, A=a(groups - 1), B=b(groups - 2), C=c(groups - 3), D=d(groups - 4))
    take(order, B=b(groups - 1), C=c(groups - 2), D=d(groups - 3))
    take(order, C=c(groups - 1), D=d(groups - 2))
    take(order, D=d(groups - 1))


class Banks:

    def __init__(self, tensor, full, free, uses):
        self.tensor, self.full, self.free, self.uses = tensor, full, free, uses
        self.n = len(full)

    def per_group(self, b):
        return (self.uses - b + self.n - 1) // self.n

    def bank(self, u):
        return self.tensor[:, u % self.n, :]

    def before(self, g, u):
        return g * self.per_group(u % self.n) + u // self.n + 1

    def acquire(self, pe, g, u):
        pe.wait_ge(self.free[u % self.n], self.before(g, u))

    def arrived(self, eng, g, u):
        eng.wait_ge(self.full[u % self.n], self.before(g, u))

    def evacuated(self, eng, g, u):
        eng.wait_ge(self.free[u % self.n], self.before(g, u) + 1)

    def filled(self, ins, u):
        ins.then_inc(self.full[u % self.n], 1)

    def release(self, ins, u):
        ins.then_inc(self.free[u % self.n], 1)


class Chain:

    def __init__(self, eng, sem, per_group):
        self.eng, self.sem, self.per_group = eng, sem, per_group

    def start(self, g):
        self.base, self.n = g * self.per_group, 0

    def add(self, ins):
        self.n += 1
        ins.then_inc(self.sem, 1)

    def link(self, ins):
        self.add(ins)
        self.eng.wait_ge(self.sem, self.base + self.n)

    def end(self):
        assert self.n == self.per_group, (self.n, self.per_group)


def build_program(nc, io):
    groups = io["x"].shape[0] // G
    with ExitStack() as ctx:
        def sb(name, shape, dt):
            return ctx.enter_context(nc.sbuf_tensor(name, shape, dt))

        def sem(name):
            return ctx.enter_context(nc.semaphore(name))

        def pair(name, shape):
            return sb(name + "_hi", shape, F32R), sb(name + "_lo", shape, F32R)

        wh = pair("w_heads", [P, H0, C, D])
        wo = pair("w_out", [P, H0 * C, D + 2])
        wf = pair("w_ffn", [P, 2, C, D])
        wp = pair("w_proj", [P, 4, C, D])
        wm = pair("w_msg", [P, 2, C, D])
        w3 = pair("w_last", [P, C, D3 + 2])
        wa = sb("w_att", [P, C, 2, 2 * H0], F32R)

        ident = sb("ident", [P, P], F32R)
        ident16 = sb("ident16", [P, P], F16)
        eye2 = sb("eye2", [P, NODES], F32)
        same = sb("same_graph", [P, P], F32R)
        mask0 = sb("mask0", [P, NODES], F32R)
        mask1 = sb("mask1", [P, NODES], F32)
        adj_t = sb("adj_t", [P, P], F32R)
        deg = sb("deg", [P, 1], F32)
        row_ok = sb("row_ok", [P, 1], F32)
        b2_bc = sb("b2_bc", [P, D], F32)
        gamma_bc = sb("gamma_bc", [P, D], F32)
        beta_bc = sb("beta_bc", [P, D], F32)
        bo_bc = sb("bo_bc", [P, D], F32)
        degb_bc = sb("degb_bc", [P, D], F32)
        b1c = sb("b1c", [P, C], F32)
        bqc = sb("bqc", [P, C], F32)
        bkc = sb("bkc", [P, C], F32)
        bvc = sb("bvc", [P, C], F32)

        work = sb("work", [P, WORK], F32)
        at = [0]

        def w32(*shape):
            n = 1
            for s in shape:
                n *= s
            v = work[:, at[0]:at[0] + n]
            at[0] += n
            if len(shape) == 2:
                v = v.rearrange("p (a b) -> p a b", a=shape[0])
            if len(shape) == 3:
                v = v.rearrange("p (a b c) -> p a b c", a=shape[0], b=shape[1])
            return v

        x_in = w32(T, D)
        xt_in = w32(C, G)
        f_raw = w32(T, 16)
        f_sum = w32(T, 8)
        rmax = w32(1, T * H0)
        rden = w32(1, T * H0)
        ex = [w32(C, G) for _ in range(2)]
        hf = [w32(C, G) for _ in range(2)]
        lg = ex[0].rearrange("p c n -> p (c n)").rearrange("p (a n) -> p a n", n=NODES)
        x_beta = w32(T, D)
        g2 = w32(T, 2)
        rmax2 = w32(1, T)
        rden2 = w32(1, T)
        ea = w32(C, G)
        eb = w32(C, G)
        lg2 = ea.rearrange("p c n -> p (c n)")[:, 0:T * NODES].rearrange("p (t n) -> p t n", t=T)
        hid = z0 = ea
        y0 = x1 = eb
        st0 = w32(T, 6)
        mv0 = w32(1, T)
        nr0 = w32(4, T)
        x1b = w32(T, D)
        sc = w32(T * H1, NODES)
        smax = w32(1, T * H1)
        sden = w32(1, T * H1)
        flat_sc = sc.rearrange("p a n -> p (a n)")
        y1 = ot1 = flat_sc[:, 0:T * D].rearrange("p (t n) -> p t n", t=T)
        x2 = flat_sc[:, T * D:2 * T * D].rearrange("p (t n) -> p t n", t=T)
        st1 = w32(T, 6)
        mv1 = w32(1, T)
        nr1 = w32(4, T)
        x2b = w32(T, D)
        x3 = w32(T, D)
        y2 = w32(T, D)
        flat_y2 = y2.rearrange("p t n -> p (t n)")
        h3 = flat_y2[:, 0:T * (D3 + 2)].rearrange("p (t n) -> p t n", t=T)
        lg3 = flat_y2[:, 288:288 + T * NODES].rearrange("p (t n) -> p t n", t=T)
        m3 = w32(1, T)
        d3 = w32(1, T)
        st2 = w32(T, 6)
        mv2 = w32(1, T)
        nr2 = w32(4, T)
        assert at[0] <= WORK, at

        raw_wh = work[:, 0:2048].rearrange("p (h c n) -> p h c n", h=H0, c=C)
        raw_wo = work[:, 2048:4096].rearrange("p (k n) -> p k n", k=H0 * C)
        raw_wp = work[:, 0:2048].rearrange("p (k c n) -> p k c n", k=4, c=C)
        raw_wf = work[:, 2048:3072].rearrange("p (k c n) -> p k c n", k=2, c=C)
        raw_wm = work[:, 3072:4096].rearrange("p (k c n) -> p k c n", k=2, c=C)
        raw_w3 = work[:, 4096:4352].rearrange("p (c n) -> p c n", c=C)
        raw_a = work[:, 4352:6400].rearrange("p (h k n) -> p h k n", h=H0, k=2)
        raw_ao = work[:, 6400:6912].rearrange("p (k n) -> p k n", k=2)
        raw_a3 = work[:, 6912:7168].rearrange("p (k n) -> p k n", k=2)
        junk = work[:, 7168:7424]
        wide = work[:, 7500:7500 + P]
        att_f = work[:, 7424:7440].rearrange("p (c n) -> p c n", c=C)
        out_f = work[:, 7440:7456].rearrange("p (k n) -> p k n", k=H0 * C)
        last_f = work[:, 7456:7460].rearrange("p (c n) -> p c n", c=C)
        adj_i = work[:, 7640:7704].bitcast(I32)
        adjt_i = work[:, 7704:7768].bitcast(I32)
        adj_f = work[:, 7768:7832]
        tmpc = work[:, 7840:7844]

        def rpair(name, shape):
            return sb(name + "_hi", shape, F32R), sb(name + "_lo", shape, F32R)

        xn = rpair("x_rows", [P, T, D])
        xt = rpair("x_cols", [P, C, G])
        dg = [xt[s][:, :, :].rearrange("p c n -> p (c n)") for s in range(2)]
        share = sb("share", [P, 2, C * H0 * G], F32R)
        zt = [share[:, s, :].rearrange("p (c h n) -> p c h n", c=C, h=H0) for s in range(2)]
        share2 = sb("share2", [P, 2, 1028], F32R)
        wh2 = [share2[:, s, 0:516].rearrange("p (t n) -> p t n", t=T) for s in range(2)]
        hdt = [share2[:, s, 0:512].rearrange("p (c n) -> p c n", c=C) for s in range(2)]
        dg2 = [share2[:, s, 516:644] for s in range(2)]
        pt2 = [share2[:, s, 644:900].rearrange("p (t n) -> p t n", t=T) for s in range(2)]
        ott = [share2[:, s, 516:1028].rearrange("p (c n) -> p c n", c=C) for s in range(2)]
        ht = rpair("heads", [P, H0 * C, G])
        pt0 = ht[0][:, :, :].rearrange("p k n -> p (k n)").rearrange("p (s t n) -> p s t n", s=2, t=T)
        one = sb("one", [P, 1], F32)
        three_halves = sb("three_halves", [P, 1], F32)
        fsm_hi = sb("fsm_hi", [P, T, H0], F32R)
        fsm_lo = sb("fsm_lo", [P, T, H0], F32R)
        fsm2_hi = sb("fsm2_hi", [P, T], F32R)
        fsm2_lo = sb("fsm2_lo", [P, T], F32R)
        fsm3_hi = sb("fsm3_hi", [P, T], F32R)
        fsm3_lo = sb("fsm3_lo", [P, T], F32R)
        pb = [sb(f"pb{s}", [P, T * H0, P], F16) for s in range(2)]
        pb2 = [sb(f"pb2{s}", [P, T, P], F16) for s in range(2)]
        pb1 = [sb(f"pb1{s}", [P, T, H1, P], F16) for s in range(2)]
        pb3 = [sb(f"pb3{s}", [P, T, P], F16) for s in range(2)]
        x16a = sb("x16a", [P, 2, T, D], F16)
        x16b = sb("x16b", [P, 2, T, D], F16)
        x16c = sb("x16c", [P, 2, T, D], F16)

        xt1 = sb("xt1", [P, 2, C, G], F32R)
        qt = rpair("qt", [P, C, G])
        kt = sb("kt", [P, 2, C, G], F32R)
        vv = rpair("v", [P, T, D])
        pt1_odd = sb("pt1", [P, 2, HC * P], F32R)
        pt1 = [kt[:, :, :, :].rearrange("p s c n -> p s (c n)"), pt1_odd[:, :, :]]
        o1 = qt

        xt2 = sb("xt2", [P, 2, C, G], F32R)
        share3 = sb("share3", [P, 2, 640], F32R)
        mj = [share3[:, s, 0:512].rearrange("p (t n) -> p t n", t=T) for s in range(2)]
        h3r = [share3[:, s, 0:256].rearrange("p (t n) -> p t n", t=T) for s in range(2)]
        dg3 = [share3[:, s, 256:384] for s in range(2)]
        pt3 = [share3[:, s, 384:640].rearrange("p (t n) -> p t n", t=T) for s in range(2)]

        psum = ctx.enter_context(nc.psum_tensor("psum", [P, 8, 512], F32))

        def ring(name, i, uses):
            return Banks(psum[:, i:i + 2, :], [sem(f"{name}_full{k}") for k in range(2)],
                         [sem(f"{name}_free{k}") for k in range(2)], uses)

        RA, RB, RC, RD = ring("a", 0, 12), ring("b", 2, 7), ring("c", 4, 17), ring("d", 6, 9)

        raw_loaded = sem("raw_loaded")
        const_loaded = sem("const_loaded")
        pool_set = sem("pool_set")
        set_act = sem("set_act")
        set_dve = sem("set_dve")
        set_chain = sem("set_chain")
        x_loaded = sem("x_loaded")
        x_split = sem("x_split")
        a_chain = sem("a_chain")
        b_chain = sem("b_chain")
        c_chain = sem("c_chain")
        d_chain = sem("d_chain")
        b_variance = sem("b_variance")
        c_variance = sem("c_variance")
        d_variance = sem("d_variance")
        b_newton = sem("b_newton")
        c_newton = sem("c_newton")
        d_newton = sem("d_newton")
        residual_loaded = sem("residual_loaded")
        residual_ready = sem("residual_ready")
        ex2_ready = sem("ex2_ready")
        att_hi = sem("att_hi")
        att_lo = sem("att_lo")
        scores_ready = sem("scores_ready")
        row_max_ready = sem("row_max_ready")
        row_sum_ready = sem("row_sum_ready")
        s_sum_ready = sem("s_sum_ready")
        diag_ready = sem("diag_ready")
        logits_ready = sem("logits_ready")
        exp_ready = sem("exp_ready")
        prob_ready = sem("prob_ready")
        ph_ready = sem("ph_ready")
        pl_ready = sem("pl_ready")
        zt_hi = sem("zt_hi")
        zt_lo = sem("zt_lo")
        ex_ready = sem("ex_ready")
        ht_hi = sem("ht_hi")
        ht_lo = sem("ht_lo")
        wh2_hi = sem("wh2_hi")
        wh2_lo = sem("wh2_lo")
        diag2_ready = sem("diag2_ready")
        logits2_ready = sem("logits2_ready")
        exp2_ready = sem("exp2_ready")
        prob2_ready = sem("prob2_ready")
        ph2_ready = sem("ph2_ready")
        pl2_ready = sem("pl2_ready")
        hid_hi = sem("hid_hi")
        hid_lo = sem("hid_lo")
        x1_ready = sem("x1_ready")
        x1_16hi = sem("x1_16hi")
        x1_16lo = sem("x1_16lo")
        x2_ready = sem("x2_ready")
        x3_ready = sem("x3_ready")
        x2_16hi = sem("x2_16hi")
        x2_16lo = sem("x2_16lo")
        x3_16hi = sem("x3_16hi")
        x3_16lo = sem("x3_16lo")
        x1b_ready = sem("x1b_ready")
        x2b_ready = sem("x2b_ready")
        q_hi = sem("q_hi")
        k_hi = sem("k_hi")
        v_hi = sem("v_hi")
        v_lo = sem("v_lo")
        s_ready = sem("s_ready")
        s_exp = sem("s_exp")
        s_prob = sem("s_prob")
        s_ph = sem("s_ph")
        s_pl = sem("s_pl")
        o_hi = sem("o_hi")
        o_lo = sem("o_lo")
        mj_hi = sem("mj_hi")
        mj_lo = sem("mj_lo")
        h3_hi = sem("h3_hi")
        diag3_ready = sem("diag3_ready")
        logits3_ready = sem("logits3_ready")
        exp3_ready = sem("exp3_ready")
        prob3_ready = sem("prob3_ready")
        ph3_ready = sem("ph3_ready")
        pl3_ready = sem("pl3_ready")
        res_ready = sem("res_ready")
        stored = sem("stored")

        x_rows = io["x"].rearrange("(g t p) n -> g p t n", t=T, p=P)
        x_cols = io["xT"].rearrange("(c p) (g n) -> g p c n", c=C, n=G)
        out_rows = io["out"].rearrange("(g t p) n -> g p t n", t=T, p=P)

        def bc(v, shape):
            return v.broadcast_to(shape)

        def col(v):
            return v.rearrange("p (n a) -> p n a", a=1)

        def row(name):
            return io[name].rearrange("(a n) -> a n", a=1)

        def own_heads(eng, copy, g, n):
            t, c = n // C, n % C
            u = 9 + 2 * n
            RC.arrived(eng, g, u)
            for h in range(HC):
                last = copy(ot1[32 * h:32 * h + 32, c, t * P:t * P + P], RC.bank(u)[32 * h:32 * h + 32, h * P:h * P + P])
            RC.release(last, u)

        RAW0, RAW1 = 6, 7

        block = ctx.enter_context(nc.Block())

        @block.sync
        def _(sp):
            def first(*pairs):
                for dst, src in pairs:
                    sp.dma_start(dst, src).then_inc(raw_loaded, 16)

            first((raw_wh, io["w_heads"].rearrange("h (c p) n -> p h c n", p=P)),
                  (raw_wo, io["w_out"].rearrange("(k p) n -> p k n", p=P)),
                  (raw_w3, io["w3"].rearrange("(c p) n -> p c n", p=P)),
                  (raw_a, io["a_heads"].rearrange("(a h) (k n) -> a h k n", a=1, k=2).broadcast_to([P, H0, 2, D])),
                  (raw_ao, io["a_out"].rearrange("(a k n) -> a k n", a=1, k=2).broadcast_to([P, 2, D])),
                  (raw_a3, io["a3"].rearrange("(a k) n -> a k n", a=1).broadcast_to([P, 2, D3])))
            sp.wait_ge(set_act, 6)
            sp.wait_ge(set_dve, 6)
            first((raw_wp[:, 0], io["wqT"].rearrange("(c p) n -> p c n", p=P)),
                  (raw_wp[:, 1], io["wkT"].rearrange("(c p) n -> p c n", p=P)),
                  (raw_wp[:, 2], io["wvT"].rearrange("(c p) n -> p c n", p=P)),
                  (raw_wp[:, 3], io["woT"].rearrange("(c p) n -> p c n", p=P)),
                  (raw_wf[:, 0], io["w1"].rearrange("(c p) n -> p c n", p=P)),
                  (raw_wf[:, 1], io["w2"].rearrange("(c p) n -> p c n", p=P)),
                  (raw_wm, io["wmT"].rearrange("(k c p) n -> p k c n", k=2, p=P)))
            sp.wait_ge(set_act, 9)
            sp.wait_ge(set_dve, 9)

            def rows(g, first=False):
                if not first:
                    sp.wait_ge(x_split, 4 * g)
                sp.dma_start(x_in, x_rows[g]).then_inc(x_loaded, 16)
                sp.dma_start(xt_in, x_cols[g]).then_inc(x_loaded, 16)

            def residual(g, first=False):
                if not first:
                    sp.wait_ge(x1_ready, g)
                sp.dma_start(x_beta, x_rows[g]).then_inc(residual_loaded, 16)

            def store(g):
                sp.wait_ge(res_ready, g + 1)
                sp.dma_start(out_rows[g], x3).then_inc(stored, 16)

            rows(0, first=True)
            rows(1)
            residual(0, first=True)
            rows(2)
            for g in (1, 2):
                residual(g)
                rows(g + 2)
            with sp.Fori(3, groups - 2) as g:
                residual(g)
                store(g - 3)
                rows(g + 2)
            residual(groups - 2)
            store(groups - 5)
            residual(groups - 1)
            for g in range(groups - 4, groups):
                store(g)
            sp.wait_ge(stored, 16 * groups)

        @block.gpsimd
        def _(pool):
            po = nc.gpsimd
            for dst, src in ((b2_bc[:, :], row("b2").broadcast_to([P, D])),
                             (gamma_bc[:, :], row("gamma").broadcast_to([P, D])),
                             (beta_bc[:, :], row("beta").broadcast_to([P, D])),
                             (bo_bc[:, :], row("bo").broadcast_to([P, D])),
                             (degb_bc[:, :], row("bm").broadcast_to([P, D])),
                             (adj_i[0:NODES, :], io["adj"]), (adj_i[NODES:P, :], io["adj"]),
                             (adjt_i[0:NODES, :], io["adjT"]), (adjt_i[NODES:P, :], io["adjT"])):
                pool.dma_start(dst, src).then_inc(const_loaded, 16)
            for n, (dst, src) in enumerate(((b1c, "b1"), (bqc, "bq"), (bkc, "bk"), (bvc, "bv"))):
                pool.dma_start(dst[:, :], io[src]).then_inc(const_loaded, 16)
            po.memset(wide, 0.0).then_inc(pool_set, 1)
            po.memset(eye2[:, :], 0.0).then_inc(pool_set, 1)
            po.memset(same[:, :].bitcast(F32), 0.0).then_inc(pool_set, 1)
            po.memset(adj_t[:, :].bitcast(F32), 0.0).then_inc(pool_set, 1)
            for t in (*pb, *pb1, *pb2, *pb3):
                v = t[tuple([slice(None)] * len(t.shape))]
                po.memset(v.bitcast(F32) if t.dtype == F32R else v, 0.0).then_inc(pool_set, 1)
            pool.wait_ge(pool_set, 12)
            po.affine_select(out=wide, in_=wide, compare_op=ALU.not_equal, fill=1.0, base=0,
                             pattern=[[-1, P]], channel_multiplier=1).then_inc(pool_set, 1)
            po.affine_select(out=eye2[:, :], in_=eye2[:, :], compare_op=ALU.not_equal, fill=1.0, base=0,
                             pattern=[[-1, NODES]], channel_multiplier=1).then_inc(pool_set, 1)
            pool.wait_ge(pool_set, 14)
            po.affine_select(out=eye2[:, :], in_=eye2[:, :], compare_op=ALU.not_equal, fill=1.0, base=-NODES,
                             pattern=[[-1, NODES]], channel_multiplier=1).then_inc(pool_set, 1)
            po.memset(three_halves[:, :], 1.5).then_inc(pool_set, 1)
            po.memset(one[:, :], 1.0).then_inc(pool_set, 1)
            po.tensor_copy(ident[:, :], wide).then_inc(pool_set, 1)
            po.tensor_copy(ident16[:, :], wide).then_inc(pool_set, 1)
            pool.wait_ge(pool_set, 19)
            pool.wait_ge(const_loaded, 16 * 13)
            pool.wait_ge(set_dve, 16)

            def newton(nr, variance, n_ready, steps, n0):
                v, q, y = nr[:, 0, :], nr[:, 1, :], nr[:, 3, :]
                pool.wait_ge(variance, n_ready)
                n = 0
                for _ in range(3):
                    for o, a, b, op in ((q, y, y, ALU.mult), (q, q, v, ALU.mult),
                                        (q, q, three_halves[:, 0:1].broadcast_to([P, T]), ALU.add), (y, y, q, ALU.mult)):
                        po.tensor_tensor(o, a, b, op).then_inc(steps, 1)
                        n += 1
                        if n < 12:
                            pool.wait_ge(steps, n0 + n)

            def split(g, first=False):
                if not first:
                    for u in range(4, 8):
                        RA.evacuated(pool, g - 1, u)
                pool.wait_ge(x_loaded, 32 * g + 32)
                po.tensor_tensor(xt[0][:, :, :], xt_in, bc(one[:, :].rearrange("p (a n) -> p a n", a=1), [P, C, G]), ALU.mult).then_inc(x_split, 1)
                po.tensor_scalar(xn[0][:, :, :], x_in, 1.0, None, ALU.mult).then_inc(x_split, 1)
                pool.wait_ge(x_split, 4 * g + 2)
                po.tensor_tensor(xt[1][:, :, :], xt_in, xt[0][:, :, :].bitcast(F32), ALU.subtract).then_inc(x_split, 1)
                po.tensor_tensor(xn[1][:, :, :], x_in, xn[0][:, :, :].bitcast(F32), ALU.subtract).then_inc(x_split, 1)
                yield from ()

            def heads(g, first=False):
                pool.wait_ge(scores_ready, g + 1)
                for s, v in enumerate((fsm_hi, fsm_lo)):
                    po.tensor_tensor(dg[s].rearrange("p (a n) -> p a n", n=NODES),
                                     bc(col(v[:, :, :].bitcast(F32).rearrange("p t h -> p (t h)")), [P, T * H0, NODES]),
                                     bc(eye2[:, :].rearrange("p (a n) -> p a n", a=1), [P, T * H0, NODES]),
                                     ALU.mult).then_inc(diag_ready, 1)
                yield 1
                pool.wait_ge(row_max_ready, g + 1)
                po.tensor_tensor(lg, lg, bc(col(rmax[:, 0, :]), [P, T * H0, NODES]), ALU.subtract).then_inc(logits_ready, 1)
                yield 2
                pool.wait_ge(row_sum_ready, g + 1)
                po.tensor_tensor(lg, lg, bc(col(rden[:, 0, :]), [P, T * H0, NODES]), ALU.mult).then_inc(prob_ready, 1)
                yield 8
                for h in range(H0):
                    pool.wait_ge(ht_hi, 4 * g + h + 1)
                    po.tensor_tensor(ht[1][:, C * h:C * h + C, :], hf[h % 2],
                                     ht[0][:, C * h:C * h + C, :].bitcast(F32), ALU.subtract).then_inc(ht_lo, 1)
                    yield 9 + h

            def rest(g, first=False):
                pool.wait_ge(residual_loaded, 16 * g + 16)
                po.tensor_tensor(x_beta, x_beta, bc(beta_bc[:, :].rearrange("p (a n) -> p a n", a=1), [P, T, D]),
                                 ALU.add).then_inc(residual_ready, 1)
                yield 7
                pool.wait_ge(att_hi, g + 1)
                po.tensor_tensor(ott[1], eb, ott[0].bitcast(F32), ALU.subtract).then_inc(att_lo, 1)
                yield 8
                pool.wait_ge(hid_hi, g + 1)
                po.tensor_tensor(hdt[1], hid, hdt[0].bitcast(F32), ALU.subtract).then_inc(hid_lo, 1)
                yield 10
                newton(nr0, b_variance, 2 * g + 1, b_newton, 24 * g)
                yield 12
                newton(nr0, b_variance, 2 * g + 2, b_newton, 24 * g + 12)
                yield 13
                pool.wait_ge(x1_16hi, g + 1)
                po.tensor_tensor(x16a[:, 1], x1, x16a[:, 0], ALU.subtract).then_inc(x1_16lo, 1)

            def dots(g, first=False):
                pool.wait_ge(x1_ready, g + 1)
                po.tensor_tensor(x1b, x1, bc(bo_bc[:, :].rearrange("p (a n) -> p a n", a=1), [P, T, D]),
                                 ALU.add).then_inc(x1b_ready, 1)
                yield 4
                pool.wait_ge(s_sum_ready, g + 1)
                po.tensor_tensor(sc, sc, bc(col(sden[:, 0, :]), [P, T * H1, NODES]), ALU.mult).then_inc(s_prob, 1)
                yield 11
                newton(nr1, c_variance, g + 1, c_newton, 12 * g)
                yield 12
                pool.wait_ge(x2_16hi, g + 1)
                po.tensor_tensor(x16b[:, 1], x2, x16b[:, 0], ALU.subtract).then_inc(x2_16lo, 1)
                if not first:
                    RD.evacuated(pool, g - 1, 1)
                po.tensor_tensor(x2b, x2, bc(degb_bc[:, :].rearrange("p (a n) -> p a n", a=1), [P, T, D]),
                                 ALU.add).then_inc(x2b_ready, 1)

            def last(g, first=False):
                yield 3
                newton(nr2, d_variance, 2 * g + 1, d_newton, 24 * g)
                yield 4
                pool.wait_ge(x3_16hi, g + 1)
                po.tensor_tensor(x16c[:, 1], x3, x16c[:, 0], ALU.subtract).then_inc(x3_16lo, 1)
                yield 11
                newton(nr2, d_variance, 2 * g + 2, d_newton, 24 * g + 12)

            pipeline(pool, ORDER['pool'], groups, split, heads, rest, dots, last)

        @block.scalar
        def _(act):
            sc_ = nc.scalar
            act.wait_ge(raw_loaded, 16 * RAW0)
            sc_.activation(wh[0][:, :, :, :], raw_wh, ACT.Copy).then_inc(set_act, 1)
            sc_.activation(wo[0][:, :, 0:D], raw_wo, ACT.Copy).then_inc(set_act, 1)
            sc_.activation(w3[0][:, :, 0:D3], raw_w3, ACT.Copy).then_inc(set_act, 1)
            act.wait_ge(set_chain, 16 + 16 + 4)
            for src, dst in ((att_f, wa[:, :, 0, :]), (out_f, wo[0][:, :, D:D + 2]), (last_f, w3[0][:, :, D3:D3 + 2])):
                sc_.activation(dst, src, ACT.Copy).then_inc(set_act, 1)
            act.wait_ge(raw_loaded, 16 * (RAW0 + RAW1))
            for dst, src in ((wf[0], raw_wf), (wp[0], raw_wp), (wm[0], raw_wm)):
                sc_.activation(dst[:, :, :, :], src, ACT.Copy).then_inc(set_act, 1)

            act.wait_ge(const_loaded, 16 * 13)
            act.wait_ge(pool_set, 19)
            act.wait_ge(set_dve, 16)

            def softmax_parts(eng, g, logits, ready, exp_done, n=1, scale=1.0):
                eng.wait_ge(ready, n * g + n)
                sc_.activation(logits, logits, ACT.Exp, scale=scale).then_inc(exp_done, 1)

            def high(g, src, dst, ready, done):
                act.wait_ge(ready, g + 1)
                sc_.activation(dst[0:NODES, :, 0:NODES], src[0:NODES], ACT.Copy).then_inc(done, 1)
                sc_.activation(dst[NODES:P, :, NODES:P], src[NODES:P], ACT.Copy).then_inc(done, 1)

            def heads(g, first=False):
                yield 2
                softmax_parts(act, g, lg, logits_ready, exp_ready)
                yield 3
                high(g, lg, pb[0][:, :, :], prob_ready, ph_ready)
                yield 4
                if not first:
                    RB.arrived(act, g - 1, 0)
                    RB.arrived(act, g - 1, 1)
                for t in range(T):
                    RA.arrived(act, g, 2 + t)
                    RA.release(sc_.activation(pt0[:, :, t, :], RA.bank(2 + t).bitcast(F16).rearrange("p (s n) -> p s n", s=2),
                                              ACT.Copy), 2 + t)
                yield 5
                for t in range(T):
                    for c in range(C):
                        u = 4 + C * t + c
                        RA.arrived(act, g, u)
                        sc_.activation(zt[0][:, c, :, t * P:t * P + P], RA.bank(u).rearrange("p (h n) -> p h n", h=H0),
                                       ACT.Copy).then_inc(zt_hi, 1)
                    yield 6 + t

                def elu_exp(n):
                    RA.arrived(act, g, 8 + n)
                    if n >= 2:
                        RA.evacuated(act, g, 8 + n - 2)
                    sc_.activation(ex[n % 2], RA.bank(8 + n).rearrange("p (c n) -> p c n", c=C), ACT.Exp).then_inc(ex_ready, 1)

                elu_exp(0)
                yield 8
                for h in range(H0):
                    if h + 1 < H0:
                        elu_exp(h + 1)
                    RA.evacuated(act, g, 8 + h)
                    sc_.activation(ht[0][:, C * h:C * h + C, :], hf[h % 2], ACT.Copy).then_inc(ht_hi, 1)
                    yield 9 + h

            def rest(g, first=False):
                for t in range(T):
                    RB.arrived(act, g, t)
                    sc_.activation(wh2[0][:, t, :], RB.bank(t)[:, 0:D + 2], ACT.Copy).then_inc(wh2_hi, 1)
                    yield 1 + t
                yield 3
                softmax_parts(act, g, lg2, logits2_ready, exp2_ready)
                yield 4
                high(g, lg2, pb2[0], prob2_ready, ph2_ready)
                yield 5
                RB.arrived(act, g, 3)
                for s in range(2):
                    last = sc_.activation(pt2[s], RB.bank(3).bitcast(F16)[:, s * T * P:(s + 1) * T * P]
                                          .rearrange("p (t n) -> p t n", t=T), ACT.Copy)
                RB.release(last, 3)
                yield 6
                RB.arrived(act, g, 4)
                sc_.activation(ea, RB.bank(4).rearrange("p (c n) -> p c n", c=C), ACT.Exp).then_inc(ex2_ready, 1)
                yield 7
                RB.evacuated(act, g, 4)
                sc_.activation(ott[0], eb, ACT.Copy).then_inc(att_hi, 1)
                yield 8
                RB.arrived(act, g, 5)
                for c in range(C):
                    last = sc_.activation(hid[:, c, :], RB.bank(5)[:, c * G:(c + 1) * G], ACT.Relu, bias=b1c[:, c:c + 1])
                RB.release(last, 5)
                RB.evacuated(act, g, 5)
                sc_.activation(hdt[0], hid, ACT.Copy).then_inc(hid_hi, 1)
                yield 13
                if not first:
                    RC.arrived(act, g - 1, 0)
                act.wait_ge(x1_ready, g + 1)
                sc_.activation(x16a[:, 0], x1, ACT.Copy).then_inc(x1_16hi, 1)

            def cols(ring, g, u, dst):
                ring.arrived(act, g, u)
                ring.release(sc_.activation(dst[:, :, :, :].rearrange("p s c n -> p (s c n)"),
                                            ring.bank(u).bitcast(F16), ACT.Copy), u)

            def dots(g, first=False):
                cols(RC, g, 0, xt1)
                for u, dst, bias, done in ((1, kt[:, 0], bkc, k_hi), (2, qt[0][:, :, :], bqc, q_hi)):
                    RC.arrived(act, g, u)
                    for c in range(C):
                        last = sc_.activation(dst[:, c, :], RC.bank(u)[:, c * G:(c + 1) * G], ACT.Identity,
                                              bias=bias[:, c:c + 1])
                    last.then_inc(done, 1)
                RC.arrived(act, g, 3)
                sc_.activation(vv[0][:, :, :], RC.bank(3).rearrange("p (t n) -> p t n", t=T), ACT.Copy).then_inc(v_hi, 1)
                yield 4
                softmax_parts(act, g, sc, s_ready, s_exp, scale=DH ** -0.5)
                yield 5
                act.wait_ge(s_prob, g + 1)
                for a, b in ((0, NODES), (NODES, P)):
                    sc_.activation(pb1[0][a:b, :, :, a:b].rearrange("p t h n -> p (t h) n"), sc[a:b], ACT.Copy).then_inc(s_ph, 1)
                yield 6

                def turned(n):
                    RC.arrived(act, g, 8 + 2 * n)
                    if n >= 2:
                        RC.arrived(act, g, 9 + 2 * (n - 2))
                    RC.release(sc_.activation(pt1[n % 2], RC.bank(8 + 2 * n).bitcast(F16).rearrange("p (s n) -> p s n", s=2),
                                              ACT.Copy), 8 + 2 * n)

                turned(0)
                for n in range(T * C):
                    if n + 1 < T * C:
                        turned(n + 1)
                    if n % C == 0:
                        own_heads(act, sc_.copy, g, n)
                    yield 7 + n
                for n in range(T * C):
                    RC.evacuated(act, g, 9 + 2 * n)
                for c in range(C):
                    last = sc_.activation(o1[0][:, c, :], ot1[:, c, :], ACT.Identity, bias=bvc[:, c:c + 1])
                last.then_inc(o_hi, 1)
                yield 12
                if not first:
                    RD.arrived(act, g - 1, 0)
                act.wait_ge(x2_ready, g + 1)
                sc_.activation(x16b[:, 0], x2, ACT.Copy).then_inc(x2_16hi, 1)

            def last(g, first=False):
                cols(RD, g, 0, xt2)
                RD.arrived(act, g, 2)
                sc_.activation(mj[0], RD.bank(2).rearrange("p (t n) -> p t n", t=T), ACT.Copy).then_inc(mj_hi, 1)
                yield 4
                act.wait_ge(x3_ready, g + 1)
                sc_.activation(x16c[:, 0], x3, ACT.Copy).then_inc(x3_16hi, 1)
                yield 5
                cols(RD, g, 4, xt2)
                RD.evacuated(act, g, 5)
                sc_.activation(h3r[0], h3[:, :, 0:D3], ACT.Copy).then_inc(h3_hi, 1)
                yield 7
                softmax_parts(act, g, lg3, logits3_ready, exp3_ready)
                yield 8
                high(g, lg3, pb3[0], prob3_ready, ph3_ready)
                yield 9
                RD.arrived(act, g, 7)
                for s in range(2):
                    last = sc_.activation(pt3[s], RD.bank(7).bitcast(F16)[:, s * T * P:(s + 1) * T * P]
                                          .rearrange("p (t n) -> p t n", t=T), ACT.Copy)
                RD.release(last, 7)

            pipeline(act, ORDER['act'], groups, idle, heads, rest, dots, last)

        @block.vector
        def _(dve):
            ve = nc.vector
            for bank in (*RA.free, *RB.free, *RC.free, *RD.free):
                dve.sem_inc(bank, 1)
            setup = Chain(dve, set_chain, 0)
            setup.start(0)
            dve.wait_ge(raw_loaded, 16 * RAW0)
            for c in range(C):
                for h in range(H0):
                    for k in range(2):
                        setup.link(ve.tensor_tensor_reduce(junk, raw_wh[:, h, c, :], raw_a[:, h, k, :], 1.0, 0.0,
                                                           ALU.mult, ALU.add, att_f[:, c, k * H0 + h:k * H0 + h + 1]))
            for q in range(H0 * C):
                for k in range(2):
                    setup.link(ve.tensor_tensor_reduce(junk, raw_wo[:, q, :], raw_ao[:, k, :], 1.0, 0.0,
                                                       ALU.mult, ALU.add, out_f[:, q, k:k + 1]))
            for c in range(C):
                for k in range(2):
                    setup.link(ve.tensor_tensor_reduce(junk[:, 0:D3], raw_w3[:, c, :], raw_a3[:, k, :], 1.0, 0.0,
                                                       ALU.mult, ALU.add, last_f[:, c, k:k + 1]))
            dve.wait_ge(set_act, 6)
            ve.tensor_tensor(wh[1][:, :, :, :], raw_wh, wh[0][:, :, :, :].bitcast(F32), ALU.subtract).then_inc(set_dve, 1)
            ve.tensor_tensor(wo[1][:, :, 0:D], raw_wo, wo[0][:, :, 0:D].bitcast(F32), ALU.subtract).then_inc(set_dve, 1)
            ve.tensor_tensor(w3[1][:, :, 0:D3], raw_w3, w3[0][:, :, 0:D3].bitcast(F32), ALU.subtract).then_inc(set_dve, 1)
            ve.tensor_tensor(wo[1][:, :, D:D + 2], out_f, wo[0][:, :, D:D + 2].bitcast(F32), ALU.subtract).then_inc(set_dve, 1)
            ve.tensor_tensor(w3[1][:, :, D3:D3 + 2], last_f, w3[0][:, :, D3:D3 + 2].bitcast(F32), ALU.subtract).then_inc(set_dve, 1)
            ve.tensor_tensor(wa[:, :, 1, :], att_f, wa[:, :, 0, :].bitcast(F32), ALU.subtract).then_inc(set_dve, 1)
            dve.wait_ge(set_act, 9)
            for w, src in ((wf, raw_wf), (wp, raw_wp), (wm, raw_wm)):
                ve.tensor_tensor(w[1][:, :, :, :], src, w[0][:, :, :, :].bitcast(F32), ALU.subtract).then_inc(set_dve, 1)
            dve.wait_ge(pool_set, 19)
            ve.memset(same[0:NODES, 0:NODES].bitcast(F32), 1.0).then_inc(set_dve, 1)
            ve.memset(same[NODES:P, NODES:P].bitcast(F32), 1.0).then_inc(set_dve, 1)
            dve.wait_ge(const_loaded, 16 * 13)
            setup.link(ve.tensor_copy(adj_f, adj_i))
            ve.tensor_scalar(mask0[:, :], adj_f, 0.0, BIG, ALU.is_le, ALU.mult).then_inc(set_dve, 1)
            ve.tensor_scalar(mask1[:, :], adj_f, 0.0, BIG, ALU.is_equal, ALU.mult).then_inc(set_dve, 1)
            ve.tensor_copy(adj_t[0:NODES, 0:NODES], adjt_i[0:NODES, :]).then_inc(set_dve, 1)
            ve.tensor_copy(adj_t[NODES:P, NODES:P], adjt_i[NODES:P, :]).then_inc(set_dve, 1)
            setup.link(ve.tensor_reduce(deg[:, :], adj_f, AX_X, ALU.add))
            setup.link(ve.tensor_scalar(adj_f, adj_f, 0.0, None, ALU.not_equal))
            setup.link(ve.tensor_reduce(tmpc[:, 0:1], adj_f, AX_X, ALU.add))
            setup.link(ve.reciprocal(tmpc[:, 1:2], tmpc[:, 0:1]))
            setup.link(ve.tensor_tensor(tmpc[:, 2:3], tmpc[:, 0:1], tmpc[:, 1:2], ALU.mult))
            setup.link(ve.tensor_scalar(row_ok[:, :], tmpc[:, 2:3], 0.0, 1.0, ALU.mult, ALU.add))
            ve.tensor_scalar(degb_bc[:, :], degb_bc[:, :], deg[:, 0:1], None, ALU.mult).then_inc(set_dve, 1)
            dve.wait_ge(set_dve, 16)

            ch_a = Chain(dve, a_chain, 9)
            ch_b = Chain(dve, b_chain, 36)
            ch_c = Chain(dve, c_chain, 19)
            ch_d = Chain(dve, d_chain, 32)

            def norm_stats(ch, src, st, mv, nr, done):
                for t in range(T):
                    (ch.link if t == T - 1 else ch.add)(ve.bn_stats(st[:, t, :], src[:, t, :]))
                me, se, mo, so = (st[:, :, k] for k in (1, 2, 4, 5))
                v, q, d, y = (nr[:, k, :] for k in range(4))
                mean = mv[:, 0, :]
                ch.add(ve.tensor_tensor(d, me, mo, ALU.subtract))
                ch.link(ve.tensor_tensor(v, se, so, ALU.add))
                ch.add(ve.tensor_scalar(v, v, 1.0 / D, EPS, ALU.mult, ALU.add))
                ch.link(ve.tensor_tensor(d, d, d, ALU.mult))
                ch.add(ve.tensor_tensor(mean, me, mo, ALU.add))
                ch.link(ve.scalar_tensor_tensor(v, d, 0.25, v, ALU.mult, ALU.add))
                ch.add(ve.tensor_scalar(q.bitcast(I32), v.bitcast(I32), 1, None, ALU.logical_shift_right))
                ch.link(ve.tensor_scalar(mean, mean, 0.5, None, ALU.mult))
                ch.add(ve.tensor_scalar(y.bitcast(I32), q.bitcast(I32), -1.0, MAGIC, ALU.mult, ALU.add))
                ve.tensor_scalar(v, v, -0.5, None, ALU.mult).then_inc(done, 1)

            def norm_apply(src, dst, mv, nr, steps, n, add):
                dve.wait_ge(steps, n)
                for t in range(T):
                    add[t](ve.tensor_scalar(dst[:, t, :], src[:, t, :], mv[:, 0, t:t + 1], nr[:, 3, t:t + 1],
                                            ALU.subtract, ALU.mult))

            def leaky_max(ch, e, mx, slope, last=None):
                if slope is not None:
                    ch.link(ve.scalar_tensor_tensor(e, e, slope, e, ALU.mult, ALU.max))
                ins = ve.tensor_reduce(mx, e, AX_X, ALU.max)
                if last is None:
                    ch.link(ins)
                else:
                    ins.then_inc(last, 1)

            def soft_logits(ch, e, mx, slope, done):
                leaky_max(ch, e, mx, slope)
                ve.tensor_tensor(e, e, bc(col(mx), list(e.shape)), ALU.subtract).then_inc(done, 1)

            def inverse_sum(ch, e, dn, ok=False, last=None):
                ch.link(ve.tensor_reduce(dn, e, AX_X, ALU.add))
                if ok:
                    ch.link(ve.tensor_scalar(dn, dn, row_ok[:, 0:1], None, ALU.mult))
                ins = ve.reciprocal(dn, dn)
                if last is None:
                    ch.link(ins)
                else:
                    ins.then_inc(last, 1)

            def soft_probs(ch, e, pr_, dn, done):
                inverse_sum(ch, e, dn)
                ve.tensor_tensor(pr_, e, bc(col(dn), list(e.shape)), ALU.mult).then_inc(done, 1)

            def low(pr_, hi, lo, done):
                for a, b in ((0, NODES), (NODES, P)):
                    ve.tensor_tensor(lo[a:b, :, a:b], pr_[a:b], hi[a:b, :, a:b], ALU.subtract).then_inc(done, 1)

            def heads(g, first=False):
                ch = ch_a
                ch.start(g)
                RA.arrived(dve, g, 0)
                RA.release(ve.tensor_copy(f_raw, RA.bank(0)[:, 0:16 * T].rearrange("p (t n) -> p t n", t=T)), 0)
                RA.evacuated(dve, g, 0)
                ch.link(ve.tensor_tensor(f_sum, f_raw[:, :, 0:8], f_raw[:, :, 8:16], ALU.add))
                ch.link(ve.tensor_copy(fsm_hi[:, :, :], f_sum[:, :, H0:2 * H0]))
                ve.tensor_tensor(fsm_lo[:, :, :], f_sum[:, :, H0:2 * H0], fsm_hi[:, :, :].bitcast(F32),
                                 ALU.subtract).then_inc(scores_ready, 1)
                yield 1
                RA.arrived(dve, g, 1)
                for t in range(T):
                    last = ve.tensor_tensor(lg[:, t * H0:(t + 1) * H0, :],
                                            RA.bank(1)[:, t * H0 * NODES:(t + 1) * H0 * NODES].rearrange("p (h n) -> p h n", h=H0),
                                            bc(col(f_sum[:, t, 0:H0]), [P, H0, NODES]), ALU.add)
                    if t < T - 1:
                        ch.add(last)
                RA.release(last, 1)
                RA.evacuated(dve, g, 1)
                leaky_max(ch, lg, rmax[:, 0, :], 0.01, row_max_ready)
                yield 2
                dve.wait_ge(exp_ready, g + 1)
                inverse_sum(ch, lg, rden[:, 0, :], last=row_sum_ready)
                yield 3
                dve.wait_ge(prob_ready, g + 1)
                dve.wait_ge(ph_ready, 2 * g + 2)
                low(lg, pb[0][:, :, :], pb[1][:, :, :], pl_ready)
                yield 5
                for t in range(T):
                    for c in range(C):
                        u = 4 + C * t + c
                        dve.wait_ge(zt_hi, 4 * g + C * t + c + 1)
                        RA.release(ve.tensor_tensor(zt[1][:, c, :, t * P:t * P + P],
                                                   RA.bank(u).rearrange("p (h n) -> p h n", h=H0),
                                                   zt[0][:, c, :, t * P:t * P + P].bitcast(F32), ALU.subtract), u)
                    yield 6 + t

                def elu(n, u):
                    dve.wait_ge(ex_ready, 4 * g + n + 1)
                    ch.link(ve.tensor_scalar(ex[n % 2], ex[n % 2], 1.0, -1.0, ALU.min, ALU.add))
                    if n >= 2:
                        dve.wait_ge(ht_lo, 4 * g + n - 1)
                    RA.release(ve.scalar_tensor_tensor(hf[n % 2], RA.bank(u).rearrange("p (c n) -> p c n", c=C), 0.0,
                                                      ex[n % 2], ALU.max, ALU.add), u)

                for h in range(H0):
                    elu(h, 8 + h)
                    yield 8 + h
                ch.end()

            def rest(g, first=False):
                ch = ch_b
                ch.start(g)
                for t in range(T):
                    dve.wait_ge(wh2_hi, T * g + t + 1)
                    ch.add(ve.tensor_copy(g2[:, t, :], RB.bank(t)[:, D:D + 2]))
                    RB.release(ve.tensor_tensor(wh2[1][:, t, :], RB.bank(t)[:, 0:D + 2],
                                               wh2[0][:, t, :].bitcast(F32), ALU.subtract), t)
                    yield 1 + t
                RB.evacuated(dve, g, 1)
                ch.link(ve.tensor_copy(fsm2_hi[:, :], g2[:, :, 1]))
                ch.link(ve.tensor_tensor(fsm2_lo[:, :], g2[:, :, 1], fsm2_hi[:, :].bitcast(F32), ALU.subtract))
                for s, v in enumerate((fsm2_hi, fsm2_lo)):
                    ve.tensor_tensor(dg2[s].rearrange("p (a n) -> p a n", n=NODES),
                                     bc(col(v[:, :].bitcast(F32)), [P, T, NODES]),
                                     bc(eye2[:, :].rearrange("p (a n) -> p a n", a=1), [P, T, NODES]),
                                     ALU.mult).then_inc(diag2_ready, 1)
                RB.arrived(dve, g, 2)
                RB.release(ve.tensor_tensor(lg2, RB.bank(2)[:, 0:T * NODES].rearrange("p (t n) -> p t n", t=T),
                                           bc(g2[:, :, 0:1], [P, T, NODES]), ALU.add), 2)
                RB.evacuated(dve, g, 2)
                soft_logits(ch, lg2, rmax2[:, 0, :], 0.01, logits2_ready)
                yield 3
                dve.wait_ge(exp2_ready, g + 1)
                soft_probs(ch, lg2, lg2, rden2[:, 0, :], prob2_ready)
                yield 4
                dve.wait_ge(prob2_ready, g + 1)
                dve.wait_ge(ph2_ready, 2 * g + 2)
                low(lg2, pb2[0], pb2[1], pl2_ready)
                yield 7
                dve.wait_ge(ex2_ready, g + 1)
                ch.link(ve.tensor_scalar(ea, ea, 1.0, -1.0, ALU.min, ALU.add))
                if not first:
                    dve.wait_ge(x1b_ready, g)
                RB.release(ve.scalar_tensor_tensor(eb, RB.bank(4).rearrange("p (c n) -> p c n", c=C), 0.0,
                                                   ea, ALU.max, ALU.add), 4)
                yield 9
                RB.arrived(dve, g, 6)
                RB.release(ve.tensor_tensor(y0, RB.bank(6).rearrange("p (t n) -> p t n", t=T),
                                           bc(b2_bc[:, :].rearrange("p (a n) -> p a n", a=1), [P, T, D]), ALU.add), 6)
                RB.evacuated(dve, g, 6)
                norm_stats(ch, y0, st0, mv0, nr0, b_variance)
                yield 11
                norm_apply(y0, z0, mv0, nr0, b_newton, 24 * g + 12, [ch.add, ch.link])
                ch.link(ve.tensor_tensor(z0, z0, bc(gamma_bc[:, :].rearrange("p (a n) -> p a n", a=1), [P, T, D]), ALU.mult))
                dve.wait_ge(residual_ready, g + 1)
                ch.link(ve.tensor_tensor(z0, z0, x_beta, ALU.add))
                norm_stats(ch, z0, st0, mv0, nr0, b_variance)
                yield 13
                norm_apply(z0, x1, mv0, nr0, b_newton, 24 * g + 24, [ch.add, lambda i: i.then_inc(x1_ready, 1)])
                ch.end()

            def dots(g, first=False):
                ch = ch_c
                ch.start(g)
                for u, dst, bias, hi in ((1, (kt[:, 0], kt[:, 1]), bkc, k_hi), (2, (qt[0][:, :, :], qt[1][:, :, :]), bqc, q_hi)):
                    dve.wait_ge(hi, g + 1)
                    for c in range(C):
                        last = ve.scalar_tensor_tensor(dst[1][:, c, :], RC.bank(u)[:, c * G:(c + 1) * G], bias[:, c:c + 1],
                                                       dst[0][:, c, :].bitcast(F32), ALU.add, ALU.subtract)
                    RC.release(last, u)
                dve.wait_ge(v_hi, g + 1)
                RC.release(ve.tensor_tensor(vv[1][:, :, :], RC.bank(3).rearrange("p (t n) -> p t n", t=T),
                                           vv[0][:, :, :].bitcast(F32), ALU.subtract), 3)
                yield 1
                if not first:
                    dve.wait_ge(x2b_ready, g)
                by_head = sc.rearrange("p (m h) n -> p m h n", h=HC)
                for h in range(HC):
                    u = 4 + h
                    RC.arrived(dve, g, u)
                    s4 = RC.bank(u).rearrange("p (m n) -> p m n", m=T * C)
                    for a, b in ((0, NODES), (NODES, P)):
                        last = ve.tensor_tensor(by_head[a:b, :, h, :], s4[a:b, :, a:b],
                                                bc(mask1[a:b, :].rearrange("p (a n) -> p a n", a=1), [NODES, T * C, NODES]),
                                                ALU.add)
                        if a == 0:
                            ch.add(last)
                    RC.release(last, u)
                    if h % 2:
                        yield 2 + h // 2
                for u in range(4, 8):
                    RC.evacuated(dve, g, u)
                soft_logits(ch, sc, smax[:, 0, :], None, s_ready)
                yield 4
                dve.wait_ge(s_exp, g + 1)
                inverse_sum(ch, sc, sden[:, 0, :], ok=True, last=s_sum_ready)
                yield 5
                dve.wait_ge(s_prob, g + 1)
                dve.wait_ge(s_ph, 2 * g + 2)
                for a, b in ((0, NODES), (NODES, P)):
                    ve.tensor_tensor(pb1[1][a:b, :, :, a:b].rearrange("p t h n -> p (t h) n"), sc[a:b],
                                     pb1[0][a:b, :, :, a:b].rearrange("p t h n -> p (t h) n"), ALU.subtract).then_inc(s_pl, 1)
                yield 6
                for n in range(T * C):
                    if n % C:
                        own_heads(dve, ve.tensor_copy, g, n)
                    yield 7 + n
                dve.wait_ge(o_hi, g + 1)
                for c in range(C):
                    last = ve.scalar_tensor_tensor(o1[1][:, c, :], ot1[:, c, :], bvc[:, c:c + 1],
                                                   o1[0][:, c, :].bitcast(F32), ALU.add, ALU.subtract)
                last.then_inc(o_lo, 1)
                dve.wait_ge(x1b_ready, g + 1)
                RC.arrived(dve, g, 16)
                RC.release(ve.tensor_tensor(y1, RC.bank(16).rearrange("p (t n) -> p t n", t=T), x1b, ALU.add), 16)
                RC.evacuated(dve, g, 16)
                norm_stats(ch, y1, st1, mv1, nr1, c_variance)
                yield 12
                norm_apply(y1, x2, mv1, nr1, c_newton, 12 * g + 12, [ch.add, lambda i: i.then_inc(x2_ready, 1)])
                ch.end()

            def last(g, first=False):
                ch = ch_d
                ch.start(g)
                dve.wait_ge(mj_hi, g + 1)
                RD.release(ve.tensor_tensor(mj[1], RD.bank(2).rearrange("p (t n) -> p t n", t=T),
                                           mj[0].bitcast(F32), ALU.subtract), 2)
                yield 2
                dve.wait_ge(x2b_ready, g + 1)
                RD.arrived(dve, g, 1)
                RD.release(ve.scalar_tensor_tensor(y2, RD.bank(1).rearrange("p (t n) -> p t n", t=T), deg[:, 0:1], x2b,
                                                   ALU.mult, ALU.add), 1)
                RD.evacuated(dve, g, 1)
                RD.arrived(dve, g, 3)
                RD.release(ve.tensor_tensor(y2, RD.bank(3).rearrange("p (t n) -> p t n", t=T), y2, ALU.add), 3)
                RD.evacuated(dve, g, 3)
                norm_stats(ch, y2, st2, mv2, nr2, d_variance)
                yield 4
                if not first:
                    dve.wait_ge(stored, 16 * g)
                norm_apply(y2, x3, mv2, nr2, d_newton, 24 * g + 12, [ch.add, lambda i: i.then_inc(x3_ready, 1)])
                yield 5
                RD.arrived(dve, g, 5)
                RD.release(ve.tensor_copy(h3, RD.bank(5)[:, 0:T * (D3 + 2)].rearrange("p (t n) -> p t n", t=T)), 5)
                RD.evacuated(dve, g, 5)
                ch.link(ve.tensor_copy(fsm3_hi[:, :], h3[:, :, D3 + 1]))
                ch.link(ve.tensor_tensor(fsm3_lo[:, :], h3[:, :, D3 + 1], fsm3_hi[:, :].bitcast(F32), ALU.subtract))
                for s, v in enumerate((fsm3_hi, fsm3_lo)):
                    ve.tensor_tensor(dg3[s].rearrange("p (a n) -> p a n", n=NODES), bc(col(v[:, :].bitcast(F32)), [P, T, NODES]),
                                     bc(eye2[:, :].rearrange("p (a n) -> p a n", a=1), [P, T, NODES]),
                                     ALU.mult).then_inc(diag3_ready, 1)
                dve.wait_ge(h3_hi, g + 1)
                ch.link(ve.tensor_tensor(h3r[1], h3[:, :, 0:D3], h3r[0].bitcast(F32), ALU.subtract))
                yield 6
                RD.arrived(dve, g, 6)
                RD.release(ve.tensor_tensor(lg3, RD.bank(6)[:, 0:T * NODES].rearrange("p (t n) -> p t n", t=T),
                                           bc(h3[:, :, D3:D3 + 1], [P, T, NODES]), ALU.add), 6)
                RD.evacuated(dve, g, 6)
                soft_logits(ch, lg3, m3[:, 0, :], 0.2, logits3_ready)
                yield 7
                dve.wait_ge(exp3_ready, g + 1)
                soft_probs(ch, lg3, lg3, d3[:, 0, :], prob3_ready)
                yield 8
                dve.wait_ge(prob3_ready, g + 1)
                dve.wait_ge(ph3_ready, 2 * g + 2)
                low(lg3, pb3[0], pb3[1], pl3_ready)
                yield 10
                ch.add(ve.tensor_tensor(x3[:, :, D3:D], h3[:, :, 0:D3], x3[:, :, D3:D], ALU.add))
                RD.arrived(dve, g, 8)
                RD.release(ve.tensor_tensor(x3[:, :, 0:D3], RD.bank(8)[:, 0:T * D3].rearrange("p (t n) -> p t n", t=T),
                                           x3[:, :, 0:D3], ALU.add), 8)
                RD.evacuated(dve, g, 8)
                norm_stats(ch, x3, st2, mv2, nr2, d_variance)
                yield 12
                norm_apply(x3, x3, mv2, nr2, d_newton, 24 * g + 24, [ch.add, lambda i: i.then_inc(res_ready, 1)])
                ch.end()

            pipeline(dve, ORDER['dve'], groups, idle, heads, rest, dots, last)

        @block.tensor
        def _(pe):
            te = nc.tensor

            def mm3(out, lhs, rhs, start, stop):
                te.matmul(out, lhs[0], rhs[0], start=start, stop=False)
                te.matmul(out, lhs[0], rhs[1], start=False, stop=False)
                return te.matmul(out, lhs[1], rhs[0], start=False, stop=stop)

            pe.wait_ge(set_dve, 16)
            pe.wait_ge(pool_set, 19)

            def heads(g, first=False):
                pe.wait_ge(x_split, 4 * g + 3)
                RA.acquire(pe, g, 0)
                for t in range(T):
                    o = RA.bank(0)[:, 16 * t:16 * t + 16]
                    cs = slice(t * P, t * P + P)
                    for c in range(C):
                        if c == C - 1:
                            for k in range(C):
                                te.matmul(o[:, 0:8], xt[1][:, k, cs], wa[:, k, 0, :], start=False, stop=False)
                        last = te.matmul(o, xt[0][:, c, cs], wa[:, c, :, :].rearrange("p s n -> p (s n)"),
                                         start=(c == 0), stop=(c == C - 1))
                RA.filled(last, 0)
                yield 1
                pe.wait_ge(diag_ready, 2 * g + 2)
                RA.acquire(pe, g, 1)
                te.matmul(RA.bank(1), same[:, :], dg[0], start=True, stop=False)
                te.matmul(RA.bank(1), same[:, :], dg[1], start=False, stop=False)
                RA.filled(te.matmul(RA.bank(1).rearrange("p (a n) -> p a n", n=NODES), ident[:, :],
                                   bc(mask0[:, :].rearrange("p (a n) -> p a n", a=1), [P, T * H0, NODES]),
                                   start=False, stop=True), 1)
                yield 4
                pe.wait_ge(ph_ready, 2 * g + 2)
                pe.wait_ge(pl_ready, 2 * g + 2)
                for t in range(T):
                    RA.acquire(pe, g, 2 + t)
                    o = RA.bank(2 + t).bitcast(F16)
                    for s in range(2):
                        for h in range(H0):
                            k = (s * H0 + h) * P
                            last = te.transpose(o[:, k:k + P], pb[s][:, t * H0 + h, :], ident16[:, :])
                    RA.filled(last, 2 + t)
                yield 5
                pe.wait_ge(x_split, 4 * g + 4)
                for t in range(T):
                    RA.evacuated(pe, g, 2 + t)
                    for c in range(C):
                        u = 4 + C * t + c
                        RA.acquire(pe, g, u)
                        RA.filled(mm3(RA.bank(u), [xn[s][:, t, c * P:c * P + P] for s in range(2)],
                                     [pt0[:, s, t, :] for s in range(2)], True, True), u)
                    yield 6 + t
                for u in range(4, 8):
                    RA.evacuated(pe, g, u)
                for h in range(H0):
                    u = 8 + h
                    RA.acquire(pe, g, u)
                    for oc in range(C):
                        for c in range(C):
                            last = mm3(RA.bank(u)[:, oc * G:oc * G + G],
                                       [wh[s][:, h, c, oc * P:oc * P + P] for s in range(2)],
                                       [zt[s][:, c, h, :] for s in range(2)], c == 0, c == C - 1)
                    RA.filled(last, u)
                    yield 8 + h
            def rest(g, first=False):
                for t in range(T):
                    u = t
                    RB.acquire(pe, g, u)
                    for k in range(H0 * C):
                        if t == 0 and k % C == 0:
                            pe.wait_ge(ht_lo, 4 * g + k // C + 1)
                        last = mm3(RB.bank(u)[:, 0:D + 2], [ht[s][:, k, t * P:t * P + P] for s in range(2)],
                                   [wo[s][:, k, :] for s in range(2)], k == 0, k == H0 * C - 1)
                    RB.filled(last, u)
                    yield 1 + t
                pe.wait_ge(diag2_ready, 2 * g + 2)
                RB.acquire(pe, g, 2)
                o = RB.bank(2)[:, 0:T * NODES]
                te.matmul(o, same[:, :], dg2[0], start=True, stop=False)
                te.matmul(o, same[:, :], dg2[1], start=False, stop=False)
                RB.filled(te.matmul(o.rearrange("p (a n) -> p a n", n=NODES), ident[:, :],
                                   bc(mask0[:, :].rearrange("p (a n) -> p a n", a=1), [P, T, NODES]),
                                   start=False, stop=True), 2)
                yield 5
                pe.wait_ge(ph2_ready, 2 * g + 2)
                pe.wait_ge(pl2_ready, 2 * g + 2)
                RB.acquire(pe, g, 3)
                o = RB.bank(3).bitcast(F16)
                for s in range(2):
                    for t in range(T):
                        k = (s * T + t) * P
                        last = te.transpose(o[:, k:k + P], pb2[s][:, t, :], ident16[:, :])
                RB.filled(last, 3)
                yield 6
                RB.evacuated(pe, g, 3)
                RB.evacuated(pe, g, 1)
                RB.acquire(pe, g, 4)
                for c in range(C):
                    for t in range(T):
                        k = c * G + t * P
                        last = mm3(RB.bank(4)[:, k:k + P], [wh2[s][:, t, c * P:c * P + P] for s in range(2)],
                                   [pt2[s][:, t, :] for s in range(2)], True, True)
                RB.filled(last, 4)
                yield 8
                pe.wait_ge(att_lo, g + 1)
                RB.acquire(pe, g, 5)
                for oc in range(C):
                    for c in range(C):
                        last = mm3(RB.bank(5)[:, oc * G:oc * G + G], [wf[s][:, 0, c, oc * P:oc * P + P] for s in range(2)],
                                   [ott[s][:, c, :] for s in range(2)], c == 0, c == C - 1)
                RB.filled(last, 5)
                yield 9
                pe.wait_ge(hid_lo, g + 1)
                RB.acquire(pe, g, 6)
                for t in range(T):
                    o = RB.bank(6)[:, t * D:t * D + D]
                    cs = slice(t * P, t * P + P)
                    for c in range(C):
                        if c == C - 1:
                            for k in range(C):
                                for s in range(2):
                                    te.matmul(o[:, k * P:k * P + P], ott[s][:, k, cs], ident[:, :], start=False, stop=False)
                        last = mm3(o, [hdt[s][:, c, cs] for s in range(2)], [wf[s][:, 1, c, :] for s in range(2)],
                                   c == 0, c == C - 1)
                RB.filled(last, 6)

            def cols(ring, g, u, src, hi, lo):
                pe.wait_ge(hi, g + 1)
                pe.wait_ge(lo, g + 1)
                ring.acquire(pe, g, u)
                o = ring.bank(u).bitcast(F16)
                for s in range(2):
                    for c in range(C):
                        for t in range(T):
                            k = (s * C + c) * G + t * P
                            last = te.transpose(o[:, k:k + P], src[:, s, t, c * P:c * P + P], ident16[:, :])
                ring.filled(last, u)
                ring.evacuated(pe, g, u)

            def rows(ring, g, u, x, w, n):
                ring.acquire(pe, g, u)
                for t in range(T):
                    for c in range(C):
                        last = mm3(ring.bank(u)[:, t * n:t * n + n], [x[:, s, c, t * P:t * P + P] for s in range(2)],
                                   [w[s][:, c, :] for s in range(2)], c == 0, c == C - 1)
                ring.filled(last, u)

            def dots(g, first=False):
                cols(RC, g, 0, x16a, x1_16hi, x1_16lo)
                for u, m in ((1, 1), (2, 0)):
                    RC.acquire(pe, g, u)
                    for oc in range(C):
                        for c in range(C):
                            last = mm3(RC.bank(u)[:, oc * G:oc * G + G], [wp[s][:, m, c, oc * P:oc * P + P] for s in range(2)],
                                       [xt1[:, s, c, :] for s in range(2)], c == 0, c == C - 1)
                    RC.filled(last, u)
                rows(RC, g, 3, xt1, [wp[s][:, 2] for s in range(2)], D)
                yield 1
                RC.evacuated(pe, g, 2)
                RC.evacuated(pe, g, 1)
                for h in range(HC):
                    u = 4 + h
                    part = slice(32 * h, 32 * h + 32)
                    RC.acquire(pe, g, u)
                    for m in range(T * C):
                        t, c = m // C, m % C
                        last = mm3(RC.bank(u)[:, m * P:m * P + P], [qt[s][part, c, t * P:t * P + P] for s in range(2)],
                                   [kt[part, s, c, t * P:t * P + P] for s in range(2)], True, True)
                    RC.filled(last, u)
                    if h % 2:
                        yield 2 + h // 2
                yield 6
                pe.wait_ge(s_ph, 2 * g + 2)
                pe.wait_ge(s_pl, 2 * g + 2)

                def turn(n):
                    t, c = n // C, n % C
                    u = 8 + 2 * n
                    RC.acquire(pe, g, u)
                    o = RC.bank(u).bitcast(F16)
                    for s in range(2):
                        for h in range(HC):
                            k = (s * HC + h) * P
                            last = te.transpose(o[:, k:k + P], pb1[s][:, t, c * HC + h, :], ident16[:, :])
                    RC.filled(last, u)

                def values(n):
                    t, c = n // C, n % C
                    u = 9 + 2 * n
                    RC.acquire(pe, g, u)
                    RC.evacuated(pe, g, u - 1)
                    RC.filled(mm3(RC.bank(u), [vv[s][:, t, c * P:c * P + P] for s in range(2)],
                                 [pt1[n % 2][:, s, :] for s in range(2)], True, True), u)

                turn(0)
                for n in range(T * C):
                    if n + 1 < T * C:
                        turn(n + 1)
                    values(n)
                    yield 7 + n
                pe.wait_ge(o_lo, g + 1)
                RC.acquire(pe, g, 16)
                for t in range(T):
                    for c in range(C):
                        last = mm3(RC.bank(16)[:, t * D:t * D + D], [o1[s][:, c, t * P:t * P + P] for s in range(2)],
                                   [wp[s][:, 3, c, :] for s in range(2)], c == 0, c == C - 1)
                RC.filled(last, 16)
            def last(g, first=False):
                cols(RD, g, 0, x16b, x2_16hi, x2_16lo)
                rows(RD, g, 1, xt2, [wm[s][:, 0] for s in range(2)], D)
                rows(RD, g, 2, xt2, [wm[s][:, 1] for s in range(2)], D)
                yield 2
                RD.evacuated(pe, g, 2)
                RD.acquire(pe, g, 3)
                for s in range(2):
                    last = te.matmul(RD.bank(3), adj_t[:, :], mj[s].rearrange("p t n -> p (t n)"), start=(s == 0), stop=(s == 1))
                RD.filled(last, 3)
                yield 5
                cols(RD, g, 4, x16c, x3_16hi, x3_16lo)
                rows(RD, g, 5, xt2, [w3[s][:, :, :] for s in range(2)], D3 + 2)
                yield 6
                pe.wait_ge(diag3_ready, 2 * g + 2)
                RD.acquire(pe, g, 6)
                o = RD.bank(6)[:, 0:T * NODES]
                te.matmul(o, same[:, :], dg3[0], start=True, stop=False)
                te.matmul(o, same[:, :], dg3[1], start=False, stop=False)
                RD.filled(te.matmul(o.rearrange("p (a n) -> p a n", n=NODES), ident[:, :],
                                   bc(mask0[:, :].rearrange("p (a n) -> p a n", a=1), [P, T, NODES]),
                                   start=False, stop=True), 6)
                yield 9
                pe.wait_ge(ph3_ready, 2 * g + 2)
                pe.wait_ge(pl3_ready, 2 * g + 2)
                RD.acquire(pe, g, 7)
                o = RD.bank(7).bitcast(F16)
                for s in range(2):
                    for t in range(T):
                        k = (s * T + t) * P
                        last = te.transpose(o[:, k:k + P], pb3[s][:, t, :], ident16[:, :])
                RD.filled(last, 7)
                yield 10
                RD.evacuated(pe, g, 7)
                RD.acquire(pe, g, 8)
                for t in range(T):
                    last = mm3(RD.bank(8)[:, t * D3:t * D3 + D3], [pt3[s][:, t, :] for s in range(2)],
                               [h3r[s][:, t, :] for s in range(2)], True, True)
                RD.filled(last, 8)

            pipeline(pe, ORDER['pe'], groups, idle, heads, rest, dots, last)


def kernel(x, adj, L0_gnn_W_heads, L0_gnn_a_heads, L0_gnn_W_out, L0_gnn_a_out, L0_gnn_w1, L0_gnn_b1, L0_gnn_w2,
           L0_gnn_b2, L0_gnn_ln_gamma, L0_gnn_ln_beta, L1_gnn_Wq, L1_gnn_bq, L1_gnn_Wk, L1_gnn_bk, L1_gnn_Wv,
           L1_gnn_bv, L1_gnn_Wo, L1_gnn_bo, L2_gnn_W, L2_gnn_b, L3_gnn_W, L3_gnn_a):
    import numpy as _np
    import concourse.bacc as _bacc
    from concourse import mybir as _mybir
    from concourse.bass_utils import run_bass_kernel_spmd as _run

    def lay(a):
        return _np.ascontiguousarray(a)

    def cols(b):
        return lay(_np.reshape(b, (2, 128)).T)

    x = _np.asarray(x)
    rows = x.reshape(-1, x.shape[-1])
    arrays = {
        "x": lay(rows), "xT": lay(rows.T), "adj": lay(adj), "adjT": lay(_np.transpose(adj)),
        "w_heads": lay(L0_gnn_W_heads), "a_heads": lay(L0_gnn_a_heads), "w_out": lay(L0_gnn_W_out), "a_out": lay(L0_gnn_a_out),
        "w1": lay(L0_gnn_w1), "b1": cols(L0_gnn_b1), "w2": lay(L0_gnn_w2), "b2": lay(L0_gnn_b2),
        "gamma": lay(L0_gnn_ln_gamma), "beta": lay(L0_gnn_ln_beta),
        "wqT": lay(_np.transpose(L1_gnn_Wq)), "bq": cols(L1_gnn_bq), "wkT": lay(_np.transpose(L1_gnn_Wk)), "bk": cols(L1_gnn_bk),
        "wvT": lay(_np.transpose(L1_gnn_Wv)), "bv": cols(L1_gnn_bv), "woT": lay(_np.transpose(L1_gnn_Wo)), "bo": lay(L1_gnn_bo),
        "wmT": lay(_np.transpose(L2_gnn_W)), "bm": lay(L2_gnn_b), "w3": lay(L3_gnn_W), "a3": lay(_np.reshape(L3_gnn_a, (2, 128))),
    }
    nc = _bacc.Bacc("TRN2", target_bir_lowering=False, num_devices=1)
    io = {n: nc.dram_tensor(n + "_dram", a.shape, _mybir.dt.from_np(a.dtype), kind="ExternalInput").ap()
          for n, a in arrays.items()}
    io["out"] = nc.dram_tensor("out_dram", rows.shape, _mybir.dt.float32, kind="ExternalOutput").ap()
    build_program(nc, io)
    r = _run(nc, [{n + "_dram": a for n, a in arrays.items()}], core_ids=[0])
    return r.results[0]["out_dram"].reshape(x.shape)
```

```python
from contextlib import ExitStack

import concourse.bass as bass
from concourse import mybir

F32 = mybir.dt.float32
F32R = mybir.dt.float32r
F16 = mybir.dt.float16
I32 = mybir.dt.int32
ALU = mybir.AluOpType
ACT = mybir.ActivationFunctionType
AX_X = mybir.AxisListType.X

P = 128
NODES = 64
D = 256
C = D // P
T = 2
G = T * P
H0 = 4
H1 = 8
HC = 4
DH = D // H1
D3 = 128
WORK = 9088
BIG = -(2.0 ** 100)
EPS = 1e-5
MAGIC = float(0x5F3759DF)


ORDER = {
    "pe": "BBABCBCCBDCACDDBCBCDCBBAACBDADCCACDCACACAAACDAAADC",
    "act": "CBBCCBDCBBBDBABABCABAAADACCDAAACCDCACCCADCCAADACDCAAAABAC",
    "dve": "BAAAABBBBBCBBBCBBBBCBAAACDDCBBDACCACDCDDDADDDCDDDCDDCDDDAABCBBABBBBABDBBBBDBBBDBDDDDDDAADBDBDBABBDAABABBBCBDADBAACBCBCBCCCBCCCCCCDCCCDCDDDDDDDDDDDD",
    "pool": "ACABBAABCDCXBBXAXDAAABCACXD",
}


def take(order, **stages):
    for k in order:
        if k in stages:
            next(stages[k], None)
    assert all(next(stage, "end") == "end" for stage in stages.values())


def idle(g, first=False):
    yield from ()


def pipeline(eng, order, groups, x, a, b, c, d):
    take(order, X=x(0, True))
    take(order, X=x(1), A=a(0, True))
    take(order, X=x(2), A=a(1), B=b(0, True))
    take(order, X=x(3), A=a(2), B=b(1), C=c(0, True))
    with eng.Fori(4, groups) as g:
        take(order, X=x(g), A=a(g - 1), B=b(g - 2), C=c(g - 3), D=d(g - 4))
    take(order, A=a(groups - 1), B=b(groups - 2), C=c(groups - 3), D=d(groups - 4))
    take(order, B=b(groups - 1), C=c(groups - 2), D=d(groups - 3))
    take(order, C=c(groups - 1), D=d(groups - 2))
    take(order, D=d(groups - 1))


class Banks:

    def __init__(self, tensor, full, free, uses):
        self.tensor, self.full, self.free, self.uses = tensor, full, free, uses
        self.n = len(full)

    def per_group(self, b):
        return (self.uses - b + self.n - 1) // self.n

    def bank(self, u):
        return self.tensor[:, u % self.n, :]

    def before(self, g, u):
        return g * self.per_group(u % self.n) + u // self.n + 1

    def acquire(self, pe, g, u):
        pe.wait_ge(self.free[u % self.n], self.before(g, u))

    def arrived(self, eng, g, u):
        eng.wait_ge(self.full[u % self.n], self.before(g, u))

    def evacuated(self, eng, g, u):
        eng.wait_ge(self.free[u % self.n], self.before(g, u) + 1)

    def filled(self, ins, u):
        ins.then_inc(self.full[u % self.n], 1)

    def release(self, ins, u):
        ins.then_inc(self.free[u % self.n], 1)


class Chain:

    def __init__(self, eng, sem, per_group):
        self.eng, self.sem, self.per_group = eng, sem, per_group

    def start(self, g):
        self.base, self.n = g * self.per_group, 0

    def add(self, ins):
        self.n += 1
        ins.then_inc(self.sem, 1)

    def wait(self):
        self.eng.wait_ge(self.sem, self.base + self.n)

    def link(self, ins):
        self.add(ins)
        self.wait()

    def end(self):
        assert self.n == self.per_group, (self.n, self.per_group)


def build_program(nc, io):
    groups = io["x"].shape[0] // G
    with ExitStack() as ctx:
        def sb(name, shape, dt):
            return ctx.enter_context(nc.sbuf_tensor(name, shape, dt))

        def sem(name):
            return ctx.enter_context(nc.semaphore(name))

        def pair(name, shape):
            return sb(name + "_hi", shape, F32R), sb(name + "_lo", shape, F32R)

        wh = pair("w_heads", [P, H0, C, D])
        wo = pair("w_out", [P, H0 * C, D + 2])
        wf = pair("w_ffn", [P, 2, C, D])
        wp = pair("w_proj", [P, 4, C, D])
        wm = pair("w_msg", [P, 2, C, D])
        w3 = pair("w_last", [P, C, D3 + 2])
        wa = sb("w_att", [P, C, 2, 2 * H0], F32R)

        ident = sb("ident", [P, P], F32R)
        ident16 = sb("ident16", [P, P], F16)
        eye2 = sb("eye2", [P, NODES], F32)
        same = sb("same_graph", [P, P], F32R)
        mask0 = sb("mask0", [P, NODES], F32R)
        mask1 = sb("mask1", [P, NODES], F32)
        adj_t = sb("adj_t", [P, P], F32R)
        deg = sb("deg", [P, 1], F32)
        row_ok = sb("row_ok", [P, 1], F32)
        b2_bc = sb("b2_bc", [P, D], F32)
        gamma_bc = sb("gamma_bc", [P, D], F32)
        beta_bc = sb("beta_bc", [P, D], F32)
        bo_bc = sb("bo_bc", [P, D], F32)
        degb_bc = sb("degb_bc", [P, D], F32)
        b1c = sb("b1c", [P, C], F32)
        bqc = sb("bqc", [P, C], F32)
        bkc = sb("bkc", [P, C], F32)
        bvc = sb("bvc", [P, C], F32)

        work = sb("work", [P, WORK], F32)
        at = [0]

        def w32(*shape):
            n = 1
            for s in shape:
                n *= s
            v = work[:, at[0]:at[0] + n]
            at[0] += n
            if len(shape) == 2:
                v = v.rearrange("p (a b) -> p a b", a=shape[0])
            if len(shape) == 3:
                v = v.rearrange("p (a b c) -> p a b c", a=shape[0], b=shape[1])
            return v

        x_in = w32(T, D)
        xt_in = w32(C, G)
        f_raw = w32(T, 16)
        f_sum = w32(T, 8)
        rmax = w32(1, T * H0)
        rden = w32(1, T * H0)
        ex = [w32(C, G) for _ in range(2)]
        hf = [w32(C, G) for _ in range(2)]
        lg = ex[0].rearrange("p c n -> p (c n)").rearrange("p (a n) -> p a n", n=NODES)
        x_beta = w32(T, D)
        g2 = w32(T, 2)
        rmax2 = w32(1, T)
        rden2 = w32(1, T)
        ea = w32(C, G)
        eb = w32(C, G)
        lg2 = ea.rearrange("p c n -> p (c n)")[:, 0:T * NODES].rearrange("p (t n) -> p t n", t=T)
        hid = z0 = ea
        y0 = x1 = eb
        st0 = w32(T, 6)
        mv0 = w32(1, T)
        nr0 = w32(4, T)
        x1b = w32(T, D)
        sc = w32(T * H1, NODES)
        smax = w32(1, T * H1)
        sden = w32(1, T * H1)
        flat_sc = sc.rearrange("p a n -> p (a n)")
        y1 = ot1 = flat_sc[:, 0:T * D].rearrange("p (t n) -> p t n", t=T)
        x2 = flat_sc[:, T * D:2 * T * D].rearrange("p (t n) -> p t n", t=T)
        st1 = w32(T, 6)
        mv1 = w32(1, T)
        nr1 = w32(4, T)
        x2b = w32(T, D)
        x3 = w32(T, D)
        y2 = w32(T, D)
        flat_y2 = y2.rearrange("p t n -> p (t n)")
        h3 = flat_y2[:, 0:T * (D3 + 2)].rearrange("p (t n) -> p t n", t=T)
        lg3 = flat_y2[:, 288:288 + T * NODES].rearrange("p (t n) -> p t n", t=T)
        m3 = w32(1, T)
        d3 = w32(1, T)
        st2 = w32(T, 6)
        mv2 = w32(1, T)
        nr2 = w32(4, T)
        assert at[0] <= WORK, at

        raw_wh = work[:, 0:2048].rearrange("p (h c n) -> p h c n", h=H0, c=C)
        raw_wo = work[:, 2048:4096].rearrange("p (k n) -> p k n", k=H0 * C)
        raw_wp = work[:, 0:2048].rearrange("p (k c n) -> p k c n", k=4, c=C)
        raw_wf = work[:, 2048:3072].rearrange("p (k c n) -> p k c n", k=2, c=C)
        raw_wm = work[:, 3072:4096].rearrange("p (k c n) -> p k c n", k=2, c=C)
        raw_w3 = work[:, 4096:4352].rearrange("p (c n) -> p c n", c=C)
        raw_a = work[:, 4352:6400].rearrange("p (h k n) -> p h k n", h=H0, k=2)
        raw_ao = work[:, 6400:6912].rearrange("p (k n) -> p k n", k=2)
        raw_a3 = work[:, 6912:7168].rearrange("p (k n) -> p k n", k=2)
        junk = work[:, 7168:7424]
        wide = work[:, 7500:7500 + P]
        att_f = work[:, 7424:7440].rearrange("p (c n) -> p c n", c=C)
        out_f = work[:, 7440:7456].rearrange("p (k n) -> p k n", k=H0 * C)
        last_f = work[:, 7456:7460].rearrange("p (c n) -> p c n", c=C)
        adj_i = work[:, 7640:7704].bitcast(I32)
        adjt_i = work[:, 7704:7768].bitcast(I32)
        adj_f = work[:, 7768:7832]
        tmpc = work[:, 7840:7844]

        def rpair(name, shape):
            return sb(name + "_hi", shape, F32R), sb(name + "_lo", shape, F32R)

        xn = rpair("x_rows", [P, T, D])
        xt = rpair("x_cols", [P, C, G])
        dg = [xt[s][:, :, :].rearrange("p c n -> p (c n)") for s in range(2)]
        share = sb("share", [P, 2, C * H0 * G], F32R)
        zt = [share[:, s, :].rearrange("p (c h n) -> p c h n", c=C, h=H0) for s in range(2)]
        share2 = sb("share2", [P, 2, 1028], F32R)
        wh2 = [share2[:, s, 0:516].rearrange("p (t n) -> p t n", t=T) for s in range(2)]
        hdt = [share2[:, s, 0:512].rearrange("p (c n) -> p c n", c=C) for s in range(2)]
        dg2 = [share2[:, s, 516:644] for s in range(2)]
        pt2 = [share2[:, s, 644:900].rearrange("p (t n) -> p t n", t=T) for s in range(2)]
        ott = [share2[:, s, 516:1028].rearrange("p (c n) -> p c n", c=C) for s in range(2)]
        ht = rpair("heads", [P, H0 * C, G])
        pt0 = ht[0][:, :, :].rearrange("p k n -> p (k n)").rearrange("p (s t n) -> p s t n", s=2, t=T)
        one = sb("one", [P, 1], F32)
        three_halves = sb("three_halves", [P, 1], F32)
        fsm_hi = sb("fsm_hi", [P, T, H0], F32R)
        fsm_lo = sb("fsm_lo", [P, T, H0], F32R)
        fsm2_hi = sb("fsm2_hi", [P, T], F32R)
        fsm2_lo = sb("fsm2_lo", [P, T], F32R)
        fsm3_hi = sb("fsm3_hi", [P, T], F32R)
        fsm3_lo = sb("fsm3_lo", [P, T], F32R)
        pb = [sb(f"pb{s}", [P, T * H0, P], F16) for s in range(2)]
        pb2 = [sb(f"pb2{s}", [P, T, P], F16) for s in range(2)]
        pb1 = [sb(f"pb1{s}", [P, T, H1, P], F16) for s in range(2)]
        pb3 = [sb(f"pb3{s}", [P, T, P], F16) for s in range(2)]
        x16a = sb("x16a", [P, 2, T, D], F16)
        x16b = sb("x16b", [P, 2, T, D], F16)
        x16c = sb("x16c", [P, 2, T, D], F16)

        xt1 = sb("xt1", [P, 2, C, G], F32R)
        qt = rpair("qt", [P, C, G])
        kt = sb("kt", [P, 2, C, G], F32R)
        vv = rpair("v", [P, T, D])
        pt1_odd = sb("pt1", [P, 2, HC * P], F32R)
        pt1 = [kt[:, :, :, :].rearrange("p s c n -> p s (c n)"), pt1_odd[:, :, :]]
        o1 = qt

        xt2 = sb("xt2", [P, 2, C, G], F32R)
        share3 = sb("share3", [P, 2, 640], F32R)
        mj = [share3[:, s, 0:512].rearrange("p (t n) -> p t n", t=T) for s in range(2)]
        h3r = [share3[:, s, 0:256].rearrange("p (t n) -> p t n", t=T) for s in range(2)]
        dg3 = [share3[:, s, 256:384] for s in range(2)]
        pt3 = [share3[:, s, 384:640].rearrange("p (t n) -> p t n", t=T) for s in range(2)]

        psum = ctx.enter_context(nc.psum_tensor("psum", [P, 8, 512], F32))

        def ring(name, i, uses):
            return Banks(psum[:, i:i + 2, :], [sem(f"{name}_full{k}") for k in range(2)],
                         [sem(f"{name}_free{k}") for k in range(2)], uses)

        RA, RB, RC, RD = ring("a", 0, 12), ring("b", 2, 7), ring("c", 4, 17), ring("d", 6, 9)

        raw_loaded = sem("raw_loaded")
        const_loaded = sem("const_loaded")
        pool_set = sem("pool_set")
        set_act = sem("set_act")
        set_dve = sem("set_dve")
        set_chain = sem("set_chain")
        x_loaded = sem("x_loaded")
        x_split = sem("x_split")
        a_chain = sem("a_chain")
        b_chain = sem("b_chain")
        c_chain = sem("c_chain")
        d_chain = sem("d_chain")
        residual_loaded = sem("residual_loaded")
        residual_ready = sem("residual_ready")
        h3_ready = sem("h3_ready")
        z_ready = sem("z_ready")
        z_scaled = sem("z_scaled")
        half_ready = sem("half_ready")
        ex2_ready = sem("ex2_ready")
        att_hi = sem("att_hi")
        att_lo = sem("att_lo")
        scores_ready = sem("scores_ready")
        row_max_ready = sem("row_max_ready")
        row_sum_ready = sem("row_sum_ready")
        s_sum_ready = sem("s_sum_ready")
        diag_ready = sem("diag_ready")
        logits_ready = sem("logits_ready")
        exp_ready = sem("exp_ready")
        prob_ready = sem("prob_ready")
        ph_ready = sem("ph_ready")
        pl_ready = sem("pl_ready")
        zt_hi = sem("zt_hi")
        ex_ready = sem("ex_ready")
        ht_hi = sem("ht_hi")
        ht_lo = sem("ht_lo")
        wh2_hi = sem("wh2_hi")
        diag2_ready = sem("diag2_ready")
        logits2_ready = sem("logits2_ready")
        exp2_ready = sem("exp2_ready")
        prob2_ready = sem("prob2_ready")
        ph2_ready = sem("ph2_ready")
        pl2_ready = sem("pl2_ready")
        hid_hi = sem("hid_hi")
        hid_lo = sem("hid_lo")
        x1_ready = sem("x1_ready")
        x1_16hi = sem("x1_16hi")
        x1_16lo = sem("x1_16lo")
        x2_ready = sem("x2_ready")
        x3_ready = sem("x3_ready")
        x2_16hi = sem("x2_16hi")
        x2_16lo = sem("x2_16lo")
        x3_16hi = sem("x3_16hi")
        x3_16lo = sem("x3_16lo")
        x1b_ready = sem("x1b_ready")
        x2b_ready = sem("x2b_ready")
        q_hi = sem("q_hi")
        k_hi = sem("k_hi")
        v_hi = sem("v_hi")
        s_ready = sem("s_ready")
        s_exp = sem("s_exp")
        s_prob = sem("s_prob")
        s_ph = sem("s_ph")
        s_pl = sem("s_pl")
        o_hi = sem("o_hi")
        o_lo = sem("o_lo")
        mj_hi = sem("mj_hi")
        diag3_ready = sem("diag3_ready")
        logits3_ready = sem("logits3_ready")
        exp3_ready = sem("exp3_ready")
        prob3_ready = sem("prob3_ready")
        ph3_ready = sem("ph3_ready")
        pl3_ready = sem("pl3_ready")
        res_ready = sem("res_ready")
        stored = sem("stored")

        x_rows = io["x"].rearrange("(g t p) n -> g p t n", t=T, p=P)
        x_cols = io["xT"].rearrange("(c p) (g n) -> g p c n", c=C, n=G)
        out_rows = io["out"].rearrange("(g t p) n -> g p t n", t=T, p=P)

        def bc(v, shape):
            return v.broadcast_to(shape)

        def col(v):
            return v.rearrange("p (n a) -> p n a", a=1)

        def row(name):
            return io[name].rearrange("(a n) -> a n", a=1)

        def own_heads(eng, copy, g, n):
            t, c = n // C, n % C
            u = 9 + 2 * n
            RC.arrived(eng, g, u)
            for h in range(HC):
                last = copy(ot1[32 * h:32 * h + 32, c, t * P:t * P + P], RC.bank(u)[32 * h:32 * h + 32, h * P:h * P + P])
            RC.release(last, u)

        RAW0, RAW1 = 6, 7

        block = ctx.enter_context(nc.Block())

        @block.sync
        def _(sp):
            def first(*pairs):
                for dst, src in pairs:
                    sp.dma_start(dst, src).then_inc(raw_loaded, 16)

            first((raw_wh, io["w_heads"].rearrange("h (c p) n -> p h c n", p=P)),
                  (raw_wo, io["w_out"].rearrange("(k p) n -> p k n", p=P)),
                  (raw_w3, io["w3"].rearrange("(c p) n -> p c n", p=P)),
                  (raw_a, io["a_heads"].rearrange("(a h) (k n) -> a h k n", a=1, k=2).broadcast_to([P, H0, 2, D])),
                  (raw_ao, io["a_out"].rearrange("(a k n) -> a k n", a=1, k=2).broadcast_to([P, 2, D])),
                  (raw_a3, io["a3"].rearrange("(a k) n -> a k n", a=1).broadcast_to([P, 2, D3])))
            sp.wait_ge(set_act, 6)
            sp.wait_ge(set_dve, 6)
            first((raw_wp[:, 0], io["wqT"].rearrange("(c p) n -> p c n", p=P)),
                  (raw_wp[:, 1], io["wkT"].rearrange("(c p) n -> p c n", p=P)),
                  (raw_wp[:, 2], io["wvT"].rearrange("(c p) n -> p c n", p=P)),
                  (raw_wp[:, 3], io["woT"].rearrange("(c p) n -> p c n", p=P)),
                  (raw_wf[:, 0], io["w1"].rearrange("(c p) n -> p c n", p=P)),
                  (raw_wf[:, 1], io["w2"].rearrange("(c p) n -> p c n", p=P)),
                  (raw_wm, io["wmT"].rearrange("(k c p) n -> p k c n", k=2, p=P)))
            sp.wait_ge(set_act, 9)
            sp.wait_ge(set_dve, 9)

            def rows(g, first=False):
                if not first:
                    sp.wait_ge(x_split, 4 * g)
                sp.dma_start(x_in, x_rows[g]).then_inc(x_loaded, 16)
                sp.dma_start(xt_in, x_cols[g]).then_inc(x_loaded, 16)

            def residual(g, first=False):
                if not first:
                    sp.wait_ge(x1_ready, g)
                sp.dma_start(x_beta, x_rows[g]).then_inc(residual_loaded, 16)

            def store(g):
                sp.wait_ge(res_ready, g + 1)
                sp.dma_start(out_rows[g], x3).then_inc(stored, 16)

            rows(0, first=True)
            rows(1)
            residual(0, first=True)
            rows(2)
            for g in (1, 2):
                residual(g)
                rows(g + 2)
            with sp.Fori(3, groups - 2) as g:
                residual(g)
                store(g - 3)
                rows(g + 2)
            residual(groups - 2)
            store(groups - 5)
            residual(groups - 1)
            for g in range(groups - 4, groups):
                store(g)
            sp.wait_ge(stored, 16 * groups)

        @block.gpsimd
        def _(pool):
            po = nc.gpsimd
            for dst, src in ((b2_bc[:, :], row("b2").broadcast_to([P, D])),
                             (gamma_bc[:, :], row("gamma").broadcast_to([P, D])),
                             (beta_bc[:, :], row("beta").broadcast_to([P, D])),
                             (bo_bc[:, :], row("bo").broadcast_to([P, D])),
                             (degb_bc[:, :], row("bm").broadcast_to([P, D])),
                             (adj_i[0:NODES, :], io["adj"]), (adj_i[NODES:P, :], io["adj"]),
                             (adjt_i[0:NODES, :], io["adjT"]), (adjt_i[NODES:P, :], io["adjT"])):
                pool.dma_start(dst, src).then_inc(const_loaded, 16)
            for n, (dst, src) in enumerate(((b1c, "b1"), (bqc, "bq"), (bkc, "bk"), (bvc, "bv"))):
                pool.dma_start(dst[:, :], io[src]).then_inc(const_loaded, 16)
            po.memset(wide, 0.0).then_inc(pool_set, 1)
            po.memset(eye2[:, :], 0.0).then_inc(pool_set, 1)
            po.memset(same[:, :].bitcast(F32), 0.0).then_inc(pool_set, 1)
            po.memset(adj_t[:, :].bitcast(F32), 0.0).then_inc(pool_set, 1)
            for t in (*pb, *pb1, *pb2, *pb3):
                v = t[tuple([slice(None)] * len(t.shape))]
                po.memset(v.bitcast(F32) if t.dtype == F32R else v, 0.0).then_inc(pool_set, 1)
            pool.wait_ge(pool_set, 12)
            po.affine_select(out=wide, in_=wide, compare_op=ALU.not_equal, fill=1.0, base=0,
                             pattern=[[-1, P]], channel_multiplier=1).then_inc(pool_set, 1)
            po.affine_select(out=eye2[:, :], in_=eye2[:, :], compare_op=ALU.not_equal, fill=1.0, base=0,
                             pattern=[[-1, NODES]], channel_multiplier=1).then_inc(pool_set, 1)
            pool.wait_ge(pool_set, 14)
            po.affine_select(out=eye2[:, :], in_=eye2[:, :], compare_op=ALU.not_equal, fill=1.0, base=-NODES,
                             pattern=[[-1, NODES]], channel_multiplier=1).then_inc(pool_set, 1)
            po.memset(three_halves[:, :], 1.5).then_inc(pool_set, 1)
            po.memset(one[:, :], 1.0).then_inc(pool_set, 1)
            po.tensor_copy(ident[:, :], wide).then_inc(pool_set, 1)
            po.tensor_copy(ident16[:, :], wide).then_inc(pool_set, 1)
            pool.wait_ge(pool_set, 19)
            pool.wait_ge(const_loaded, 16 * 13)
            pool.wait_ge(set_dve, 16)

            def split(g, first=False):
                if not first:
                    for u in (6, 7):
                        RA.evacuated(pool, g - 1, u)
                pool.wait_ge(x_loaded, 32 * g + 32)
                po.tensor_tensor(xt[0][:, :, :], xt_in, bc(one[:, :].rearrange("p (a n) -> p a n", a=1), [P, C, G]), ALU.mult).then_inc(x_split, 1)
                yield
                po.tensor_scalar(xn[0][:, :, :], x_in, 1.0, None, ALU.mult).then_inc(x_split, 1)
                yield
                pool.wait_ge(x_split, 4 * g + 2)
                po.tensor_tensor(xt[1][:, :, :], xt_in, xt[0][:, :, :].bitcast(F32), ALU.subtract).then_inc(x_split, 1)
                yield
                po.tensor_tensor(xn[1][:, :, :], x_in, xn[0][:, :, :].bitcast(F32), ALU.subtract).then_inc(x_split, 1)

            def heads(g, first=False):
                pool.wait_ge(scores_ready, g + 1)
                for s, v in enumerate((fsm_hi, fsm_lo)):
                    po.tensor_tensor(dg[s].rearrange("p (a n) -> p a n", n=NODES),
                                     bc(col(v[:, :, :].bitcast(F32).rearrange("p t h -> p (t h)")), [P, T * H0, NODES]),
                                     bc(eye2[:, :].rearrange("p (a n) -> p a n", a=1), [P, T * H0, NODES]),
                                     ALU.mult).then_inc(diag_ready, 1)
                yield
                pool.wait_ge(row_max_ready, g + 1)
                po.tensor_tensor(lg, lg, bc(col(rmax[:, 0, :]), [P, T * H0, NODES]), ALU.subtract).then_inc(logits_ready, 1)
                yield
                pool.wait_ge(row_sum_ready, g + 1)
                po.tensor_tensor(lg, lg, bc(col(rden[:, 0, :]), [P, T * H0, NODES]), ALU.mult).then_inc(prob_ready, 1)
                yield
                pool.wait_ge(ph_ready, 2 * g + 1)
                po.tensor_tensor(pb[1][0:NODES, :, 0:NODES], lg[0:NODES], pb[0][0:NODES, :, 0:NODES],
                                 ALU.subtract).then_inc(pl_ready, 1)
                yield
                for h in range(H0):
                    pool.wait_ge(ht_hi, 4 * g + h + 1)
                    po.tensor_tensor(ht[1][:, C * h:C * h + C, :], hf[h % 2],
                                     ht[0][:, C * h:C * h + C, :].bitcast(F32), ALU.subtract).then_inc(ht_lo, 1)
                    yield

            def rest(g, first=False):
                pool.wait_ge(residual_loaded, 16 * g + 16)
                po.tensor_tensor(x_beta, x_beta, bc(beta_bc[:, :].rearrange("p (a n) -> p a n", a=1), [P, T, D]),
                                 ALU.add).then_inc(residual_ready, 1)
                yield
                pool.wait_ge(att_hi, g + 1)
                po.tensor_tensor(ott[1], eb, ott[0].bitcast(F32), ALU.subtract).then_inc(att_lo, 1)
                yield
                pool.wait_ge(hid_hi, g + 1)
                po.tensor_tensor(hdt[1], hid, hdt[0].bitcast(F32), ALU.subtract).then_inc(hid_lo, 1)
                yield
                pool.wait_ge(z_ready, g + 1)
                po.tensor_tensor(z0, z0, bc(gamma_bc[:, :].rearrange("p (a n) -> p a n", a=1), [P, T, D]),
                                 ALU.mult).then_inc(z_scaled, 1)
                yield
                pool.wait_ge(z_scaled, 2 * g + 1)
                pool.wait_ge(residual_ready, g + 1)
                po.tensor_tensor(z0, z0, x_beta, ALU.add).then_inc(z_scaled, 1)
                yield
                pool.wait_ge(x1_16hi, g + 1)
                po.tensor_tensor(x16a[:, 1], x1, x16a[:, 0], ALU.subtract).then_inc(x1_16lo, 1)

            def dots(g, first=False):
                pool.wait_ge(x1_ready, g + 1)
                po.tensor_tensor(x1b, x1, bc(bo_bc[:, :].rearrange("p (a n) -> p a n", a=1), [P, T, D]),
                                 ALU.add).then_inc(x1b_ready, 1)
                yield
                pool.wait_ge(s_sum_ready, g + 1)
                po.tensor_tensor(sc, sc, bc(col(sden[:, 0, :]), [P, T * H1, NODES]), ALU.mult).then_inc(s_prob, 1)
                yield
                pool.wait_ge(s_ph, 2 * g + 1)
                a, b = 0, NODES
                po.tensor_tensor(pb1[1][a:b, :, :, a:b].rearrange("p t h n -> p (t h) n"), sc[a:b],
                                 pb1[0][a:b, :, :, a:b].rearrange("p t h n -> p (t h) n"), ALU.subtract).then_inc(s_pl, 1)
                yield
                pool.wait_ge(x2_16hi, g + 1)
                po.tensor_tensor(x16b[:, 1], x2, x16b[:, 0], ALU.subtract).then_inc(x2_16lo, 1)
                yield
                if not first:
                    RD.evacuated(pool, g - 1, 1)
                po.tensor_tensor(x2b, x2, bc(degb_bc[:, :].rearrange("p (a n) -> p a n", a=1), [P, T, D]),
                                 ALU.add).then_inc(x2b_ready, 1)

            def last(g, first=False):
                pool.wait_ge(x3_16hi, g + 1)
                po.tensor_tensor(x16c[:, 1], x3, x16c[:, 0], ALU.subtract).then_inc(x3_16lo, 1)
                yield
                pool.wait_ge(h3_ready, g + 1)
                po.tensor_tensor(x3[:, :, D3:D], h3[:, :, 0:D3], x3[:, :, D3:D], ALU.add).then_inc(half_ready, 1)
                yield

            pipeline(pool, ORDER['pool'], groups, split, heads, rest, dots, last)

        @block.scalar
        def _(act):
            sc_ = nc.scalar
            act.wait_ge(raw_loaded, 16 * RAW0)
            sc_.activation(wh[0][:, :, :, :], raw_wh, ACT.Copy).then_inc(set_act, 1)
            sc_.activation(wo[0][:, :, 0:D], raw_wo, ACT.Copy).then_inc(set_act, 1)
            sc_.activation(w3[0][:, :, 0:D3], raw_w3, ACT.Copy).then_inc(set_act, 1)
            act.wait_ge(set_chain, 16 + 16 + 4)
            for src, dst in ((att_f, wa[:, :, 0, :]), (out_f, wo[0][:, :, D:D + 2]), (last_f, w3[0][:, :, D3:D3 + 2])):
                sc_.activation(dst, src, ACT.Copy).then_inc(set_act, 1)
            act.wait_ge(raw_loaded, 16 * (RAW0 + RAW1))
            for dst, src in ((wf[0], raw_wf), (wp[0], raw_wp), (wm[0], raw_wm)):
                sc_.activation(dst[:, :, :, :], src, ACT.Copy).then_inc(set_act, 1)

            act.wait_ge(const_loaded, 16 * 13)
            act.wait_ge(pool_set, 19)
            act.wait_ge(set_dve, 16)

            def softmax_parts(eng, g, logits, ready, exp_done, n=1, scale=1.0):
                eng.wait_ge(ready, n * g + n)
                sc_.activation(logits, logits, ACT.Exp, scale=scale).then_inc(exp_done, 1)

            def high(g, src, dst, ready, done):
                act.wait_ge(ready, g + 1)
                sc_.activation(dst[0:NODES, :, 0:NODES], src[0:NODES], ACT.Copy).then_inc(done, 1)
                sc_.activation(dst[NODES:P, :, NODES:P], src[NODES:P], ACT.Copy).then_inc(done, 1)

            def heads(g, first=False):
                softmax_parts(act, g, lg, logits_ready, exp_ready)
                yield
                high(g, lg, pb[0][:, :, :], prob_ready, ph_ready)
                yield
                if not first:
                    RB.arrived(act, g - 1, 0)
                    RB.arrived(act, g - 1, 1)
                for t in range(T):
                    RA.arrived(act, g, 2 + t)
                    RA.release(sc_.activation(pt0[:, :, t, :], RA.bank(2 + t).bitcast(F16).rearrange("p (s n) -> p s n", s=2),
                                              ACT.Copy), 2 + t)
                    yield
                yield
                for t in range(T):
                    for c in range(C):
                        u = 4 + C * t + c
                        RA.arrived(act, g, u)
                        sc_.activation(zt[0][:, c, :, t * P:t * P + P], RA.bank(u).rearrange("p (h n) -> p h n", h=H0),
                                       ACT.Copy).then_inc(zt_hi, 1)
                        yield
                    yield

                def elu_exp(n):
                    RA.arrived(act, g, 8 + n)
                    if n >= 2:
                        RA.evacuated(act, g, 8 + n - 2)
                    sc_.activation(ex[n % 2], RA.bank(8 + n).rearrange("p (c n) -> p c n", c=C), ACT.Exp).then_inc(ex_ready, 1)

                elu_exp(0)
                yield
                for h in range(H0):
                    if h + 1 < H0:
                        elu_exp(h + 1)
                        yield
                    RA.evacuated(act, g, 8 + h)
                    sc_.activation(ht[0][:, C * h:C * h + C, :], hf[h % 2], ACT.Copy).then_inc(ht_hi, 1)
                    yield

            def rest(g, first=False):
                for t in range(T):
                    RB.arrived(act, g, t)
                    sc_.activation(wh2[0][:, t, :], RB.bank(t)[:, 0:D + 2], ACT.Copy).then_inc(wh2_hi, 1)
                    yield
                yield
                softmax_parts(act, g, lg2, logits2_ready, exp2_ready)
                yield
                high(g, lg2, pb2[0], prob2_ready, ph2_ready)
                yield
                RB.arrived(act, g, 3)
                for s in range(2):
                    last = sc_.activation(pt2[s], RB.bank(3).bitcast(F16)[:, s * T * P:(s + 1) * T * P]
                                          .rearrange("p (t n) -> p t n", t=T), ACT.Copy)
                RB.release(last, 3)
                yield
                RB.arrived(act, g, 4)
                sc_.activation(ea, RB.bank(4).rearrange("p (c n) -> p c n", c=C), ACT.Exp).then_inc(ex2_ready, 1)
                yield
                RB.evacuated(act, g, 4)
                sc_.activation(ott[0], eb, ACT.Copy).then_inc(att_hi, 1)
                yield
                RB.arrived(act, g, 5)
                for c in range(C):
                    last = sc_.activation(hid[:, c, :], RB.bank(5)[:, c * G:(c + 1) * G], ACT.Relu, bias=b1c[:, c:c + 1])
                RB.release(last, 5)
                yield
                RB.evacuated(act, g, 5)
                sc_.activation(hdt[0], hid, ACT.Copy).then_inc(hid_hi, 1)
                yield
                if not first:
                    RC.arrived(act, g - 1, 0)
                act.wait_ge(x1_ready, g + 1)
                sc_.activation(x16a[:, 0], x1, ACT.Copy).then_inc(x1_16hi, 1)

            def cols(ring, g, u, dst):
                ring.arrived(act, g, u)
                ring.release(sc_.activation(dst[:, :, :, :].rearrange("p s c n -> p (s c n)"),
                                            ring.bank(u).bitcast(F16), ACT.Copy), u)

            def dots(g, first=False):
                cols(RC, g, 0, xt1)
                yield
                for u, dst, bias, done in ((1, kt[:, 0], bkc, k_hi), (2, qt[0][:, :, :], bqc, q_hi)):
                    RC.arrived(act, g, u)
                    for c in range(C):
                        last = sc_.activation(dst[:, c, :], RC.bank(u)[:, c * G:(c + 1) * G], ACT.Identity,
                                              bias=bias[:, c:c + 1])
                    last.then_inc(done, 1)
                    yield
                RC.arrived(act, g, 3)
                sc_.activation(vv[0][:, :, :], RC.bank(3).rearrange("p (t n) -> p t n", t=T), ACT.Copy).then_inc(v_hi, 1)
                yield
                softmax_parts(act, g, sc, s_ready, s_exp, scale=DH ** -0.5)
                yield
                act.wait_ge(s_prob, g + 1)
                for a, b in ((0, NODES), (NODES, P)):
                    sc_.activation(pb1[0][a:b, :, :, a:b].rearrange("p t h n -> p (t h) n"), sc[a:b], ACT.Copy).then_inc(s_ph, 1)
                    yield
                yield

                def turned(n):
                    RC.arrived(act, g, 8 + 2 * n)
                    if n >= 2:
                        RC.arrived(act, g, 9 + 2 * (n - 2))
                    RC.release(sc_.activation(pt1[n % 2], RC.bank(8 + 2 * n).bitcast(F16).rearrange("p (s n) -> p s n", s=2),
                                              ACT.Copy), 8 + 2 * n)

                turned(0)
                yield
                for n in range(T * C):
                    if n + 1 < T * C:
                        turned(n + 1)
                        yield
                    own_heads(act, sc_.copy, g, n)
                    yield
                RC.evacuated(act, g, 9 + 2 * (T * C - 1))
                for c in range(C):
                    last = sc_.activation(o1[0][:, c, :], ot1[:, c, :], ACT.Identity, bias=bvc[:, c:c + 1])
                last.then_inc(o_hi, 1)
                yield
                if not first:
                    RD.arrived(act, g - 1, 0)
                act.wait_ge(x2_ready, g + 1)
                sc_.activation(x16b[:, 0], x2, ACT.Copy).then_inc(x2_16hi, 1)

            def last(g, first=False):
                cols(RD, g, 0, xt2)
                yield
                RD.arrived(act, g, 2)
                sc_.activation(mj[0], RD.bank(2).rearrange("p (t n) -> p t n", t=T), ACT.Copy).then_inc(mj_hi, 1)
                yield
                act.wait_ge(x3_ready, g + 1)
                sc_.activation(x16c[:, 0], x3, ACT.Copy).then_inc(x3_16hi, 1)
                yield
                cols(RD, g, 4, xt2)
                yield
                RD.arrived(act, g, 5)
                rows5 = RD.bank(5)[:, 0:T * (D3 + 2)].rearrange("p (t n) -> p t n", t=T)
                sc_.activation(h3, rows5, ACT.Copy).then_inc(h3_ready, 1)
                RD.release(sc_.activation(h3r[0], rows5[:, :, 0:D3], ACT.Copy), 5)
                yield
                softmax_parts(act, g, lg3, logits3_ready, exp3_ready)
                yield
                high(g, lg3, pb3[0], prob3_ready, ph3_ready)
                yield
                RD.arrived(act, g, 7)
                for s in range(2):
                    last = sc_.activation(pt3[s], RD.bank(7).bitcast(F16)[:, s * T * P:(s + 1) * T * P]
                                          .rearrange("p (t n) -> p t n", t=T), ACT.Copy)
                RD.release(last, 7)

            pipeline(act, ORDER['act'], groups, idle, heads, rest, dots, last)

        @block.vector
        def _(dve):
            ve = nc.vector
            for bank in (*RA.free, *RB.free, *RC.free, *RD.free):
                dve.sem_inc(bank, 1)
            setup = Chain(dve, set_chain, 0)
            setup.start(0)
            dve.wait_ge(raw_loaded, 16 * RAW0)
            for c in range(C):
                for h in range(H0):
                    for k in range(2):
                        setup.link(ve.tensor_tensor_reduce(junk, raw_wh[:, h, c, :], raw_a[:, h, k, :], 1.0, 0.0,
                                                           ALU.mult, ALU.add, att_f[:, c, k * H0 + h:k * H0 + h + 1]))
            for q in range(H0 * C):
                for k in range(2):
                    setup.link(ve.tensor_tensor_reduce(junk, raw_wo[:, q, :], raw_ao[:, k, :], 1.0, 0.0,
                                                       ALU.mult, ALU.add, out_f[:, q, k:k + 1]))
            for c in range(C):
                for k in range(2):
                    setup.link(ve.tensor_tensor_reduce(junk[:, 0:D3], raw_w3[:, c, :], raw_a3[:, k, :], 1.0, 0.0,
                                                       ALU.mult, ALU.add, last_f[:, c, k:k + 1]))
            dve.wait_ge(set_act, 6)
            ve.tensor_tensor(wh[1][:, :, :, :], raw_wh, wh[0][:, :, :, :].bitcast(F32), ALU.subtract).then_inc(set_dve, 1)
            ve.tensor_tensor(wo[1][:, :, 0:D], raw_wo, wo[0][:, :, 0:D].bitcast(F32), ALU.subtract).then_inc(set_dve, 1)
            ve.tensor_tensor(w3[1][:, :, 0:D3], raw_w3, w3[0][:, :, 0:D3].bitcast(F32), ALU.subtract).then_inc(set_dve, 1)
            ve.tensor_tensor(wo[1][:, :, D:D + 2], out_f, wo[0][:, :, D:D + 2].bitcast(F32), ALU.subtract).then_inc(set_dve, 1)
            ve.tensor_tensor(w3[1][:, :, D3:D3 + 2], last_f, w3[0][:, :, D3:D3 + 2].bitcast(F32), ALU.subtract).then_inc(set_dve, 1)
            ve.tensor_tensor(wa[:, :, 1, :], att_f, wa[:, :, 0, :].bitcast(F32), ALU.subtract).then_inc(set_dve, 1)
            dve.wait_ge(set_act, 9)
            for w, src in ((wf, raw_wf), (wp, raw_wp), (wm, raw_wm)):
                ve.tensor_tensor(w[1][:, :, :, :], src, w[0][:, :, :, :].bitcast(F32), ALU.subtract).then_inc(set_dve, 1)
            dve.wait_ge(pool_set, 19)
            ve.memset(same[0:NODES, 0:NODES].bitcast(F32), 1.0).then_inc(set_dve, 1)
            ve.memset(same[NODES:P, NODES:P].bitcast(F32), 1.0).then_inc(set_dve, 1)
            dve.wait_ge(const_loaded, 16 * 13)
            setup.link(ve.tensor_copy(adj_f, adj_i))
            ve.tensor_scalar(mask0[:, :], adj_f, 0.0, BIG, ALU.is_le, ALU.mult).then_inc(set_dve, 1)
            ve.tensor_scalar(mask1[:, :], adj_f, 0.0, BIG, ALU.is_equal, ALU.mult).then_inc(set_dve, 1)
            ve.tensor_copy(adj_t[0:NODES, 0:NODES], adjt_i[0:NODES, :]).then_inc(set_dve, 1)
            ve.tensor_copy(adj_t[NODES:P, NODES:P], adjt_i[NODES:P, :]).then_inc(set_dve, 1)
            setup.link(ve.tensor_reduce(deg[:, :], adj_f, AX_X, ALU.add))
            setup.link(ve.tensor_scalar(adj_f, adj_f, 0.0, None, ALU.not_equal))
            setup.link(ve.tensor_reduce(tmpc[:, 0:1], adj_f, AX_X, ALU.add))
            setup.link(ve.reciprocal(tmpc[:, 1:2], tmpc[:, 0:1]))
            setup.link(ve.tensor_tensor(tmpc[:, 2:3], tmpc[:, 0:1], tmpc[:, 1:2], ALU.mult))
            setup.link(ve.tensor_scalar(row_ok[:, :], tmpc[:, 2:3], 0.0, 1.0, ALU.mult, ALU.add))
            ve.tensor_scalar(degb_bc[:, :], degb_bc[:, :], deg[:, 0:1], None, ALU.mult).then_inc(set_dve, 1)
            dve.wait_ge(set_dve, 16)

            ch_a = Chain(dve, a_chain, 9)
            ch_b = Chain(dve, b_chain, 51)
            ch_c = Chain(dve, c_chain, 28)
            ch_d = Chain(dve, d_chain, 49)

            def inverse_std(ch, src, st, mv, nr):
                for t in range(T):
                    ch.add(ve.bn_stats(st[:, t, :], src[:, t, :]))
                yield
                ch.wait()
                me, se, mo, so = (st[:, :, k] for k in (1, 2, 4, 5))
                v, q, d, y = (nr[:, k, :] for k in range(4))
                mean = mv[:, 0, :]
                qi, yi = q.bitcast(I32), y.bitcast(I32)
                ch.add(ve.tensor_tensor(d, me, mo, ALU.subtract))
                ch.add(ve.tensor_tensor(v, se, so, ALU.add))
                yield
                ch.wait()
                ch.add(ve.tensor_scalar(v, v, 1.0 / D, EPS, ALU.mult, ALU.add))
                ch.add(ve.tensor_tensor(d, d, d, ALU.mult))
                yield
                ch.wait()
                ch.add(ve.tensor_tensor(mean, me, mo, ALU.add))
                ch.add(ve.scalar_tensor_tensor(v, d, 0.25, v, ALU.mult, ALU.add))
                yield
                ch.wait()
                ch.add(ve.tensor_scalar(mean, mean, 0.5, None, ALU.mult))
                ch.add(ve.tensor_scalar(qi, v.bitcast(I32), 1, None, ALU.logical_shift_right))
                yield
                ch.wait()
                ch.add(ve.tensor_scalar(v, v, -0.5, None, ALU.mult))
                ch.add(ve.tensor_scalar(yi, qi, -1.0, MAGIC, ALU.mult, ALU.add))
                yield
                ch.wait()
                ch.add(ve.tensor_tensor(q, y, y, ALU.mult))
                yield
                ch.wait()
                ch.add(ve.tensor_tensor(q, q, v, ALU.mult))
                yield
                ch.wait()
                ch.add(ve.tensor_scalar(d, q, 1.5, 2.5, ALU.mult, ALU.add))
                yield
                ch.wait()
                ch.add(ve.tensor_tensor(d, d, q, ALU.mult))
                yield
                ch.wait()
                ch.add(ve.scalar_tensor_tensor(y, d, 1.875, y, ALU.add, ALU.mult))
                yield
                ch.wait()
                ch.add(ve.tensor_tensor(q, y, y, ALU.mult))
                yield
                ch.wait()
                ch.add(ve.tensor_tensor(q, q, v, ALU.mult))
                yield
                ch.wait()
                ch.add(ve.scalar_tensor_tensor(y, q, 1.5, y, ALU.add, ALU.mult))
                yield
                ch.wait()

            def norm_apply(src, dst, mv, nr, add):
                for t in range(T):
                    add[t](ve.tensor_scalar(dst[:, t, :], src[:, t, :], mv[:, 0, t:t + 1], nr[:, 3, t:t + 1],
                                            ALU.subtract, ALU.mult))

            def leaky_max(ch, e, mx, slope, last=None):
                if slope is not None:
                    ch.add(ve.scalar_tensor_tensor(e, e, slope, e, ALU.mult, ALU.max))
                    yield
                    ch.wait()
                ins = ve.tensor_reduce(mx, e, AX_X, ALU.max)
                if last is None:
                    ch.add(ins)
                    yield
                    ch.wait()
                else:
                    ins.then_inc(last, 1)

            def soft_logits(ch, e, mx, slope, done):
                yield from leaky_max(ch, e, mx, slope)
                ve.tensor_tensor(e, e, bc(col(mx), list(e.shape)), ALU.subtract).then_inc(done, 1)

            def inverse_sum(ch, e, dn, ok=False, last=None):
                ch.add(ve.tensor_reduce(dn, e, AX_X, ALU.add))
                yield
                ch.wait()
                if ok:
                    ch.add(ve.tensor_scalar(dn, dn, row_ok[:, 0:1], None, ALU.mult))
                    yield
                    ch.wait()
                ins = ve.reciprocal(dn, dn)
                if last is None:
                    ch.add(ins)
                    yield
                    ch.wait()
                else:
                    ins.then_inc(last, 1)

            def soft_probs(ch, e, pr_, dn, done):
                yield from inverse_sum(ch, e, dn)
                ve.tensor_tensor(pr_, e, bc(col(dn), list(e.shape)), ALU.mult).then_inc(done, 1)

            def low(pr_, hi, lo, done, parts=((0, NODES), (NODES, P))):
                for a, b in parts:
                    ve.tensor_tensor(lo[a:b, :, a:b], pr_[a:b], hi[a:b, :, a:b], ALU.subtract).then_inc(done, 1)

            def heads(g, first=False):
                ch = ch_a
                ch.start(g)
                RA.arrived(dve, g, 0)
                RA.release(ve.tensor_copy(f_raw, RA.bank(0)[:, 0:16 * T].rearrange("p (t n) -> p t n", t=T)), 0)
                yield
                RA.evacuated(dve, g, 0)
                ch.add(ve.tensor_tensor(f_sum, f_raw[:, :, 0:8], f_raw[:, :, 8:16], ALU.add))
                yield
                ch.wait()
                ch.add(ve.tensor_copy(fsm_hi[:, :, :], f_sum[:, :, H0:2 * H0]))
                yield
                ch.wait()
                ve.tensor_tensor(fsm_lo[:, :, :], f_sum[:, :, H0:2 * H0], fsm_hi[:, :, :].bitcast(F32),
                                 ALU.subtract).then_inc(scores_ready, 1)
                yield
                RA.arrived(dve, g, 1)
                for t in range(T):
                    last = ve.tensor_tensor(lg[:, t * H0:(t + 1) * H0, :],
                                            RA.bank(1)[:, t * H0 * NODES:(t + 1) * H0 * NODES].rearrange("p (h n) -> p h n", h=H0),
                                            bc(col(f_sum[:, t, 0:H0]), [P, H0, NODES]), ALU.add)
                    if t < T - 1:
                        ch.add(last)
                RA.release(last, 1)
                yield
                RA.evacuated(dve, g, 1)
                yield from leaky_max(ch, lg, rmax[:, 0, :], 0.01, row_max_ready)
                yield
                dve.wait_ge(exp_ready, g + 1)
                yield from inverse_sum(ch, lg, rden[:, 0, :], last=row_sum_ready)
                yield
                dve.wait_ge(prob_ready, g + 1)
                dve.wait_ge(ph_ready, 2 * g + 2)
                low(lg, pb[0][:, :, :], pb[1][:, :, :], pl_ready, ((NODES, P),))
                yield
                for t in range(T):
                    for c in range(C):
                        u = 4 + C * t + c
                        dve.wait_ge(zt_hi, 4 * g + C * t + c + 1)
                        RA.release(ve.tensor_tensor(zt[1][:, c, :, t * P:t * P + P],
                                                   RA.bank(u).rearrange("p (h n) -> p h n", h=H0),
                                                   zt[0][:, c, :, t * P:t * P + P].bitcast(F32), ALU.subtract), u)
                        yield

                def elu(n, u):
                    dve.wait_ge(ex_ready, 4 * g + n + 1)
                    ch.add(ve.tensor_scalar(ex[n % 2], ex[n % 2], 1.0, -1.0, ALU.min, ALU.add))
                    yield
                    ch.wait()
                    if n >= 2:
                        dve.wait_ge(ht_lo, 4 * g + n - 1)
                    RA.release(ve.scalar_tensor_tensor(hf[n % 2], RA.bank(u).rearrange("p (c n) -> p c n", c=C), 0.0,
                                                      ex[n % 2], ALU.max, ALU.add), u)

                for h in range(H0):
                    yield from elu(h, 8 + h)
                    yield
                ch.end()

            def rest(g, first=False):
                ch = ch_b
                ch.start(g)
                for t in range(T):
                    dve.wait_ge(wh2_hi, T * g + t + 1)
                    ch.add(ve.tensor_copy(g2[:, t, :], RB.bank(t)[:, D:D + 2]))
                    RB.release(ve.tensor_tensor(wh2[1][:, t, :], RB.bank(t)[:, 0:D + 2],
                                               wh2[0][:, t, :].bitcast(F32), ALU.subtract), t)
                    yield
                yield
                RB.evacuated(dve, g, 1)
                ch.add(ve.tensor_copy(fsm2_hi[:, :], g2[:, :, 1]))
                yield
                ch.wait()
                ch.add(ve.tensor_tensor(fsm2_lo[:, :], g2[:, :, 1], fsm2_hi[:, :].bitcast(F32), ALU.subtract))
                yield
                ch.wait()
                for s, v in enumerate((fsm2_hi, fsm2_lo)):
                    ve.tensor_tensor(dg2[s].rearrange("p (a n) -> p a n", n=NODES),
                                     bc(col(v[:, :].bitcast(F32)), [P, T, NODES]),
                                     bc(eye2[:, :].rearrange("p (a n) -> p a n", a=1), [P, T, NODES]),
                                     ALU.mult).then_inc(diag2_ready, 1)
                yield
                RB.arrived(dve, g, 2)
                RB.release(ve.tensor_tensor(lg2, RB.bank(2)[:, 0:T * NODES].rearrange("p (t n) -> p t n", t=T),
                                           bc(g2[:, :, 0:1], [P, T, NODES]), ALU.add), 2)
                yield
                RB.evacuated(dve, g, 2)
                yield from soft_logits(ch, lg2, rmax2[:, 0, :], 0.01, logits2_ready)
                yield
                dve.wait_ge(exp2_ready, g + 1)
                yield from soft_probs(ch, lg2, lg2, rden2[:, 0, :], prob2_ready)
                yield
                dve.wait_ge(prob2_ready, g + 1)
                dve.wait_ge(ph2_ready, 2 * g + 2)
                low(lg2, pb2[0], pb2[1], pl2_ready)
                yield
                dve.wait_ge(ex2_ready, g + 1)
                ch.add(ve.tensor_scalar(ea, ea, 1.0, -1.0, ALU.min, ALU.add))
                yield
                ch.wait()
                if not first:
                    dve.wait_ge(x1b_ready, g)
                RB.release(ve.scalar_tensor_tensor(eb, RB.bank(4).rearrange("p (c n) -> p c n", c=C), 0.0,
                                                   ea, ALU.max, ALU.add), 4)
                yield
                RB.arrived(dve, g, 6)
                RB.release(ve.tensor_tensor(y0, RB.bank(6).rearrange("p (t n) -> p t n", t=T),
                                           bc(b2_bc[:, :].rearrange("p (a n) -> p a n", a=1), [P, T, D]), ALU.add), 6)
                yield
                RB.evacuated(dve, g, 6)
                yield from inverse_std(ch, y0, st0, mv0, nr0)
                norm_apply(y0, z0, mv0, nr0, [ch.add, lambda i: i.then_inc(z_ready, 1)])
                yield
                dve.wait_ge(z_scaled, 2 * g + 2)
                yield from inverse_std(ch, z0, st0, mv0, nr0)
                norm_apply(z0, x1, mv0, nr0, [ch.add, lambda i: i.then_inc(x1_ready, 1)])
                ch.end()

            def dots(g, first=False):
                ch = ch_c
                ch.start(g)
                for u, dst, bias, hi in ((1, (kt[:, 0], kt[:, 1]), bkc, k_hi), (2, (qt[0][:, :, :], qt[1][:, :, :]), bqc, q_hi)):
                    dve.wait_ge(hi, g + 1)
                    for c in range(C):
                        last = ve.scalar_tensor_tensor(dst[1][:, c, :], RC.bank(u)[:, c * G:(c + 1) * G], bias[:, c:c + 1],
                                                       dst[0][:, c, :].bitcast(F32), ALU.add, ALU.subtract)
                    RC.release(last, u)
                    yield
                dve.wait_ge(v_hi, g + 1)
                RC.release(ve.tensor_tensor(vv[1][:, :, :], RC.bank(3).rearrange("p (t n) -> p t n", t=T),
                                           vv[0][:, :, :].bitcast(F32), ALU.subtract), 3)
                yield
                if not first:
                    dve.wait_ge(x2b_ready, g)
                by_head = sc.rearrange("p (m h) n -> p m h n", h=HC)
                for h in range(HC):
                    u = 4 + h
                    RC.arrived(dve, g, u)
                    s4 = RC.bank(u).rearrange("p (m n) -> p m n", m=T * C)
                    for a, b in ((0, NODES), (NODES, P)):
                        last = ve.tensor_tensor(by_head[a:b, :, h, :], s4[a:b, :, a:b],
                                                bc(mask1[a:b, :].rearrange("p (a n) -> p a n", a=1), [NODES, T * C, NODES]),
                                                ALU.add)
                        if a == 0:
                            ch.add(last)
                    RC.release(last, u)
                    yield
                for u in (6, 7):
                    RC.evacuated(dve, g, u)
                yield from soft_logits(ch, sc, smax[:, 0, :], None, s_ready)
                yield
                dve.wait_ge(s_exp, g + 1)
                yield from inverse_sum(ch, sc, sden[:, 0, :], ok=True, last=s_sum_ready)
                yield
                dve.wait_ge(s_prob, g + 1)
                dve.wait_ge(s_ph, 2 * g + 2)
                a, b = NODES, P
                ve.tensor_tensor(pb1[1][a:b, :, :, a:b].rearrange("p t h n -> p (t h) n"), sc[a:b],
                                 pb1[0][a:b, :, :, a:b].rearrange("p t h n -> p (t h) n"), ALU.subtract).then_inc(s_pl, 1)
                yield
                dve.wait_ge(o_hi, g + 1)
                for c in range(C):
                    last = ve.scalar_tensor_tensor(o1[1][:, c, :], ot1[:, c, :], bvc[:, c:c + 1],
                                                   o1[0][:, c, :].bitcast(F32), ALU.add, ALU.subtract)
                last.then_inc(o_lo, 1)
                yield
                dve.wait_ge(x1b_ready, g + 1)
                RC.arrived(dve, g, 16)
                RC.release(ve.tensor_tensor(y1, RC.bank(16).rearrange("p (t n) -> p t n", t=T), x1b, ALU.add), 16)
                yield
                RC.evacuated(dve, g, 16)
                yield from inverse_std(ch, y1, st1, mv1, nr1)
                norm_apply(y1, x2, mv1, nr1, [ch.add, lambda i: i.then_inc(x2_ready, 1)])
                ch.end()

            def last(g, first=False):
                ch = ch_d
                ch.start(g)
                dve.wait_ge(mj_hi, g + 1)
                RD.release(ve.tensor_tensor(mj[1], RD.bank(2).rearrange("p (t n) -> p t n", t=T),
                                           mj[0].bitcast(F32), ALU.subtract), 2)
                yield
                dve.wait_ge(x2b_ready, g + 1)
                RD.arrived(dve, g, 1)
                RD.release(ve.scalar_tensor_tensor(y2, RD.bank(1).rearrange("p (t n) -> p t n", t=T), deg[:, 0:1], x2b,
                                                   ALU.mult, ALU.add), 1)
                yield
                RD.evacuated(dve, g, 1)
                RD.arrived(dve, g, 3)
                RD.release(ve.tensor_tensor(y2, RD.bank(3).rearrange("p (t n) -> p t n", t=T), y2, ALU.add), 3)
                yield
                RD.evacuated(dve, g, 3)
                yield from inverse_std(ch, y2, st2, mv2, nr2)
                if not first:
                    dve.wait_ge(stored, 16 * g)
                norm_apply(y2, x3, mv2, nr2, [ch.add, lambda i: i.then_inc(x3_ready, 1)])
                yield
                dve.wait_ge(h3_ready, g + 1)
                ch.add(ve.tensor_copy(fsm3_hi[:, :], h3[:, :, D3 + 1]))
                yield
                ch.wait()
                ch.add(ve.tensor_tensor(fsm3_lo[:, :], h3[:, :, D3 + 1], fsm3_hi[:, :].bitcast(F32), ALU.subtract))
                yield
                ch.wait()
                for s, v in enumerate((fsm3_hi, fsm3_lo)):
                    ve.tensor_tensor(dg3[s].rearrange("p (a n) -> p a n", n=NODES), bc(col(v[:, :].bitcast(F32)), [P, T, NODES]),
                                     bc(eye2[:, :].rearrange("p (a n) -> p a n", a=1), [P, T, NODES]),
                                     ALU.mult).then_inc(diag3_ready, 1)
                yield
                RD.evacuated(dve, g, 5)
                ch.add(ve.tensor_tensor(h3r[1], h3[:, :, 0:D3], h3r[0].bitcast(F32), ALU.subtract))
                yield
                ch.wait()
                yield
                RD.arrived(dve, g, 6)
                RD.release(ve.tensor_tensor(lg3, RD.bank(6)[:, 0:T * NODES].rearrange("p (t n) -> p t n", t=T),
                                           bc(h3[:, :, D3:D3 + 1], [P, T, NODES]), ALU.add), 6)
                yield
                RD.evacuated(dve, g, 6)
                yield from soft_logits(ch, lg3, m3[:, 0, :], 0.2, logits3_ready)
                yield
                dve.wait_ge(exp3_ready, g + 1)
                yield from soft_probs(ch, lg3, lg3, d3[:, 0, :], prob3_ready)
                yield
                dve.wait_ge(prob3_ready, g + 1)
                dve.wait_ge(ph3_ready, 2 * g + 2)
                low(lg3, pb3[0], pb3[1], pl3_ready)
                yield
                RD.arrived(dve, g, 8)
                RD.release(ve.tensor_tensor(x3[:, :, 0:D3], RD.bank(8)[:, 0:T * D3].rearrange("p (t n) -> p t n", t=T),
                                           x3[:, :, 0:D3], ALU.add), 8)
                yield
                RD.evacuated(dve, g, 8)
                dve.wait_ge(half_ready, g + 1)
                yield from inverse_std(ch, x3, st2, mv2, nr2)
                norm_apply(x3, x3, mv2, nr2, [ch.add, lambda i: i.then_inc(res_ready, 1)])
                ch.end()

            pipeline(dve, ORDER['dve'], groups, idle, heads, rest, dots, last)

        @block.tensor
        def _(pe):
            te = nc.tensor

            def mm3(out, lhs, rhs, start, stop):
                te.matmul(out, lhs[0], rhs[0], start=start, stop=False)
                te.matmul(out, lhs[0], rhs[1], start=False, stop=False)
                return te.matmul(out, lhs[1], rhs[0], start=False, stop=stop)

            pe.wait_ge(set_dve, 16)
            pe.wait_ge(pool_set, 19)

            def heads(g, first=False):
                pe.wait_ge(x_split, 4 * g + 3)
                RA.acquire(pe, g, 0)
                for t in range(T):
                    o = RA.bank(0)[:, 16 * t:16 * t + 16]
                    cs = slice(t * P, t * P + P)
                    for c in range(C):
                        if c == C - 1:
                            for k in range(C):
                                te.matmul(o[:, 0:8], xt[1][:, k, cs], wa[:, k, 0, :], start=False, stop=False)
                        last = te.matmul(o, xt[0][:, c, cs], wa[:, c, :, :].rearrange("p s n -> p (s n)"),
                                         start=(c == 0), stop=(c == C - 1))
                RA.filled(last, 0)
                yield
                pe.wait_ge(diag_ready, 2 * g + 2)
                RA.acquire(pe, g, 1)
                te.matmul(RA.bank(1), same[:, :], dg[0], start=True, stop=False)
                te.matmul(RA.bank(1), same[:, :], dg[1], start=False, stop=False)
                RA.filled(te.matmul(RA.bank(1).rearrange("p (a n) -> p a n", n=NODES), ident[:, :],
                                   bc(mask0[:, :].rearrange("p (a n) -> p a n", a=1), [P, T * H0, NODES]),
                                   start=False, stop=True), 1)
                yield
                pe.wait_ge(ph_ready, 2 * g + 2)
                pe.wait_ge(pl_ready, 2 * g + 2)
                for t in range(T):
                    RA.acquire(pe, g, 2 + t)
                    o = RA.bank(2 + t).bitcast(F16)
                    for s in range(2):
                        for h in range(H0):
                            k = (s * H0 + h) * P
                            last = te.transpose(o[:, k:k + P], pb[s][:, t * H0 + h, :], ident16[:, :])
                    RA.filled(last, 2 + t)
                yield
                pe.wait_ge(x_split, 4 * g + 4)
                for t in range(T):
                    RA.evacuated(pe, g, 2 + t)
                    for c in range(C):
                        u = 4 + C * t + c
                        RA.acquire(pe, g, u)
                        RA.filled(mm3(RA.bank(u), [xn[s][:, t, c * P:c * P + P] for s in range(2)],
                                     [pt0[:, s, t, :] for s in range(2)], True, True), u)
                    yield
                for u in (6, 7):
                    RA.evacuated(pe, g, u)
                for h in range(H0):
                    u = 8 + h
                    RA.acquire(pe, g, u)
                    for oc in range(C):
                        for c in range(C):
                            last = mm3(RA.bank(u)[:, oc * G:oc * G + G],
                                       [wh[s][:, h, c, oc * P:oc * P + P] for s in range(2)],
                                       [zt[s][:, c, h, :] for s in range(2)], c == 0, c == C - 1)
                        if oc == 0:
                            yield
                    RA.filled(last, u)
                    yield
            def rest(g, first=False):
                for t in range(T):
                    u = t
                    RB.acquire(pe, g, u)
                    for k in range(H0 * C):
                        if t == 0 and k % C == 0:
                            pe.wait_ge(ht_lo, 4 * g + k // C + 1)
                        last = mm3(RB.bank(u)[:, 0:D + 2], [ht[s][:, k, t * P:t * P + P] for s in range(2)],
                                   [wo[s][:, k, :] for s in range(2)], k == 0, k == H0 * C - 1)
                        if k == 3:
                            yield
                    RB.filled(last, u)
                    yield
                pe.wait_ge(diag2_ready, 2 * g + 2)
                RB.acquire(pe, g, 2)
                o = RB.bank(2)[:, 0:T * NODES]
                te.matmul(o, same[:, :], dg2[0], start=True, stop=False)
                te.matmul(o, same[:, :], dg2[1], start=False, stop=False)
                RB.filled(te.matmul(o.rearrange("p (a n) -> p a n", n=NODES), ident[:, :],
                                   bc(mask0[:, :].rearrange("p (a n) -> p a n", a=1), [P, T, NODES]),
                                   start=False, stop=True), 2)
                yield
                pe.wait_ge(ph2_ready, 2 * g + 2)
                pe.wait_ge(pl2_ready, 2 * g + 2)
                RB.acquire(pe, g, 3)
                o = RB.bank(3).bitcast(F16)
                for s in range(2):
                    for t in range(T):
                        k = (s * T + t) * P
                        last = te.transpose(o[:, k:k + P], pb2[s][:, t, :], ident16[:, :])
                RB.filled(last, 3)
                yield
                RB.evacuated(pe, g, 3)
                RB.evacuated(pe, g, 1)
                RB.acquire(pe, g, 4)
                for c in range(C):
                    for t in range(T):
                        k = c * G + t * P
                        last = mm3(RB.bank(4)[:, k:k + P], [wh2[s][:, t, c * P:c * P + P] for s in range(2)],
                                   [pt2[s][:, t, :] for s in range(2)], True, True)
                RB.filled(last, 4)
                yield
                pe.wait_ge(att_lo, g + 1)
                RB.acquire(pe, g, 5)
                for oc in range(C):
                    for c in range(C):
                        last = mm3(RB.bank(5)[:, oc * G:oc * G + G], [wf[s][:, 0, c, oc * P:oc * P + P] for s in range(2)],
                                   [ott[s][:, c, :] for s in range(2)], c == 0, c == C - 1)
                    if oc == 0:
                        yield
                RB.filled(last, 5)
                yield
                pe.wait_ge(hid_lo, g + 1)
                RB.acquire(pe, g, 6)
                for t in range(T):
                    o = RB.bank(6)[:, t * D:t * D + D]
                    cs = slice(t * P, t * P + P)
                    for c in range(C):
                        if c == C - 1:
                            for k in range(C):
                                for s in range(2):
                                    te.matmul(o[:, k * P:k * P + P], ott[s][:, k, cs], ident[:, :], start=False, stop=False)
                        last = mm3(o, [hdt[s][:, c, cs] for s in range(2)], [wf[s][:, 1, c, :] for s in range(2)],
                                   c == 0, c == C - 1)
                RB.filled(last, 6)

            def cols(ring, g, u, src, hi, lo):
                pe.wait_ge(hi, g + 1)
                pe.wait_ge(lo, g + 1)
                ring.acquire(pe, g, u)
                o = ring.bank(u).bitcast(F16)
                for s in range(2):
                    for c in range(C):
                        for t in range(T):
                            k = (s * C + c) * G + t * P
                            last = te.transpose(o[:, k:k + P], src[:, s, t, c * P:c * P + P], ident16[:, :])
                ring.filled(last, u)

            def rows(ring, g, u, x, w, n):
                ring.acquire(pe, g, u)
                for t in range(T):
                    for c in range(C):
                        last = mm3(ring.bank(u)[:, t * n:t * n + n], [x[:, s, c, t * P:t * P + P] for s in range(2)],
                                   [w[s][:, c, :] for s in range(2)], c == 0, c == C - 1)
                ring.filled(last, u)

            def dots(g, first=False):
                cols(RC, g, 0, x16a, x1_16hi, x1_16lo)
                yield
                RC.evacuated(pe, g, 0)
                for u, m in ((1, 1), (2, 0)):
                    RC.acquire(pe, g, u)
                    for oc in range(C):
                        for c in range(C):
                            last = mm3(RC.bank(u)[:, oc * G:oc * G + G], [wp[s][:, m, c, oc * P:oc * P + P] for s in range(2)],
                                       [xt1[:, s, c, :] for s in range(2)], c == 0, c == C - 1)
                    RC.filled(last, u)
                    yield
                rows(RC, g, 3, xt1, [wp[s][:, 2] for s in range(2)], D)
                yield
                RC.evacuated(pe, g, 2)
                RC.evacuated(pe, g, 1)
                for h in range(HC):
                    u = 4 + h
                    part = slice(32 * h, 32 * h + 32)
                    RC.acquire(pe, g, u)
                    for m in range(T * C):
                        t, c = m // C, m % C
                        last = mm3(RC.bank(u)[:, m * P:m * P + P], [qt[s][part, c, t * P:t * P + P] for s in range(2)],
                                   [kt[part, s, c, t * P:t * P + P] for s in range(2)], True, True)
                    RC.filled(last, u)
                    yield
                yield
                pe.wait_ge(s_ph, 2 * g + 2)
                pe.wait_ge(s_pl, 2 * g + 2)

                def turn(n):
                    t, c = n // C, n % C
                    u = 8 + 2 * n
                    RC.acquire(pe, g, u)
                    o = RC.bank(u).bitcast(F16)
                    for s in range(2):
                        for h in range(HC):
                            k = (s * HC + h) * P
                            last = te.transpose(o[:, k:k + P], pb1[s][:, t, c * HC + h, :], ident16[:, :])
                    RC.filled(last, u)

                def values(n):
                    t, c = n // C, n % C
                    u = 9 + 2 * n
                    RC.acquire(pe, g, u)
                    RC.evacuated(pe, g, u - 1)
                    RC.filled(mm3(RC.bank(u), [vv[s][:, t, c * P:c * P + P] for s in range(2)],
                                 [pt1[n % 2][:, s, :] for s in range(2)], True, True), u)

                turn(0)
                for n in range(T * C):
                    if n + 1 < T * C:
                        turn(n + 1)
                        yield
                    values(n)
                    yield
                pe.wait_ge(o_lo, g + 1)
                RC.acquire(pe, g, 16)
                for t in range(T):
                    for c in range(C):
                        last = mm3(RC.bank(16)[:, t * D:t * D + D], [o1[s][:, c, t * P:t * P + P] for s in range(2)],
                                   [wp[s][:, 3, c, :] for s in range(2)], c == 0, c == C - 1)
                RC.filled(last, 16)
            def last(g, first=False):
                cols(RD, g, 0, x16b, x2_16hi, x2_16lo)
                yield
                RD.evacuated(pe, g, 0)
                rows(RD, g, 1, xt2, [wm[s][:, 0] for s in range(2)], D)
                yield
                rows(RD, g, 2, xt2, [wm[s][:, 1] for s in range(2)], D)
                yield
                RD.evacuated(pe, g, 2)
                RD.acquire(pe, g, 3)
                for s in range(2):
                    last = te.matmul(RD.bank(3), adj_t[:, :], mj[s].rearrange("p t n -> p (t n)"), start=(s == 0), stop=(s == 1))
                RD.filled(last, 3)
                yield
                cols(RD, g, 4, x16c, x3_16hi, x3_16lo)
                yield
                RD.evacuated(pe, g, 4)
                rows(RD, g, 5, xt2, [w3[s][:, :, :] for s in range(2)], D3 + 2)
                yield
                pe.wait_ge(diag3_ready, 2 * g + 2)
                RD.acquire(pe, g, 6)
                o = RD.bank(6)[:, 0:T * NODES]
                te.matmul(o, same[:, :], dg3[0], start=True, stop=False)
                te.matmul(o, same[:, :], dg3[1], start=False, stop=False)
                RD.filled(te.matmul(o.rearrange("p (a n) -> p a n", n=NODES), ident[:, :],
                                   bc(mask0[:, :].rearrange("p (a n) -> p a n", a=1), [P, T, NODES]),
                                   start=False, stop=True), 6)
                yield
                pe.wait_ge(ph3_ready, 2 * g + 2)
                pe.wait_ge(pl3_ready, 2 * g + 2)
                RD.acquire(pe, g, 7)
                o = RD.bank(7).bitcast(F16)
                for s in range(2):
                    for t in range(T):
                        k = (s * T + t) * P
                        last = te.transpose(o[:, k:k + P], pb3[s][:, t, :], ident16[:, :])
                RD.filled(last, 7)
                yield
                RD.evacuated(pe, g, 7)
                RD.acquire(pe, g, 8)
                for t in range(T):
                    last = mm3(RD.bank(8)[:, t * D3:t * D3 + D3], [pt3[s][:, t, :] for s in range(2)],
                               [h3r[s][:, t, :] for s in range(2)], True, True)
                RD.filled(last, 8)

            pipeline(pe, ORDER['pe'], groups, idle, heads, rest, dots, last)


def kernel(x, adj, L0_gnn_W_heads, L0_gnn_a_heads, L0_gnn_W_out, L0_gnn_a_out, L0_gnn_w1, L0_gnn_b1, L0_gnn_w2,
           L0_gnn_b2, L0_gnn_ln_gamma, L0_gnn_ln_beta, L1_gnn_Wq, L1_gnn_bq, L1_gnn_Wk, L1_gnn_bk, L1_gnn_Wv,
           L1_gnn_bv, L1_gnn_Wo, L1_gnn_bo, L2_gnn_W, L2_gnn_b, L3_gnn_W, L3_gnn_a):
    import numpy as _np
    import concourse.bacc as _bacc
    from concourse import mybir as _mybir
    from concourse.bass_utils import run_bass_kernel_spmd as _run

    def lay(a):
        return _np.ascontiguousarray(a)

    def cols(b):
        return lay(_np.reshape(b, (2, 128)).T)

    x = _np.asarray(x)
    rows = x.reshape(-1, x.shape[-1])
    arrays = {
        "x": lay(rows), "xT": lay(rows.T), "adj": lay(adj), "adjT": lay(_np.transpose(adj)),
        "w_heads": lay(L0_gnn_W_heads), "a_heads": lay(L0_gnn_a_heads), "w_out": lay(L0_gnn_W_out), "a_out": lay(L0_gnn_a_out),
        "w1": lay(L0_gnn_w1), "b1": cols(L0_gnn_b1), "w2": lay(L0_gnn_w2), "b2": lay(L0_gnn_b2),
        "gamma": lay(L0_gnn_ln_gamma), "beta": lay(L0_gnn_ln_beta),
        "wqT": lay(_np.transpose(L1_gnn_Wq)), "bq": cols(L1_gnn_bq), "wkT": lay(_np.transpose(L1_gnn_Wk)), "bk": cols(L1_gnn_bk),
        "wvT": lay(_np.transpose(L1_gnn_Wv)), "bv": cols(L1_gnn_bv), "woT": lay(_np.transpose(L1_gnn_Wo)), "bo": lay(L1_gnn_bo),
        "wmT": lay(_np.transpose(L2_gnn_W)), "bm": lay(L2_gnn_b), "w3": lay(L3_gnn_W), "a3": lay(_np.reshape(L3_gnn_a, (2, 128))),
    }
    nc = _bacc.Bacc("TRN2", target_bir_lowering=False, num_devices=1)
    io = {n: nc.dram_tensor(n + "_dram", a.shape, _mybir.dt.from_np(a.dtype), kind="ExternalInput").ap()
          for n, a in arrays.items()}
    io["out"] = nc.dram_tensor("out_dram", rows.shape, _mybir.dt.float32, kind="ExternalOutput").ap()
    build_program(nc, io)
    r = _run(nc, [{n + "_dram": a for n, a in arrays.items()}], core_ids=[0])
    return r.results[0]["out_dram"].reshape(x.shape)
```
